# Optimizing a Trainium2 kernel written in Bass

```python
import numpy as np
import jax
import jax.numpy as jnp

def _softmax(x, axis=-1):
    return jax.nn.softmax(x, axis=axis)

def _gelu(x):
    return jax.nn.gelu(x, approximate=True)

def _silu(x):
    return jax.nn.silu(x)

def _sigmoid(x):
    return jax.nn.sigmoid(x)

def _layernorm(x, axis=-1, eps=1e-05):
    m = jnp.mean(x, axis=axis, keepdims=True)
    v = jnp.var(x, axis=axis, keepdims=True)
    return (x - m) / jnp.sqrt(v + eps)

def _scatter_add(tgt, idx, src, axis=0):
    return tgt.at[idx].add(src)

def _segment_sum(src, seg, n):
    return jax.ops.segment_sum(src, seg, n)
kernel_name = 'mk_decoder_preln_d2_seqx_r2_92545e'

def setup_inputs(seed: int=0):
    np.random.seed(seed)
    _w = jnp.asarray

    def _rec_inputs():
        import jax
        import jax.numpy as jnp
        _rk = jax.random.key(seed)
        x = 7.22e-05 + 1 * jax.random.normal(jax.random.fold_in(_rk, 1), (2, 2048, 512), jnp.float32)
        _lenS = 2048 - jax.random.randint(jax.random.fold_in(_rk, 7), (2,), 0, max(1, 2048 // 4) + 1, jnp.int32)
        _lenS2 = 77 - jax.random.randint(jax.random.fold_in(_rk, 8), (2,), 0, max(1, 77 // 4) + 1, jnp.int32)
        _ctx_1024P = jax.random.normal(jax.random.fold_in(_rk, 11), (2, 16, 512), jnp.float32)
        _ctx_1024c = jax.random.dirichlet(jax.random.fold_in(_rk, 511), 0.3 * jnp.ones((16,), jnp.float32), (2, 77))
        _ctx_1024t = jnp.einsum('bsk,bkd->bsd', _ctx_1024c, _ctx_1024P)
        _ctx_1024t = _ctx_1024t * jax.lax.rsqrt(jnp.mean(jnp.square(_ctx_1024t)) + 1e-12) * 0.953939
        ctx_1024 = 4.13588e-05 + 0.999923 * (_ctx_1024t + 0.3 * jax.random.normal(jax.random.fold_in(_rk, 611), (2, 77, 512), jnp.float32))
        _validS = jnp.arange(2048)[None, :] < _lenS[:, None]
        _validS2 = jnp.arange(77)[None, :] < _lenS2[:, None]
        _causal = jnp.tril(jnp.ones((2048, 2048), dtype=bool))
        mask_BxS2_if1 = jnp.where(jnp.ones((2, 77), dtype=bool), 1, 0).astype(jnp.int32)
        return (x, ctx_1024, mask_BxS2_if1)
    x, ctx_1024, mask_BxS2_if1 = _rec_inputs()

    def _L0_attn_setup():
        import jax, jax.numpy as jnp
        import numpy as np
        EPS = 1e-12

        def _l2norm(t):
            n = jnp.linalg.norm(t, axis=-1, keepdims=True)
            return t / jnp.maximum(n, EPS)
        key = jax.random.key(seed)
        kx, kq, kk, kv = jax.random.split(key, 4)
        B, N, D = (8, 2048, 512)
        s = 1.0 / np.sqrt(D)
        return {'x': jax.random.normal(kx, (B, N, D), dtype=jnp.float32), 'W_q': jax.random.normal(kq, (D, D), dtype=jnp.float32) * s, 'W_k': jax.random.normal(kk, (D, D), dtype=jnp.float32) * s, 'W_v': jax.random.normal(kv, (D, D), dtype=jnp.float32) * s}
    _L0_attn_all = _L0_attn_setup()
    _L0_attn_in = {k: v for k, v in _L0_attn_all.items() if k in ('W_q', 'W_k', 'W_v')}
    del _L0_attn_all

    def _L0_xattn_setup():
        import jax, jax.numpy as jnp
        import numpy as np
        D_MODEL = 512
        NUM_HEADS = 16
        D_KEY = D_MODEL // NUM_HEADS
        MASK_FUTURE = True
        NEG_INF = -jnp.inf
        key = jax.random.key(seed)
        ks = jax.random.split(key, 7)
        B, N = (4, 1024)
        return {'query': jax.random.normal(ks[0], (B, N, D_MODEL), dtype=jnp.float32), 'key': jax.random.normal(ks[1], (B, N, D_MODEL), dtype=jnp.float32), 'value': jax.random.normal(ks[2], (B, N, D_MODEL), dtype=jnp.float32), 'mask': jnp.ones((B, N), dtype=jnp.int32), 'Wq': jax.random.normal(ks[3], (D_MODEL, D_MODEL), dtype=jnp.float32) * 0.02, 'Wk': jax.random.normal(ks[4], (D_MODEL, D_MODEL), dtype=jnp.float32) * 0.02, 'Wv': jax.random.normal(ks[5], (D_MODEL, D_MODEL), dtype=jnp.float32) * 0.02, 'Wo': jax.random.normal(ks[6], (D_MODEL, D_MODEL), dtype=jnp.float32) * 0.02}
    _L0_xattn_all = _L0_xattn_setup()
    _L0_xattn_in = {k: v for k, v in _L0_xattn_all.items() if k in ('Wq', 'Wk', 'Wv', 'Wo')}
    del _L0_xattn_all

    def _L0_ffn_setup():
        import jax, jax.numpy as jnp
        import numpy as np
        EPS = 1e-05

        def rmsnorm(x):
            return x * jax.lax.rsqrt(jnp.mean(x * x, axis=-1, keepdims=True) + EPS)

        def act_quant(x):
            scale = 127.0 / jnp.clip(jnp.max(jnp.abs(x), axis=-1, keepdims=True), 1e-05)
            q = jnp.clip(jnp.round(x * scale), -128.0, 127.0) / scale
            return x + jax.lax.stop_gradient(q - x)

        def weight_quant(w):
            scale = 1.0 / jnp.clip(jnp.mean(jnp.abs(w)), 1e-05)
            q = jnp.clip(jnp.round(w * scale), -1.0, 1.0) / scale
            return w + jax.lax.stop_gradient(q - w)

        def bitlinear(x, w, b):
            xq = act_quant(rmsnorm(x))
            wq = weight_quant(w)
            return jnp.einsum('bsd,fd->bsf', xq, wq) + b
        key = jax.random.key(seed)
        k0, k1, k2 = jax.random.split(key, 3)
        B, S, D, F = (2, 4096, 512, 2048)
        x = jax.random.normal(k0, (B, S, D), dtype=jnp.float32)
        w1 = jax.random.normal(k1, (F, D), dtype=jnp.float32) * (1.0 / np.sqrt(D))
        b1 = jnp.zeros((F,), dtype=jnp.float32)
        w2 = jax.random.normal(k2, (D, F), dtype=jnp.float32) * (1.0 / np.sqrt(F))
        b2 = jnp.zeros((D,), dtype=jnp.float32)
        return {'x': x, 'w1': w1, 'b1': b1, 'w2': w2, 'b2': b2}
    _L0_ffn_all = _L0_ffn_setup()
    _L0_ffn_in = {k: v for k, v in _L0_ffn_all.items() if k in ('w1', 'b1', 'w2', 'b2')}
    del _L0_ffn_all

    def _L1_attn_setup():
        import jax, jax.numpy as jnp
        import numpy as np
        N_HEADS = 16
        SEG = 64
        EPS = 1e-06

        def _sigma(x):
            return jax.nn.elu(x) + 1.0

        def _infini_attention(x, W_q, W_k, W_v, W_o, beta_param):
            B, T, D = x.shape
            H = N_HEADS
            dk = D // H
            assert T % SEG == 0
            S = T // SEG

            def proj(W):
                y = (x @ W.T).reshape(B, T, H, dk).transpose(0, 2, 1, 3)
                return y.reshape(B, H, S, SEG, dk).transpose(2, 0, 1, 3, 4)
            Qs, Ks, Vs = (proj(W_q), proj(W_k), proj(W_v))
            beta = jax.nn.sigmoid(beta_param).reshape(1, H, 1, 1)
            causal = jnp.triu(jnp.ones((SEG, SEG), dtype=bool), k=1)
            inv_sqrt_dk = 1.0 / jnp.sqrt(jnp.asarray(dk, x.dtype))
            M0 = jnp.zeros((B, H, dk, dk), dtype=x.dtype)
            z0 = jnp.zeros((B, H, dk), dtype=x.dtype)

            def step(carry, qkv):
                M, z = carry
                q, k, v = qkv
                sq = _sigma(q)
                denom_q = jnp.sum(sq * z[:, :, None, :], axis=-1, keepdims=True) + EPS
                A_mem = jnp.matmul(sq, M) / denom_q
                scores = jnp.matmul(q, jnp.swapaxes(k, -2, -1)) * inv_sqrt_dk
                scores = jnp.where(causal, -jnp.inf, scores)
                A_dot = jnp.matmul(jax.nn.softmax(scores, axis=-1), v)
                A_s = beta * A_mem + (1.0 - beta) * A_dot
                sk = _sigma(k)
                denom_k = jnp.sum(sk * z[:, :, None, :], axis=-1, keepdims=True) + EPS
                V_prev = jnp.matmul(sk, M) / denom_k
                M_new = M + jnp.einsum('bhtk,bhtv->bhkv', sk, v - V_prev)
                z_new = z + jnp.sum(sk, axis=-2)
                return ((M_new, z_new), A_s)
            (M, z), outs = jax.lax.scan(step, (M0, z0), (Qs, Ks, Vs))
            out = outs.transpose(1, 3, 0, 2, 4).reshape(B, S * SEG, H, dk)
            out = outs.transpose(1, 2, 0, 3, 4).reshape(B, H, T, dk)
            out = out.transpose(0, 2, 1, 3).reshape(B, T, D)
            out = out @ W_o.T
            return (out, M.mean(0), z.mean(0))

        def _reference_tuple_inner(x, W_q, W_k, W_v, W_o, beta_param):
            return _infini_attention(x, W_q, W_k, W_v, W_o, beta_param)
        key = jax.random.key(seed)
        kx, kq, kk, kv, ko = jax.random.split(key, 5)
        B, T, D = (4, 2048, 512)
        scale = D ** (-0.5)
        return {'x': jax.random.normal(kx, (B, T, D), dtype=jnp.float32), 'W_q': jax.random.normal(kq, (D, D), dtype=jnp.float32) * scale, 'W_k': jax.random.normal(kk, (D, D), dtype=jnp.float32) * scale, 'W_v': jax.random.normal(kv, (D, D), dtype=jnp.float32) * scale, 'W_o': jax.random.normal(ko, (D, D), dtype=jnp.float32) * scale, 'beta_param': jnp.zeros((N_HEADS,), dtype=jnp.float32)}
    _L1_attn_all = _L1_attn_setup()
    _L1_attn_in = {k: v for k, v in _L1_attn_all.items() if k in ('W_q', 'W_k', 'W_v', 'W_o', 'beta_param')}
    del _L1_attn_all

    def _L1_xattn_setup():
        import jax, jax.numpy as jnp
        import numpy as np
        B, L_ENC, L_DEC, D = (16, 256, 128, 512)
        key = jax.random.key(seed)
        k1, k2, k3, k4, k5, k6 = jax.random.split(key, 6)
        encoder_hc = jax.random.normal(k1, (B, L_ENC, D), dtype=jnp.float32)
        decoder_hq = jax.random.normal(k2, (B, L_DEC, D), dtype=jnp.float32)
        w_sim = jax.random.normal(k3, (3 * D,), dtype=jnp.float32) * 0.02
        b_sim = jax.random.normal(k4, (1,), dtype=jnp.float32) * 0.02
        W_qv = jax.random.normal(k5, (4 * D, D), dtype=jnp.float32) * 0.02
        b_qv = jax.random.normal(k6, (D,), dtype=jnp.float32) * 0.02
        return {'encoder_hc': encoder_hc, 'decoder_hq': decoder_hq, 'w_sim': w_sim, 'b_sim': b_sim, 'W_qv': W_qv, 'b_qv': b_qv}
    _L1_xattn_all = _L1_xattn_setup()
    _L1_xattn_in = {k: v for k, v in _L1_xattn_all.items() if k in ('w_sim', 'b_sim', 'W_qv', 'b_qv')}
    del _L1_xattn_all

    def _L1_ffn_setup():
        import jax, jax.numpy as jnp
        import numpy as np
        MICRO_BATCHES = 2
        TOP_K = 2
        NUM_EXPERTS = 8
        B, S, D = (4, 2048, 512)
        H = 4 * D
        key = jax.random.key(seed)
        ks = jax.random.split(key, 8)
        s = 0.02
        return {'x': jax.random.normal(ks[0], (B, S, D), jnp.float32), 'ln_scale': jnp.ones((D,), jnp.float32), 'ln_bias': jnp.zeros((D,), jnp.float32), 'attn_w': jax.random.normal(ks[1], (D, D), jnp.float32) * s, 'attn_b': jnp.zeros((D,), jnp.float32), 'gate_w': jax.random.normal(ks[2], (NUM_EXPERTS, D), jnp.float32) * s, 'w1': jax.random.normal(ks[3], (NUM_EXPERTS, D, H), jnp.float32) * s, 'b1': jnp.zeros((NUM_EXPERTS, H), jnp.float32), 'w2': jax.random.normal(ks[4], (NUM_EXPERTS, H, D), jnp.float32) * s, 'b2': jnp.zeros((NUM_EXPERTS, D), jnp.float32), 'next_w': jax.random.normal(ks[5], (D, D), jnp.float32) * s, 'next_b': jnp.zeros((D,), jnp.float32)}
    _L1_ffn_all = _L1_ffn_setup()
    _L1_ffn_in = {k: v for k, v in _L1_ffn_all.items() if k in ('ln_scale', 'ln_bias', 'attn_w', 'attn_b', 'gate_w', 'w1', 'b1', 'w2', 'b2', 'next_w', 'next_b')}
    del _L1_ffn_all
    return {'x': x, 'ctx_1024': ctx_1024, 'mask_BxS2_if1': mask_BxS2_if1, 'L0_attn_W_q': _L0_attn_in['W_q'], 'L0_attn_W_k': _L0_attn_in['W_k'], 'L0_attn_W_v': _L0_attn_in['W_v'], 'L0_xattn_Wq': _L0_xattn_in['Wq'], 'L0_xattn_Wk': _L0_xattn_in['Wk'], 'L0_xattn_Wv': _L0_xattn_in['Wv'], 'L0_xattn_Wo': _L0_xattn_in['Wo'], 'L0_ffn_w1': _L0_ffn_in['w1'], 'L0_ffn_b1': _L0_ffn_in['b1'], 'L0_ffn_w2': _L0_ffn_in['w2'], 'L0_ffn_b2': _L0_ffn_in['b2'], 'L1_attn_W_q': _L1_attn_in['W_q'], 'L1_attn_W_k': _L1_attn_in['W_k'], 'L1_attn_W_v': _L1_attn_in['W_v'], 'L1_attn_W_o': _L1_attn_in['W_o'], 'L1_attn_beta_param': _L1_attn_in['beta_param'], 'L1_xattn_w_sim': _L1_xattn_in['w_sim'], 'L1_xattn_b_sim': _L1_xattn_in['b_sim'], 'L1_xattn_W_qv': _L1_xattn_in['W_qv'], 'L1_xattn_b_qv': _L1_xattn_in['b_qv'], 'L1_ffn_ln_scale': _L1_ffn_in['ln_scale'], 'L1_ffn_ln_bias': _L1_ffn_in['ln_bias'], 'L1_ffn_attn_w': _L1_ffn_in['attn_w'], 'L1_ffn_attn_b': _L1_ffn_in['attn_b'], 'L1_ffn_gate_w': _L1_ffn_in['gate_w'], 'L1_ffn_w1': _L1_ffn_in['w1'], 'L1_ffn_b1': _L1_ffn_in['b1'], 'L1_ffn_w2': _L1_ffn_in['w2'], 'L1_ffn_b2': _L1_ffn_in['b2'], 'L1_ffn_next_w': _L1_ffn_in['next_w'], 'L1_ffn_next_b': _L1_ffn_in['next_b']}

def reference(x, ctx_1024, mask_BxS2_if1, L0_attn_W_q, L0_attn_W_k, L0_attn_W_v, L0_xattn_Wq, L0_xattn_Wk, L0_xattn_Wv, L0_xattn_Wo, L0_ffn_w1, L0_ffn_b1, L0_ffn_w2, L0_ffn_b2, L1_attn_W_q, L1_attn_W_k, L1_attn_W_v, L1_attn_W_o, L1_attn_beta_param, L1_xattn_w_sim, L1_xattn_b_sim, L1_xattn_W_qv, L1_xattn_b_qv, L1_ffn_ln_scale, L1_ffn_ln_bias, L1_ffn_attn_w, L1_ffn_attn_b, L1_ffn_gate_w, L1_ffn_w1, L1_ffn_b1, L1_ffn_w2, L1_ffn_b2, L1_ffn_next_w, L1_ffn_next_b):
    import jax
    import jax.numpy as jnp

    def _L0_attn_ref(x, W_q, W_k, W_v):
        import jax, jax.numpy as jnp
        import numpy as np
        EPS = 1e-12

        def _l2norm(t):
            n = jnp.linalg.norm(t, axis=-1, keepdims=True)
            return t / jnp.maximum(n, EPS)
        Q = _l2norm(jnp.einsum('bnd,ed->bne', x, W_q))
        K = _l2norm(jnp.einsum('bnd,ed->bne', x, W_k))
        V = jnp.einsum('bnd,ed->bne', x, W_v)
        C = x.shape[1]
        global_feat = jnp.sum(K * V, axis=1, keepdims=True) / C
        return Q * global_feat

    def _L0_xattn_ref(query, key, value, mask, Wq, Wk, Wv, Wo):
        import jax, jax.numpy as jnp
        import numpy as np
        D_MODEL = 512
        NUM_HEADS = 16
        D_KEY = D_MODEL // NUM_HEADS
        MASK_FUTURE = True
        NEG_INF = -jnp.inf
        B, Nq, _ = query.shape
        Nk = key.shape[1]

        def proj(x, W, N):
            return (x @ W).reshape(B, N, NUM_HEADS, D_KEY).transpose(0, 2, 1, 3)
        Q = proj(query, Wq, Nq)
        K = proj(key, Wk, Nk)
        V = proj(value, Wv, Nk)
        scores = jnp.einsum('bhqd,bhkd->bhqk', Q, K) / np.sqrt(D_KEY).astype(np.float32)
        scores = jnp.where(mask[:, None, None, :] == 0, NEG_INF, scores)
        if MASK_FUTURE:
            causal = jnp.triu(jnp.ones((Nq, Nk), dtype=jnp.bool_), k=1)
            scores = jnp.where(causal[None, None, :, :], NEG_INF, scores)
        attn = jax.nn.softmax(scores, axis=-1)
        out = jnp.einsum('bhqk,bhkd->bhqd', attn, V)
        out = out.transpose(0, 2, 1, 3).reshape(B, Nq, D_MODEL)
        return out @ Wo

    def _L0_ffn_ref(x, w1, b1, w2, b2):
        import jax, jax.numpy as jnp
        import numpy as np
        EPS = 1e-05

        def rmsnorm(x):
            return x * jax.lax.rsqrt(jnp.mean(x * x, axis=-1, keepdims=True) + EPS)

        def act_quant(x):
            scale = 127.0 / jnp.clip(jnp.max(jnp.abs(x), axis=-1, keepdims=True), 1e-05)
            q = jnp.clip(jnp.round(x * scale), -128.0, 127.0) / scale
            return x + jax.lax.stop_gradient(q - x)

        def weight_quant(w):
            scale = 1.0 / jnp.clip(jnp.mean(jnp.abs(w)), 1e-05)
            q = jnp.clip(jnp.round(w * scale), -1.0, 1.0) / scale
            return w + jax.lax.stop_gradient(q - w)

        def bitlinear(x, w, b):
            xq = act_quant(rmsnorm(x))
            wq = weight_quant(w)
            return jnp.einsum('bsd,fd->bsf', xq, wq) + b
        h = bitlinear(x, w1, b1)
        h = jax.nn.gelu(h, approximate=False)
        return bitlinear(h, w2, b2)

    def _L1_attn_ref(x, W_q, W_k, W_v, W_o, beta_param):
        import jax, jax.numpy as jnp
        import numpy as np
        N_HEADS = 16
        SEG = 64
        EPS = 1e-06

        def _sigma(x):
            return jax.nn.elu(x) + 1.0

        def _infini_attention(x, W_q, W_k, W_v, W_o, beta_param):
            B, T, D = x.shape
            H = N_HEADS
            dk = D // H
            assert T % SEG == 0
            S = T // SEG

            def proj(W):
                y = (x @ W.T).reshape(B, T, H, dk).transpose(0, 2, 1, 3)
                return y.reshape(B, H, S, SEG, dk).transpose(2, 0, 1, 3, 4)
            Qs, Ks, Vs = (proj(W_q), proj(W_k), proj(W_v))
            beta = jax.nn.sigmoid(beta_param).reshape(1, H, 1, 1)
            causal = jnp.triu(jnp.ones((SEG, SEG), dtype=bool), k=1)
            inv_sqrt_dk = 1.0 / jnp.sqrt(jnp.asarray(dk, x.dtype))
            M0 = jnp.zeros((B, H, dk, dk), dtype=x.dtype)
            z0 = jnp.zeros((B, H, dk), dtype=x.dtype)

            def step(carry, qkv):
                M, z = carry
                q, k, v = qkv
                sq = _sigma(q)
                denom_q = jnp.sum(sq * z[:, :, None, :], axis=-1, keepdims=True) + EPS
                A_mem = jnp.matmul(sq, M) / denom_q
                scores = jnp.matmul(q, jnp.swapaxes(k, -2, -1)) * inv_sqrt_dk
                scores = jnp.where(causal, -jnp.inf, scores)
                A_dot = jnp.matmul(jax.nn.softmax(scores, axis=-1), v)
                A_s = beta * A_mem + (1.0 - beta) * A_dot
                sk = _sigma(k)
                denom_k = jnp.sum(sk * z[:, :, None, :], axis=-1, keepdims=True) + EPS
                V_prev = jnp.matmul(sk, M) / denom_k
                M_new = M + jnp.einsum('bhtk,bhtv->bhkv', sk, v - V_prev)
                z_new = z + jnp.sum(sk, axis=-2)
                return ((M_new, z_new), A_s)
            (M, z), outs = jax.lax.scan(step, (M0, z0), (Qs, Ks, Vs))
            out = outs.transpose(1, 3, 0, 2, 4).reshape(B, S * SEG, H, dk)
            out = outs.transpose(1, 2, 0, 3, 4).reshape(B, H, T, dk)
            out = out.transpose(0, 2, 1, 3).reshape(B, T, D)
            out = out @ W_o.T
            return (out, M.mean(0), z.mean(0))

        def _reference_tuple_inner(x, W_q, W_k, W_v, W_o, beta_param):
            return _infini_attention(x, W_q, W_k, W_v, W_o, beta_param)
        return _reference_tuple_inner(x, W_q, W_k, W_v, W_o, beta_param)[0]

    def _L1_xattn_ref(encoder_hc, decoder_hq, w_sim, b_sim, W_qv, b_qv):
        import jax, jax.numpy as jnp
        import numpy as np
        B, L_ENC, L_DEC, D = (16, 256, 128, 512)
        d = encoder_hc.shape[-1]
        w1, w2, w3 = (w_sim[:d], w_sim[d:2 * d], w_sim[2 * d:])
        Sim = (encoder_hc @ w1)[:, :, None] + (decoder_hq @ w2)[:, None, :] + jnp.einsum('bid,bjd->bij', encoder_hc * w3, decoder_hq) + b_sim[0]
        A = jax.nn.softmax(Sim, axis=2)
        hq_hat = jnp.einsum('bij,bjd->bid', A, decoder_hq)
        Batt = jax.nn.softmax(jnp.max(Sim, axis=2), axis=1)
        hc_bar = jnp.einsum('bi,bid->bd', Batt, encoder_hc)[:, None, :]
        hc_hat = jnp.broadcast_to(hc_bar, encoder_hc.shape)
        feats = jnp.concatenate([encoder_hc, hq_hat, encoder_hc * hq_hat, encoder_hc * hc_hat], axis=-1)
        hcq = feats @ W_qv + b_qv
        return hcq

    def _L1_ffn_ref(x, ln_scale, ln_bias, attn_w, attn_b, gate_w, w1, b1, w2, b2, next_w, next_b):
        import jax, jax.numpy as jnp
        import numpy as np
        MICRO_BATCHES = 2
        TOP_K = 2
        NUM_EXPERTS = 8
        B, S, D = (4, 2048, 512)
        H = 4 * D
        b, s, d = x.shape
        flat = x.reshape(b * s, d)
        mu = jnp.mean(flat, axis=-1, keepdims=True)
        var = jnp.mean((flat - mu) ** 2, axis=-1, keepdims=True)
        xn = (flat - mu) * jax.lax.rsqrt(var + 1e-05) * ln_scale + ln_bias
        x_attn = xn @ attn_w.T + attn_b + flat
        logits = x_attn @ gate_w.T
        _vals, _idx = jax.lax.top_k(logits, TOP_K)
        e = w1.shape[0]
        n = b * s // (MICRO_BATCHES * e)
        xe = x_attn.reshape(MICRO_BATCHES, e, n, d)
        h = jax.nn.gelu(jnp.einsum('mend,edh->menh', xe, w1) + b1[None, :, None, :], approximate=False)
        eo = jnp.einsum('menh,ehd->mend', h, w2) + b2[None, :, None, :]
        eo = eo.reshape(b * s, d)
        out = jax.nn.gelu(eo @ next_w.T + next_b, approximate=False)
        return out.reshape(b, s, d)
    x = x + _L0_attn_ref(_layernorm(x, axis=-1), L0_attn_W_q, L0_attn_W_k, L0_attn_W_v)
    x = x + _L0_xattn_ref(_layernorm(x, axis=-1), ctx_1024, ctx_1024, mask_BxS2_if1, L0_xattn_Wq, L0_xattn_Wk, L0_xattn_Wv, L0_xattn_Wo)
    x = x + _L0_ffn_ref(_layernorm(x, axis=-1), L0_ffn_w1, L0_ffn_b1, L0_ffn_w2, L0_ffn_b2)
    x = x + _L1_attn_ref(_layernorm(x, axis=-1), L1_attn_W_q, L1_attn_W_k, L1_attn_W_v, L1_attn_W_o, L1_attn_beta_param)
    x = x + _L1_xattn_ref(_layernorm(x, axis=-1), ctx_1024, L1_xattn_w_sim, L1_xattn_b_sim, L1_xattn_W_qv, L1_xattn_b_qv)
    x = x + _L1_ffn_ref(_layernorm(x, axis=-1), L1_ffn_ln_scale, L1_ffn_ln_bias, L1_ffn_attn_w, L1_ffn_attn_b, L1_ffn_gate_w, L1_ffn_w1, L1_ffn_b1, L1_ffn_w2, L1_ffn_b2, L1_ffn_next_w, L1_ffn_next_b)
    return x

_drawn_inputs = setup_inputs


def setup_inputs(seed=0):
    import zlib

    import numpy as np

    out = dict(_drawn_inputs(seed))
    spreads = {'L0_ffn_b1': (0.0, 0.1),
     'L0_ffn_b2': (0.0, 0.1),
     'L1_attn_beta_param': (0.0, 0.8),
     'L1_ffn_ln_scale': (1.0, 0.6),
     'L1_ffn_ln_bias': (0.0, 0.8),
     'L1_ffn_attn_b': (0.0, 0.8),
     'L1_ffn_b1': (0.0, 0.8),
     'L1_ffn_b2': (0.0, 0.47),
     'L1_ffn_next_b': (0.0, 0.1)}
    factors = {'L0_attn_W_q': 200.0,
     'L0_attn_W_k': 200.0,
     'L0_attn_W_v': 200.0,
     'L0_xattn_Wq': 3.804,
     'L0_xattn_Wk': 3.782,
     'L1_xattn_b_qv': 3.767,
     'L1_ffn_attn_w': 2.897}
    for name, (base, spread) in spreads.items():
        noise = np.random.default_rng([zlib.crc32(name.encode()), seed]).standard_normal(out[name].shape)
        drawn = base * np.exp(spread * noise) if base else spread * noise
        out[name] = jnp.asarray(drawn.astype(out[name].dtype))
    for name, factor in factors.items():
        out[name] = (out[name] * factor).astype(out[name].dtype)
    return out
```

```python
from contextlib import ExitStack

import concourse.bass as bass
from concourse import mybir

F32 = mybir.dt.float32
BF16 = mybir.dt.bfloat16
I32 = mybir.dt.int32
ALU = mybir.AluOpType
ACT = mybir.ActivationFunctionType
AX_X = mybir.AxisListType.X

P = 128
B = 2
S = 2048
D = 512
DC = D // P
TB = S // P
N_TILES = B * TB
LN_EPS = 1e-5



def run_stages(eng, stages, n=N_TILES):
    top = max(lag for lag, _ in stages)
    head = top + 2

    def once(i):
        for lag, stage in stages:
            if 0 <= i - lag < n:
                stage((i - lag) // 2, (i - lag) % 2)

    for i in range(head):
        once(i)
    pairs = (n - head) // 2
    if pairs:
        with eng.Fori(0, pairs) as k:
            for u in (0, 1):
                for lag, stage in stages:
                    c = head + u - lag
                    stage(k + c // 2, c % 2)
    for i in range(head + 2 * pairs, n + top):
        once(i)


def reached(eng, sem, h, p, k=1, per=1):
    eng.wait_ge(sem, h * (2 * per) + (p * per + k))


def freed(eng, sem, h, p, k=1, per=1, back=2, n=N_TILES):
    if isinstance(h, int):
        t = min(2 * h + p - back, n - 1)
        if t >= 0:
            eng.wait_ge(sem, t * per + k)
        return
    eng.wait_ge(sem, h * (2 * per) + ((p - back) * per + k))


def carry_wait(nc, eng, consts):
    a, b = consts
    if eng is nc.gpsimd:
        nc.gpsimd.tensor_tensor(b[:, 0:1], a[:, 0:1], a[:, 1:2], ALU.add)
    else:
        nc.vector.tensor_copy(b[:, 1:2], a[:, 0:1])


class Phase:

    def __init__(self, nc, ctx, name):
        self.nc, self.ctx, self.name = nc, ctx, name
        self.sems = []
        ctx.callback(self.end)

    def sb(self, name, shape, dt=F32):
        return self.ctx.enter_context(self.nc.sbuf_tensor(f"{self.name}_{name}", shape, dt))

    def banks(self, n=8):
        return self.ctx.enter_context(self.nc.psum_tensor(f"{self.name}_banks", [P, n, 512], F32))

    def sem(self, name):
        self.sems.append(self.nc.alloc_semaphore(f"{self.name}_{name}"))
        return self.sems[-1]

    def end(self):
        if self.sems:
            self.nc.clear_and_free_semaphores(self.sems)
            self.nc.all_engine_barrier()



def l0_attention(nc, d, x, q_hat, gf, ident, ones, minus_half, consts):
    with ExitStack() as ctx:
        ph = Phase(nc, ctx, "a0")
        w = ph.sb("w", [P, 3, DC, D])
        xn = ph.sb("xn", [P, 2, D])
        xnT = ph.sb("xnT", [P, 2, DC, P])
        stats = ph.sb("stats", [P, 2, 6])
        mv = ph.sb("mv", [P, 2, 2])
        var_eps = ph.sb("var_eps", [P, 2])
        rstd = ph.sb("rstd", [P, 2])
        squares = ph.sb("squares", [P, D])
        ss = ph.sb("ss", [P, 2, 2])
        ss_max = ph.sb("ss_max", [P, 2, 2])
        rnorm = ph.sb("rnorm", [P, 2, 2])
        v_sb = ph.sb("v_sb", [P, 2, D])
        kv = ph.sb("kv", [P, 2, D])
        acc = ph.sb("acc", [P, 2, D])
        ps = ph.banks()
        psT, psG = ps[:, 0], ps[:, 7]
        psQ, psK, psV = (lambda p: ps[:, 1 + p]), (lambda p: ps[:, 3 + p]), (lambda p: ps[:, 5 + p])

        x_in = [ph.sem(f"x_in{p}") for p in range(2)]
        w_in = ph.sem("w_in")
        acc_zero = ph.sem("acc_zero")
        stats_done = ph.sem("stats_done")
        mv_ready = ph.sem("mv_ready")
        var_ready = ph.sem("var_ready")
        ss_ready = ph.sem("ss_ready")
        rstd_ready = ph.sem("rstd_ready")
        xn_ready = ph.sem("xn_ready")
        xnT_psum = ph.sem("xnT_psum")
        xnT_ready = ph.sem("xnT_ready")
        proj = ph.sem("proj")
        act_qkv = ph.sem("act_qkv")
        rnorm_ready = ph.sem("rnorm_ready")
        q_kept = ph.sem("q_kept")
        kv_ready = ph.sem("kv_ready")
        kv_added = ph.sem("kv_added")
        gf_psum = ph.sem("gf_psum")
        gf_ready = ph.sem("gf_ready")
        block = ctx.enter_context(nc.Block())

        @block.sync
        def _(sp):
            def load(h, p):
                if not (isinstance(h, int) and h == 0):
                    sp.wait_ge(x_in[p], h * 16)
                sp.dma_start(x[:, p, h, :], d["x"][p, h]).then_inc(x_in[p], 16)

            run_stages(sp, [(0, load)])
            for p in range(2):
                sp.wait_ge(x_in[p], TB * 16)

        @block.gpsimd
        def _(pool):
            nc.gpsimd.memset(acc[:], 0.0).then_inc(acc_zero, 1)

            def layernorm_scale(h, p):
                reached(pool, mv_ready, h, p)
                freed(pool, rstd_ready, h, p)
                carry_wait(nc, pool, consts)
                nc.gpsimd.tensor_scalar(var_eps[:, p:p + 1], mv[:, p, 1:2], LN_EPS, None, ALU.add).then_inc(var_ready, 1)
                reached(pool, var_ready, h, p)
                nc.gpsimd.tensor_tensor(rstd[:, p:p + 1], var_eps[:, p:p + 1], minus_half[:, 0:1],
                                        ALU.pow).then_inc(rstd_ready, 1)

            def norms(h, p):
                reached(pool, act_qkv, h, p, 2, 3)
                freed(pool, rnorm_ready, h, p)
                carry_wait(nc, pool, consts)
                nc.gpsimd.tensor_scalar(ss_max[:, p, :], ss[:, p, :], 1e-24, None, ALU.max).then_inc(ss_ready, 1)
                reached(pool, ss_ready, h, p)
                freed(pool, kv_ready, h, p)
                nc.gpsimd.tensor_tensor(rnorm[:, p, :], ss_max[:, p, :], minus_half[:, 0:2],
                                        ALU.pow).then_inc(rnorm_ready, 1)

            def add_kv(h, p):
                reached(pool, kv_ready, h, p)
                freed(pool, kv_added, h, p)
                nc.gpsimd.tensor_tensor(acc[:, p, :], acc[:, p, :], kv[:, p, :], ALU.add).then_inc(kv_added, 1)

            pool.wait_ge(acc_zero, 1)
            run_stages(pool, [(0, layernorm_scale), (2, norms), (2, add_kv)])

        @block.vector
        def _(dve):
            def normalise(h, p):
                dve.wait_ge(x_in[p], h * 16 + 16)
                nc.vector.bn_stats(stats[:, p, :], x[:, p, h, :]).then_inc(stats_done, 1)
                reached(dve, stats_done, h, p)
                carry_wait(nc, dve, consts)
                nc.vector.bn_aggr(mv[:, p, :], stats[:, p, :]).then_inc(mv_ready, 1)
                reached(dve, rstd_ready, h, p)
                freed(dve, xnT_psum, h, p)
                nc.vector.tensor_scalar(xn[:, p, :], x[:, p, h, :], mv[:, p, 0:1], rstd[:, p:p + 1],
                                        ALU.subtract, ALU.mult).then_inc(xn_ready, 1)

            def products(h, p):
                reached(dve, rnorm_ready, h, p)
                nc.vector.tensor_scalar(q_hat[:, p, h, :], psQ(p), rnorm[:, p, 0:1], None,
                                        ALU.mult).then_inc(q_kept, 1)
                reached(dve, act_qkv, h, p, 3, 3)
                freed(dve, kv_added, h, p)
                nc.vector.scalar_tensor_tensor(out=kv[:, p, :], in0=psK(p), scalar=rnorm[:, p, 1:2],
                                               in1=v_sb[:, p, :], op0=ALU.mult, op1=ALU.mult).then_inc(kv_ready, 1)

            run_stages(dve, [(0, normalise), (2, products)])
            for p in range(2):
                dve.wait_ge(gf_psum, p + 1)
                nc.vector.tensor_scalar(gf[:, p, :], psG, 1.0 / S, None, ALU.mult).then_inc(gf_ready, 1)

        @block.scalar
        def _(act):
            act.dma_start(w[:], d["w_a0"]).then_inc(w_in, 16)

            def keep_xnT(h, p):
                reached(act, xnT_psum, h, p)
                freed(act, proj, h, p, 3, 3)
                nc.scalar.copy(xnT[:, p].rearrange("p c t -> p (c t)"), psT).then_inc(xnT_ready, 1)

            def square_sums(h, p):
                freed(act, rnorm_ready, h, p)
                freed(act, act_qkv, h, p, 2, 3, back=1)
                reached(act, proj, h, p, 1, 3)
                nc.scalar.activation(squares[:], psQ(p), ACT.Square, accum_out=ss[:, p, 0:1]).then_inc(act_qkv, 1)
                reached(act, proj, h, p, 2, 3)
                reached(act, act_qkv, h, p, 1, 3)
                nc.scalar.activation(squares[:], psK(p), ACT.Square, accum_out=ss[:, p, 1:2]).then_inc(act_qkv, 1)
                reached(act, proj, h, p, 3, 3)
                freed(act, kv_ready, h, p)
                nc.scalar.copy(v_sb[:, p, :], psV(p)).then_inc(act_qkv, 1)

            run_stages(act, [(1, keep_xnT), (2, square_sums)])

        @block.tensor
        def _(pe):
            def transposes(h, p):
                reached(pe, xn_ready, h, p)
                freed(pe, xnT_ready, h, p, back=1)
                for c in range(DC):
                    mm = nc.tensor.transpose(psT[:, c * P:(c + 1) * P], xn[:, p, c * P:(c + 1) * P], ident[:])
                mm.then_inc(xnT_psum, 1)

            def project(h, p):
                reached(pe, xnT_ready, h, p)
                freed(pe, act_qkv, h, p, 3, 3)
                freed(pe, q_kept, h, p)
                freed(pe, kv_ready, h, p)
                for j, bank in enumerate((psQ(p), psK(p), psV(p))):
                    for c in range(DC):
                        mm = nc.tensor.matmul(bank, xnT[:, p, c, :], w[:, j, c, :], start=c == 0, stop=c == DC - 1)
                    mm.then_inc(proj, 1)

            pe.wait_ge(w_in, 16)
            run_stages(pe, [(1, transposes), (2, project)])
            pe.wait_ge(kv_added, N_TILES)
            for p in range(2):
                if p:
                    pe.wait_ge(gf_ready, p)
                nc.tensor.matmul(psG, ones[:], acc[:, p, :], start=True, stop=True).then_inc(gf_psum, 1)



K = 77
H = 16
DK = D // H
HC = P // DK
NEG = -1e30


def l0_cross_attention(nc, d, x, q_hat, gf, ident, minus_half, eps, consts):
    with ExitStack() as ctx:
        ph = Phase(nc, ctx, "x0")
        wq = ph.sb("wq", [P, DC, D])
        wo = ph.sb("wo", [P, DC, D])
        keys = ph.sb("keys", [P, B, DC, HC * K])
        values = ph.sb("values", [K, B, H, P])
        bias = ph.sb("bias", [P, 2, B, K])
        ps = ph.banks()
        ctx_in = ph.sem("ctx_in")
        w_in = ph.sem("w_in")

        with ExitStack() as ctx2:
            ph2 = Phase(nc, ctx2, "x0s")
            ctxT = ph2.sb("ctxT", [P, DC, B * K])
            wk = ph2.sb("wk", [P, DC, D])
            wv = ph2.sb("wv", [P, DC, D])
            mask = ph2.sb("mask", [P, B, K], I32)
            keys_zero = ph2.sem("keys_zero")
            masked_made = ph2.sem("masked_made")
            causal_made = ph2.sem("causal_made")
            k_psum = ph2.sem("k_psum")
            k_kept = ph2.sem("k_kept")
            v_psum = ph2.sem("v_psum")
            v_kept = ph2.sem("v_kept")
            with nc.Block() as block:
                @block.sync
                def _(sp):
                    sp.dma_start(ctxT[:], d["ctxT"]).then_inc(ctx_in, 16)
                    sp.dma_start(mask[:], d["mask"]).then_inc(ctx_in, 16)
                    sp.dma_start(wk[:], d["w_x0k"]).then_inc(ctx_in, 16)
                    sp.dma_start(wv[:], d["w_x0v"]).then_inc(ctx_in, 16)

                @block.gpsimd
                def _(pool):
                    nc.gpsimd.memset(keys[:], 0.0).then_inc(keys_zero, 1)
                    nc.gpsimd.memset(values[:], 0.0).then_inc(keys_zero, 1)
                    pool.wait_ge(masked_made, 2)
                    nc.gpsimd.affine_select(out=bias[:, 0], in_=bias[:, 0], compare_op=ALU.is_ge, fill=NEG, base=0,
                                            pattern=[[0, B], [-1, K]], channel_multiplier=1).then_inc(causal_made, 1)

                @block.tensor
                def _(pe):
                    pe.wait_ge(ctx_in, 64)
                    for j in range(DC):
                        for c in range(DC):
                            mm = nc.tensor.matmul(ps[:, j, 0:B * K], wk[:, c, j * P:(j + 1) * P], ctxT[:, c, :],
                                                  start=c == 0, stop=c == DC - 1)
                        mm.then_inc(k_psum, 1)
                    for b in range(B):
                        for c in range(DC):
                            mm = nc.tensor.matmul(ps[0:K, DC + b], ctxT[:, c, b * K:(b + 1) * K], wv[:, c, :],
                                                  start=c == 0, stop=c == DC - 1)
                        mm.then_inc(v_psum, 1)

                @block.vector
                def _(dve):
                    dve.wait_ge(ctx_in, 64)
                    for n in range(2):
                        nc.vector.tensor_scalar(bias[:, n], mask[:], 0, NEG, ALU.is_equal,
                                                ALU.mult).then_inc(masked_made, 1)

                @block.scalar
                def _(act):
                    act.dma_start(wq[:], d["w_x0q"]).then_inc(w_in, 16)
                    act.dma_start(wo[:], d["w_x0o"]).then_inc(w_in, 16)
                    act.wait_ge(keys_zero, 2)
                    for j in range(DC):
                        act.wait_ge(k_psum, j + 1)
                        for g in range(HC):
                            r = slice(g * DK, (g + 1) * DK)
                            for b in range(B):
                                nc.scalar.activation(keys[r, b, j, g * K:(g + 1) * K], ps[r, j, b * K:(b + 1) * K],
                                                     ACT.Copy, scale=float(DK) ** -0.5).then_inc(k_kept, 1)
                    for b in range(B):
                        act.wait_ge(v_psum, b + 1)
                        for g in range(HC):
                            nc.scalar.copy(values[:, b].rearrange("k (c g) n -> k g c n", g=HC)[:, g, :, g * DK:(g + 1) * DK],
                                           ps[0:K, DC + b].rearrange("k (c g n) -> k g c n", g=HC, n=DK)[:, g]).then_inc(v_kept, 1)

        moved = ph.sb("moved", [P, 2, D])
        xn = ph.sb("xn", [P, 2, D])
        xnT = ph.sb("xnT", [P, DC, P])
        qT = ph.sb("qT", [P, 2, DC, P])
        stats = ph.sb("stats", [P, 2, 6])
        mv = ph.sb("mv", [P, 2, 2])
        var_eps = ph.sb("var_eps", [P, 2])
        rstd = ph.sb("rstd", [P, 2])
        probs = ph.sb("probs", [P, 2, H, K])
        top = ph.sb("top", [P, 2, H])
        total = ph.sb("total", [P, 2, H])
        inv = ph.sb("inv", [P, 2, H])
        pT = ph.sb("pT", [K, 2, HC, P])
        attnT = ph.sb("attnT", [P, DC, P])
        psT, psQ, psV, psY = ps[:, 0], ps[:, 1], ps[:, 6], ps[:, 7]
        psS = lambda j: ps[:, 2 + j % 2, 0:HC * K]
        psP = lambda g: ps[0:K, 4 + g % 2]

        names = ("moved_ready x_moved stats_done mv_ready var_ready rstd_ready xn_ready xnT_psum xnT_ready qT_psum "
                 "qT_ready scores biased top_ready shifted exp_ready total_ready inv_ready probs_ready pT_psum pT_ready "
                 "attnT_psum attnT_ready y_psum x_added").split()
        (moved_ready, x_moved, stats_done, mv_ready, var_ready, rstd_ready, xn_ready, xnT_psum, xnT_ready, qT_psum,
         qT_ready, scores, biased, top_ready, shifted, exp_ready, total_ready, inv_ready, probs_ready, pT_psum, pT_ready,
         attnT_psum, attnT_ready, y_psum, x_added) = (ph.sem(n) for n in names)
        block = ctx.enter_context(nc.Block())

        @block.gpsimd
        def _(pool):
            def move(h, p):
                freed(pool, x_moved, h, p)
                nc.gpsimd.tensor_tensor(moved[:, p], q_hat[:, p, h, :], gf[:, p, :], ALU.mult).then_inc(moved_ready, 1)

            def layernorm_scale(h, p):
                reached(pool, mv_ready, h, p)
                freed(pool, xn_ready, h, p)
                nc.gpsimd.tensor_tensor(var_eps[:, p:p + 1], mv[:, p, 1:2], eps[:], ALU.add).then_inc(var_ready, 1)
                reached(pool, var_ready, h, p)
                nc.gpsimd.tensor_tensor(rstd[:, p:p + 1], var_eps[:, p:p + 1], minus_half[:, 0:1],
                                        ALU.pow).then_inc(rstd_ready, 1)

            run_stages(pool, [(0, move), (0, layernorm_scale)])

        @block.vector
        def _(dve):
            def statistics(h, p):
                reached(dve, moved_ready, h, p)
                nc.vector.tensor_tensor(x[:, p, h, :], x[:, p, h, :], moved[:, p], ALU.add).then_inc(x_moved, 1)
                reached(dve, x_moved, h, p)
                carry_wait(nc, dve, consts)
                nc.vector.bn_stats(stats[:, p, :], x[:, p, h, :]).then_inc(stats_done, 1)
                reached(dve, stats_done, h, p)
                freed(dve, xn_ready, h, p)
                carry_wait(nc, dve, consts)
                nc.vector.bn_aggr(mv[:, p, :], stats[:, p, :]).then_inc(mv_ready, 1)

            def normalise(h, p):
                reached(dve, rstd_ready, h, p)
                freed(dve, xnT_psum, h, p)
                nc.vector.tensor_scalar(xn[:, p, :], x[:, p, h, :], mv[:, p, 0:1], rstd[:, p:p + 1],
                                        ALU.subtract, ALU.mult).then_inc(xn_ready, 1)

            def residual(h, p):
                reached(dve, y_psum, h, p)
                nc.vector.tensor_tensor(x[:, p, h, :], psY, x[:, p, h, :], ALU.add).then_inc(x_added, 1)

            def divide(h, p):
                reached(dve, exp_ready, h, p)
                freed(dve, inv_ready, h, p)
                nc.vector.tensor_reduce(total[:, p], probs[:, p], AX_X, ALU.add).then_inc(total_ready, 1)
                reached(dve, total_ready, h, p)
                freed(dve, probs_ready, h, p)
                nc.vector.reciprocal(inv[:, p], total[:, p]).then_inc(inv_ready, 1)
                reached(dve, inv_ready, h, p)
                nc.vector.tensor_tensor(probs[:, p], probs[:, p], inv[:, p].unsqueeze(2).to_broadcast([P, H, K]),
                                        ALU.mult).then_inc(probs_ready, 1)

            def shift(h, p):
                first = 0 if isinstance(h, int) and h == 0 else 1
                freed(dve, probs_ready, h, p)
                freed(dve, pT_psum, h, p, 4, 4)
                for j in range(DC):
                    reached(dve, scores, h, p, j + 1, DC)
                    nc.vector.tensor_tensor(probs[:, p, j * HC:(j + 1) * HC], psS(j).rearrange("t (n k) -> t n k", n=HC),
                                            bias[:, first, p].unsqueeze(1).to_broadcast([P, HC, K]),
                                            ALU.add).then_inc(biased, 1)
                reached(dve, biased, h, p, DC, DC)
                freed(dve, shifted, h, p)
                nc.vector.tensor_reduce(top[:, p], probs[:, p], AX_X, ALU.max).then_inc(top_ready, 1)
                reached(dve, top_ready, h, p)
                nc.vector.tensor_tensor(probs[:, p], probs[:, p], top[:, p].unsqueeze(2).to_broadcast([P, H, K]),
                                        ALU.subtract).then_inc(shifted, 1)

            run_stages(dve, [(3, divide), (0, statistics), (2, shift), (4, residual), (0, normalise)])

        @block.scalar
        def _(act):
            flat = "p c t -> p (c t)"

            def keep_attnT(h, p):
                reached(act, attnT_psum, h, p)
                freed(act, y_psum, h, p, back=1)
                nc.scalar.copy(attnT[:].rearrange(flat), psV).then_inc(attnT_ready, 1)

            def keep_xnT(h, p):
                reached(act, xnT_psum, h, p)
                freed(act, qT_psum, h, p, back=1)
                nc.scalar.copy(xnT[:].rearrange(flat), psT).then_inc(xnT_ready, 1)

            def keep_qT(h, p):
                reached(act, qT_psum, h, p)
                freed(act, scores, h, p, DC, DC)
                nc.scalar.copy(qT[:, p].rearrange(flat), psQ).then_inc(qT_ready, 1)

            def keep_pT(h, p):
                for g in range(4):
                    reached(act, pT_psum, h, p, g + 1, 4)
                    nc.scalar.copy(pT[:, g % 2].rearrange("k n t -> k (n t)"), psP(g)).then_inc(pT_ready, 1)

            def exponentials(h, p):
                reached(act, shifted, h, p)
                flat_p = probs[:, p].rearrange("t n k -> t (n k)")
                nc.scalar.activation(flat_p, flat_p, ACT.Exp).then_inc(exp_ready, 1)

            run_stages(act, [(2, keep_qT), (1, keep_xnT), (3, keep_pT), (3, keep_attnT), (2, exponentials)])

        @block.tensor
        def _(pe):
            def turn_xn(h, p):
                reached(pe, xn_ready, h, p)
                freed(pe, xnT_ready, h, p, back=1)
                for c in range(DC):
                    mm = nc.tensor.transpose(psT[:, c * P:(c + 1) * P], xn[:, p, c * P:(c + 1) * P], ident[:])
                mm.then_inc(xnT_psum, 1)

            def out_projection(h, p):
                reached(pe, attnT_ready, h, p)
                freed(pe, x_added, h, p, back=1)
                for c in range(DC):
                    mm = nc.tensor.matmul(psY, attnT[:, c, :], wo[:, c, :], start=c == 0, stop=c == DC - 1)
                mm.then_inc(y_psum, 1)

            def queries(h, p):
                reached(pe, xnT_ready, h, p)
                freed(pe, qT_ready, h, p, back=1)
                for j in range(DC):
                    for c in range(DC):
                        mm = nc.tensor.matmul(psQ[:, j * P:(j + 1) * P], wq[:, c, j * P:(j + 1) * P], xnT[:, c, :],
                                              start=c == 0, stop=c == DC - 1)
                mm.then_inc(qT_psum, 1)

            def score(h, p):
                reached(pe, qT_ready, h, p)
                for j in range(DC):
                    if j < 2:
                        freed(pe, biased, h, p, j + 3, DC, back=1)
                    else:
                        reached(pe, biased, h, p, j - 1, DC)
                    nc.tensor.matmul(psS(j), qT[:, p, j, :], keys[:, p, j, :], start=True, stop=True).then_inc(scores, 1)

            def attend(h, p):
                reached(pe, probs_ready, h, p)
                freed(pe, attnT_ready, h, p, back=1)

                def turn(g):
                    if g < 2:
                        freed(pe, pT_ready, h, p, g + 3, 4, back=1)
                    else:
                        reached(pe, pT_ready, h, p, g - 1, 4)
                    for n in range(HC):
                        mm = nc.tensor.transpose(psP(g)[:, n * P:(n + 1) * P], probs[:, p, g * HC + n, :], ident[:])
                    mm.then_inc(pT_psum, 1)

                def mix(g):
                    reached(pe, pT_ready, h, p, g + 1, 4)
                    for n in range(HC):
                        mm = nc.tensor.matmul(psV[:, g * P:(g + 1) * P], values[:, p, g * HC + n], pT[:, g % 2, n, :],
                                              start=n == 0, stop=n == HC - 1)
                    if g == 3:
                        mm.then_inc(attnT_psum, 1)

                turn(0)
                turn(1)
                for g in range(4):
                    mix(g)
                    if g < 2:
                        turn(g + 2)

            pe.wait_ge(w_in, 32)
            run_stages(pe, [(2, queries), (4, out_projection), (2, score), (1, turn_xn), (3, attend)])



F = 4 * D
FC = F // P
ROUND = 1.5 * 2.0 ** 23


def l0_ffn(nc, d, x, ident, ones, minus_half, eps, consts):
    with ExitStack() as ctx:
        ph = Phase(nc, ctx, "f0")
        w1 = ph.sb("w1", [P, DC, F], BF16)
        w2 = ph.sb("w2", [P, FC, D], BF16)
        b1 = ph.sb("b1", [P, F])
        b2 = ph.sb("b2", [P, D])
        w_unit = ph.sb("w_unit", [P, 2])
        identb = ph.sb("identb", [P, P], BF16)
        ps = ph.banks()
        b_in = ph.sem("b_in")

        with ExitStack() as ctx2:
            ph2 = Phase(nc, ctx2, "f0s")
            raw = ph2.sb("raw", [P, 2, 4, F])
            sums = ph2.sb("sums", [P, 2, 4])
            sum1 = ph2.sb("sum1", [P, 2])
            mean = ph2.sb("mean", [P, 2])
            inv = ph2.sb("inv", [P, 2])
            w_in = [ph2.sem(f"w_in{n}") for n in range(2)]
            summed, sum_ready, sum_psum, mean_ready, inv_ready, clipped, scaled, w_ready = (
                ph2.sem(n) for n in "summed sum_ready sum_psum mean_ready inv_ready clipped scaled w_ready".split())
            with nc.Block() as block:
                @block.sync
                def _(sp):
                    sp.dma_start(raw[:, 0], d["w_f0_1"]).then_inc(w_in[0], 16)
                    sp.dma_start(raw[:, 1], d["w_f0_2"]).then_inc(w_in[1], 16)
                    sp.dma_start(b1[:], d["b_f0_1"]).then_inc(b_in, 16)
                    sp.dma_start(b2[:], d["b_f0_2"]).then_inc(b_in, 16)

                @block.vector
                def _(dve):
                    nc.vector.tensor_copy(identb[:], ident[:])
                    for n in range(2):
                        dve.wait_ge(w_in[n], 16)
                        nc.vector.tensor_reduce(sums[:, n], raw[:, n], AX_X, ALU.add,
                                                apply_absolute_value=True).then_inc(summed, 1)
                    dve.wait_ge(summed, 2)
                    nc.vector.tensor_reduce(sum1[:], sums[:], AX_X, ALU.add).then_inc(sum_ready, 1)
                    dve.wait_ge(sum_psum, 1)
                    nc.vector.tensor_scalar(mean[:], ps[:, 0, 0:2], 1.0 / (D * F), 1e-5, ALU.mult,
                                            ALU.max).then_inc(mean_ready, 1)
                    dve.wait_ge(mean_ready, 1)
                    nc.vector.reciprocal(inv[:], mean[:]).then_inc(inv_ready, 1)
                    nc.vector.tensor_scalar(w_unit[:], mean[:], 1.0 / 127.0, None, ALU.mult)
                    dve.wait_ge(inv_ready, 1)
                    for n in range(2):
                        for q in range(4):
                            part = raw[:, n, q]
                            nc.vector.tensor_scalar(part, part, inv[:, n:n + 1], 1.0, ALU.mult, ALU.min).then_inc(clipped, 1)
                            dve.wait_ge(clipped, 4 * n + q + 1)
                            nc.vector.tensor_scalar(part, part, -1.0, ROUND, ALU.max, ALU.add).then_inc(scaled, 1)

                @block.tensor
                def _(pe):
                    pe.wait_ge(sum_ready, 1)
                    nc.tensor.matmul(ps[:, 0, 0:2], ones[:], sum1[:], start=True, stop=True).then_inc(sum_psum, 1)

                @block.scalar
                def _(act):
                    for n in range(2):
                        for q in range(4):
                            act.wait_ge(scaled, 4 * n + q + 1)
                            to = w1[:, q] if n == 0 else w2[:, 4 * q:4 * q + 4].rearrange("p f n -> p (f n)")
                            nc.scalar.activation(to, raw[:, n, q], ACT.Copy, bias=-ROUND).then_inc(w_ready, 1)

        xn = ph.sb("xn", [P, 2, D])
        qx = ph.sb("qx", [P, 2, D], BF16)
        qxT = ph.sb("qxT", [P, 2, DC, P], BF16)
        stats = ph.sb("stats", [P, 2, 6])
        mv = ph.sb("mv", [P, 2, 2])
        rs = ph.sb("rs", [P, 2, 6])
        ax = ph.sb("ax", [P, 2, 4])
        sx = ph.sb("sx", [P, 8])
        hid = ph.sb("hid", [P, 2, F])
        squares = ph.sb("squares", [P, F])
        ssh = ph.sb("ssh", [P, 2])
        rh = ph.sb("rh", [P, 2, 3])
        ah = ph.sb("ah", [P, 2, 4])
        sh = ph.sb("sh", [P, 2])
        qh = ph.sb("qh", [P, 2, F], BF16)
        qhT = ph.sb("qhT", [P, 2, FC, P], BF16)
        inv_f = ph.sb("inv_f", [P, 1])
        psT = ps[:, 0, 0:D // 2].bitcast(BF16)
        psH = lambda n: ps[:, 1 + n]
        psU = [ps[:, 5 + n].bitcast(BF16) for n in range(2)]
        psY = ps[:, 7]

        names = ("stats_done mv_ready rs_own rx_ready xn_ready top_ready ax_own kx_ready rounded qx_ready qxT_psum "
                 "qxT_ready b2_added h_psum h_biased gelu_done square_done hsquare_own rh_ready toph_ready ah_own "
                 "kh_ready h_rounded qh_ready qhT_psum qhT_ready y_psum x_added made").split()
        (stats_done, mv_ready, rs_own, rx_ready, xn_ready, top_ready, ax_own, kx_ready, rounded, qx_ready, qxT_psum,
         qxT_ready, b2_added, h_psum, h_biased, gelu_done, square_done, hsquare_own, rh_ready, toph_ready, ah_own,
         kh_ready, h_rounded, qh_ready, qhT_psum, qhT_ready, y_psum, x_added, made) = (ph.sem(n) for n in names)
        block = ctx.enter_context(nc.Block())

        @block.gpsimd
        def _(pool):
            nc.gpsimd.memset(inv_f[:], 1.0 / F).then_inc(made, 1)
            pool.wait_ge(made, 1)
            pool.wait_ge(b_in, 32)
            tt = nc.gpsimd.tensor_tensor

            def x_roots(h, p):
                v = mv[:, p, 1:2]
                r = [rs[:, p, n:n + 1] for n in range(6)]
                reached(pool, mv_ready, h, p)
                freed(pool, kx_ready, h, p)
                steps = [(r[0], v, eps[:], ALU.add), (r[1], r[0], minus_half[:, 0:1], ALU.pow), (r[2], v, r[1], ALU.mult),
                         (r[3], r[2], r[1], ALU.mult), (r[4], r[3], eps[:], ALU.add),
                         (r[5], r[4], minus_half[:, 0:1], ALU.pow)]
                for n, (out, a, b, op) in enumerate(steps):
                    if n:
                        reached(pool, rs_own, h, p, n, 6)
                    tt(out, a, b, op).then_inc(rs_own, 1)

            def add_b2(h, p):
                reached(pool, xn_ready, h, p)
                tt(x[:, p, h, :], x[:, p, h, :], b2[:], ALU.add).then_inc(b2_added, 1)

            def h_root(h, p):
                reached(pool, square_done, h, p)
                freed(pool, kh_ready, h, p)
                tt(rh[:, p, 0:1], ssh[:, p:p + 1], inv_f[:], ALU.mult).then_inc(hsquare_own, 1)
                reached(pool, hsquare_own, h, p, 1, 2)
                tt(rh[:, p, 1:2], rh[:, p, 0:1], eps[:], ALU.add).then_inc(hsquare_own, 1)
                reached(pool, hsquare_own, h, p, 2, 2)
                tt(rh[:, p, 2:3], rh[:, p, 1:2], minus_half[:, 0:1], ALU.pow).then_inc(rh_ready, 1)

            def round_h(h, p):
                freed(pool, qhT_psum, h, p, 2, 2)
                reached(pool, h_rounded, h, p)
                carry_wait(nc, pool, consts)
                nc.gpsimd.tensor_scalar(qh[:, p], hid[:, p], -ROUND, 1.0, ALU.add, ALU.mult).then_inc(qh_ready, 1)

            run_stages(pool, [(3, round_h), (0, x_roots), (2, h_root), (2, add_b2)])

        @block.vector
        def _(dve):
            def statistics(h, p):
                nc.vector.bn_stats(stats[:, p, :], x[:, p, h, :]).then_inc(stats_done, 1)
                reached(dve, stats_done, h, p)
                freed(dve, rs_own, h, p, 3, 6)
                carry_wait(nc, dve, consts)
                nc.vector.bn_aggr(mv[:, p, :], stats[:, p, :]).then_inc(mv_ready, 1)

            def normalise(h, p):
                reached(dve, rs_own, h, p, 2, 6)
                freed(dve, rounded, h, p)
                nc.vector.tensor_scalar(xn[:, p, :], x[:, p, h, :], mv[:, p, 0:1], rs[:, p, 1:2],
                                        ALU.subtract, ALU.mult).then_inc(xn_ready, 1)
                reached(dve, xn_ready, h, p)
                freed(dve, ax_own, h, p, 1, 2)
                nc.vector.tensor_reduce(ax[:, p, 0:1], xn[:, p, :], AX_X, ALU.max,
                                        apply_absolute_value=True).then_inc(top_ready, 1)

            def quantise(h, p):
                reached(dve, top_ready, h, p)
                reached(dve, rs_own, h, p, 6, 6)
                freed(dve, kx_ready, h, p)
                nc.vector.tensor_scalar(ax[:, p, 1:2], ax[:, p, 0:1], rs[:, p, 5:6], 1e-5, ALU.mult,
                                        ALU.max).then_inc(ax_own, 1)
                reached(dve, ax_own, h, p, 1, 2)
                nc.vector.reciprocal(ax[:, p, 2:3], ax[:, p, 1:2]).then_inc(ax_own, 1)
                nc.vector.tensor_scalar(sx[:, p:p + 1], ax[:, p, 1:2], w_unit[:, 0:1], None, ALU.mult)
                reached(dve, ax_own, h, p, 2, 2)
                freed(dve, rounded, h, p)
                nc.vector.tensor_scalar(ax[:, p, 3:4], ax[:, p, 2:3], rs[:, p, 5:6], 127.0, ALU.mult,
                                        ALU.mult).then_inc(kx_ready, 1)
                reached(dve, kx_ready, h, p)
                nc.vector.tensor_scalar(xn[:, p], xn[:, p], ax[:, p, 3:4], ROUND, ALU.mult, ALU.add).then_inc(rounded, 1)
                reached(dve, rounded, h, p)
                freed(dve, qxT_psum, h, p)
                nc.vector.tensor_scalar(qx[:, p], xn[:, p], -ROUND, None, ALU.add).then_inc(qx_ready, 1)

            def bias(h, p):
                freed(dve, qh_ready, h, p)
                for n in range(4):
                    reached(dve, h_psum, h, p, n + 1, 4)
                    cols = slice(n * D, (n + 1) * D)
                    nc.vector.scalar_tensor_tensor(out=hid[:, p, cols], in0=psH(n), scalar=sx[:, p:p + 1],
                                                   in1=b1[:, cols], op0=ALU.mult, op1=ALU.add).then_inc(h_biased, 1)

            def top_h(h, p):
                reached(dve, gelu_done, h, p)
                freed(dve, ah_own, h, p, 1, 2)
                nc.vector.tensor_reduce(ah[:, p, 0:1], hid[:, p], AX_X, ALU.max,
                                        apply_absolute_value=True).then_inc(toph_ready, 1)

            def scale_h(h, p):
                reached(dve, toph_ready, h, p)
                reached(dve, rh_ready, h, p)
                freed(dve, kh_ready, h, p)
                nc.vector.tensor_scalar(ah[:, p, 1:2], ah[:, p, 0:1], rh[:, p, 2:3], 1e-5, ALU.mult,
                                        ALU.max).then_inc(ah_own, 1)
                reached(dve, ah_own, h, p, 1, 2)
                nc.vector.reciprocal(ah[:, p, 2:3], ah[:, p, 1:2]).then_inc(ah_own, 1)
                freed(dve, x_added, h, p)
                nc.vector.tensor_scalar(sh[:, p:p + 1], ah[:, p, 1:2], w_unit[:, 1:2], None, ALU.mult)
                reached(dve, ah_own, h, p, 2, 2)
                freed(dve, h_rounded, h, p)
                nc.vector.tensor_scalar(ah[:, p, 3:4], ah[:, p, 2:3], rh[:, p, 2:3], 127.0, ALU.mult,
                                        ALU.mult).then_inc(kh_ready, 1)

            def residual(h, p):
                reached(dve, y_psum, h, p)
                reached(dve, b2_added, h, p)
                nc.vector.scalar_tensor_tensor(out=x[:, p, h, :], in0=psY, scalar=sh[:, p:p + 1], in1=x[:, p, h, :],
                                               op0=ALU.mult, op1=ALU.add).then_inc(x_added, 1)

            run_stages(dve, [(3, scale_h), (1, normalise), (2, bias), (0, statistics), (1, quantise), (2, top_h), (4, residual)])

        @block.scalar
        def _(act):
            def keep_qxT(h, p):
                reached(act, qxT_psum, h, p)
                freed(act, h_psum, h, p, 4, 4)
                nc.scalar.copy(qxT[:, p].rearrange("p c t -> p (c t)"), psT).then_inc(qxT_ready, 1)

            def keep_qhT(h, p):
                freed(act, y_psum, h, p)
                for n in range(2):
                    reached(act, qhT_psum, h, p, n + 1, 2)
                    nc.scalar.copy(qhT[:, p, 8 * n:8 * n + 8].rearrange("p c t -> p (c t)"), psU[n]).then_inc(qhT_ready, 1)

            def gelu(h, p):
                reached(act, h_biased, h, p, 4, 4)
                nc.scalar.activation(hid[:, p], hid[:, p], ACT.Gelu).then_inc(gelu_done, 1)
                reached(act, gelu_done, h, p)
                freed(act, hsquare_own, h, p, 1, 2)
                nc.scalar.activation(squares[:], hid[:, p], ACT.Square, accum_out=ssh[:, p:p + 1]).then_inc(square_done, 1)

            def scale_h(h, p):
                reached(act, kh_ready, h, p)
                nc.scalar.activation(hid[:, p], hid[:, p], ACT.Copy, scale=ah[:, p, 3:4], bias=ROUND).then_inc(h_rounded, 1)

            run_stages(act, [(3, scale_h), (2, gelu), (1, keep_qxT), (3, keep_qhT)])

        @block.tensor
        def _(pe):
            def turn_x(h, p):
                reached(pe, qx_ready, h, p)
                freed(pe, qxT_ready, h, p, back=1)
                for c in range(DC):
                    mm = nc.tensor.transpose(psT[:, c * P:(c + 1) * P], qx[:, p, c * P:(c + 1) * P], identb[:])
                mm.then_inc(qxT_psum, 1)

            def turn_h(h, p):
                reached(pe, qh_ready, h, p)
                for n in range(2):
                    freed(pe, qhT_ready, h, p, n + 1, 2, back=1)
                    for c in range(8):
                        mm = nc.tensor.transpose(psU[n][:, c * P:(c + 1) * P],
                                                 qh[:, p, (8 * n + c) * P:(8 * n + c + 1) * P], identb[:])
                    mm.then_inc(qhT_psum, 1)

            def up(h, p):
                reached(pe, qxT_ready, h, p)
                for n in range(4):
                    freed(pe, h_biased, h, p, n + 1, 4, back=1)
                    for c in range(DC):
                        mm = nc.tensor.matmul(psH(n), qxT[:, p, c, :], w1[:, c, n * D:(n + 1) * D],
                                              start=c == 0, stop=c == DC - 1)
                    mm.then_inc(h_psum, 1)

            def down(h, p):
                freed(pe, x_added, h, p, back=1)
                for c in range(FC):
                    if c % 8 == 0:
                        reached(pe, qhT_ready, h, p, c // 8 + 1, 2)
                    mm = nc.tensor.matmul(psY, qhT[:, p, c, :], w2[:, c, :], start=c == 0, stop=c == FC - 1)
                mm.then_inc(y_psum, 1)

            run_stages(pe, [(2, up), (4, down), (1, turn_x), (3, turn_h)])



SEG = 64
CW = P + HC


def split_weights(nc, ph, d, names, shape, first=()):
    high = ph.sb("w_high", [P, len(names), *shape], BF16)
    low = ph.sb("w_low", [P, len(names), *shape], BF16)
    with ExitStack() as ctx2:
        ph2 = Phase(nc, ctx2, ph.name + "w")
        raw = ph2.sb("raw", [P, len(names), *shape])
        w_in = [ph2.sem(f"w_in{n}") for n in range(len(names))]
        high_made, low_made = ph2.sem("high_made"), ph2.sem("low_made")
        with nc.Block() as block:
            @block.sync
            def _(sp):
                for n, name in enumerate(names):
                    sp.dma_start(raw[:, n], d[name]).then_inc(w_in[n], 16)

            @block.scalar
            def _(act):
                for n in range(len(names)):
                    act.wait_ge(w_in[n], 16)
                    nc.scalar.copy(high[:, n], raw[:, n]).then_inc(high_made, 1)

            @block.vector
            def _(dve):
                for n in range(len(names)):
                    dve.wait_ge(high_made, n + 1)
                    nc.vector.tensor_tensor(low[:, n], raw[:, n], high[:, n], ALU.subtract).then_inc(low_made, 1)
    return high, low


def l1_attention(nc, d, x, ident, minus_half, eps, consts):
    with ExitStack() as ctx:
        ph = Phase(nc, ctx, "a1")
        wh, wl = split_weights(nc, ph, d, [f"w_a1{n}" for n in "qkvo"], [DC, D])
        WQ, WK, WV, WO = range(4)
        beta = ph.sb("beta", [P, H])
        rest = ph.sb("rest", [P, H])
        causal = ph.sb("causal", [P, SEG])
        blocks = ph.sb("blocks", [P, CW])
        memory = ph.sb("memory", [P, B, DC, CW])
        kdiag = ph.sb("kdiag", [P, 2, DC, 2, HC, SEG])
        pdiag = ph.sb("pdiag", [P, 2, H, P])
        vd = ph.sb("vd", [P, 2, DC, CW])
        xn = ph.sb("xn", [P, 2, D])
        xh = ph.sb("xh", [P, 2, DC, P], BF16)
        xl = ph.sb("xl", [P, 2, DC, P], BF16)
        ah = ph.sb("ah", [P, 2, DC, P], BF16)
        al = ph.sb("al", [P, 2, DC, P], BF16)
        stats = ph.sb("stats", [P, 2, 6])
        mv = ph.sb("mv", [P, 2, 2])
        rs = ph.sb("rs", [P, 2, 2])
        expo = ph.sb("expo", [P, 2, DC, 2, SEG])
        relu = ph.sb("relu", [P, 2, DC, 2, SEG])
        qT = ph.sb("qT", [P, 2, DC, P])
        skq = ph.sb("skq", [P, 2, DC, 4, SEG])
        sk = ph.sb("sk", [P, 2, D])
        v = ph.sb("v", [P, 2, D])
        den = ph.sb("den", [P, 2, H])
        rden = ph.sb("rden", [P, 2, H])
        rden_b = ph.sb("rden_b", [P, 2, H])
        v_prev = ph.sb("v_prev", [P, D])
        update = ph.sb("update", [P, 2, DC, CW])
        from_memory = ph.sb("from_memory", [P, 2, D])
        score = ph.sb("score", [P, 2, H, SEG])
        top = ph.sb("top", [P, 2, H])
        total = ph.sb("total", [P, 2, H])
        inv = ph.sb("inv", [P, 2, H])
        inv_r = ph.sb("inv_r", [P, 2, H])
        pT = ph.sb("pT", [P, 2, HC, P])
        mixed = ph.sb("mixed", [P, D])
        a = ph.sb("a", [P, 2, D])
        ps = ph.banks()
        psT, psA, psB, psP = ps[:, 0], ps[:, 1], ps[:, 2], ps[:, 5]
        psS = ps[:, 3:5].rearrange("p b n -> p (b n)")
        psM = ps[:, 6:8, 0:2 * CW].rearrange("p b (c n) -> p b c n", c=2)

        made, beta_in, causal_made = ph.sem("made"), ph.sem("beta_in"), ph.sem("causal_made")
        with nc.Block() as block:
            @block.sync
            def _(sp):
                sp.dma_start(beta[:], d["beta"]).then_inc(beta_in, 16)

            @block.scalar
            def _(act):
                act.wait_ge(beta_in, 16)
                nc.scalar.activation(beta[:], beta[:], ACT.Sigmoid).then_inc(beta_in, 1)
                act.wait_ge(beta_in, 17)
                nc.scalar.activation(rest[:], beta[:], ACT.Copy, scale=-1.0, bias=1.0)

            @block.vector
            def _(dve):
                nc.vector.memset(memory[:], 0.0)
                nc.vector.memset(blocks[:], 0.0).then_inc(made, 1)
                dve.wait_ge(made, 1)
                for g in range(HC):
                    nc.vector.memset(blocks[g * DK:(g + 1) * DK, g * DK:(g + 1) * DK], 1.0)
                    nc.vector.memset(blocks[g * DK:(g + 1) * DK, P + g:P + g + 1], 1.0)
                nc.vector.memset(kdiag[:], 0.0)
                nc.vector.memset(vd[:], 1.0)

            @block.gpsimd
            def _(pool):
                nc.gpsimd.memset(pdiag[:], 0.0).then_inc(causal_made, 1)
                nc.gpsimd.memset(causal[:], 0.0).then_inc(causal_made, 1)
                for s in range(2):
                    pool.wait_ge(causal_made, 2 + s)
                    half = causal[s * SEG:(s + 1) * SEG]
                    nc.gpsimd.affine_select(out=half, in_=half, compare_op=ALU.is_ge, fill=NEG, base=0,
                                            pattern=[[-1, SEG]], channel_multiplier=1).then_inc(causal_made, 1)

        names = ("stats_done mv_ready var_ready rstd_ready xn_ready xnT_psum xh_ready xl_ready q_psum q_expo q_relu "
                 "q_read k_psum k_expo k_relu k_read v_psum v_ready sq_ready sk_ready skT_psum sk_kept readout "
                 "den_ready rden_ready beta_ready vprev_ready vd_ready fm_ready u_psum masked m_ready scores biased "
                 "top_ready shifted probs_ready e_ready total_ready inv_ready invr_ready pT_psum pT_ready pv mixed_ready "
                 "a_ready aT_psum ah_ready al_ready y_psum x_added").split()
        (stats_done, mv_ready, var_ready, rstd_ready, xn_ready, xnT_psum, xh_ready, xl_ready, q_psum, q_expo, q_relu,
         q_read, k_psum, k_expo, k_relu, k_read, v_psum, v_ready, sq_ready, sk_ready, skT_psum, sk_kept, readout,
         den_ready, rden_ready, beta_ready, vprev_ready, vd_ready, fm_ready, u_psum, masked, m_ready, scores, biased,
         top_ready, shifted, probs_ready, e_ready, total_ready, inv_ready, invr_ready, pT_psum, pT_ready, pv, mixed_ready,
         a_ready, aT_psum, ah_ready, al_ready, y_psum, x_added) = (ph.sem(n) for n in names)
        block = ctx.enter_context(nc.Block())
        rows = [slice(0, SEG), slice(SEG, P)]

        def heads(ap):
            return ap.rearrange("t (n k) -> t n k", k=DK)

        @block.gpsimd
        def _(pool):
            def layernorm_scale(h, p):
                reached(pool, mv_ready, h, p)
                freed(pool, xn_ready, h, p)
                nc.gpsimd.tensor_tensor(rs[:, p, 0:1], mv[:, p, 1:2], eps[:], ALU.add).then_inc(var_ready, 1)
                reached(pool, var_ready, h, p)
                nc.gpsimd.tensor_tensor(rs[:, p, 1:2], rs[:, p, 0:1], minus_half[:, 0:1], ALU.pow).then_inc(rstd_ready, 1)

            def remember(s):
                def stage(h, p):
                    reached(pool, masked, h, p, s + 1, 2)
                    nc.gpsimd.tensor_tensor(memory[:, p], memory[:, p], update[:, s], ALU.add).then_inc(m_ready, 1)
                return stage

            run_stages(pool, [(3, remember(0)), (0, layernorm_scale), (3, remember(1))])

        @block.vector
        def _(dve):
            def statistics(h, p):
                nc.vector.bn_stats(stats[:, p, :], x[:, p, h, :]).then_inc(stats_done, 1)
                reached(dve, stats_done, h, p)
                freed(dve, var_ready, h, p)
                carry_wait(nc, dve, consts)
                nc.vector.bn_aggr(mv[:, p, :], stats[:, p, :]).then_inc(mv_ready, 1)

            def normalise(h, p):
                reached(dve, rstd_ready, h, p)
                freed(dve, xnT_psum, h, p)
                nc.vector.tensor_scalar(xn[:, p, :], x[:, p, h, :], mv[:, p, 0:1], rs[:, p, 1:2],
                                        ALU.subtract, ALU.mult).then_inc(xn_ready, 1)

            def low_xn(h, p):
                reached(dve, xh_ready, h, p)
                freed(dve, v_psum, h, p)
                flat = "p c t -> p (c t)"
                nc.vector.tensor_tensor(xl[:, p].rearrange(flat), psT, xh[:, p].rearrange(flat),
                                        ALU.subtract).then_inc(xl_ready, 1)

            def low_a(h, p):
                reached(dve, ah_ready, h, p)
                freed(dve, y_psum, h, p)
                flat = "p c t -> p (c t)"
                nc.vector.tensor_tensor(al[:, p].rearrange(flat), psT, ah[:, p].rearrange(flat),
                                        ALU.subtract).then_inc(al_ready, 1)

            def sigma_q(h, p):
                reached(dve, q_relu, h, p)
                freed(dve, readout, h, p, 2, 2)
                for s in range(2):
                    nc.vector.scalar_tensor_tensor(out=skq[:, p, :, 3 * s], in0=expo[:, 0, :, s], scalar=1.0,
                                                   in1=relu[:, 0, :, s], op0=ALU.min, op1=ALU.add).then_inc(sq_ready, 1)

            def sigma_k(h, p):
                reached(dve, k_relu, h, p)
                freed(dve, skT_psum, h, p)
                nc.vector.scalar_tensor_tensor(out=skq[:, p, :, 1:3], in0=expo[:, 1], scalar=1.0, in1=relu[:, 1],
                                               op0=ALU.min, op1=ALU.add).then_inc(sk_ready, 1)

            def read_memory(s):
                def stage(h, p):
                    here, k_rows, q_rows = rows[s], rows[1 - s], rows[s]
                    reached(dve, readout, h, p, s + 1, 2)
                    flat_den = den[:, s].rearrange("p (b c n) -> p b c n", b=2, c=2)
                    nc.vector.tensor_scalar(flat_den, psM[:, :, :, P:CW], 1e-6, None, ALU.add).then_inc(den_ready, 1)
                    reached(dve, den_ready, h, p, s + 1, 2)
                    nc.vector.reciprocal(rden[:, s], den[:, s]).then_inc(rden_ready, 1)
                    reached(dve, rden_ready, h, p, s + 1, 2)
                    for b in range(2):
                        cols = slice(b * 8 * DK, (b + 1) * 8 * DK)
                        nc.vector.tensor_tensor(
                            v_prev[here, cols].rearrange("t (c n k) -> t c n k", c=2, k=DK),
                            psM[k_rows, b, :, 0:P].rearrange("t c (n k) -> t c n k", k=DK),
                            rden[k_rows, s, b * 8:b * 8 + 8].rearrange("t (c n) -> t c n", c=2).unsqueeze(3)
                            .to_broadcast([SEG, 2, HC, DK]), ALU.mult).then_inc(vprev_ready, 1)
                    reached(dve, vprev_ready, h, p, 2 * s + 2, 4)
                    reached(dve, v_ready, h, p)
                    nc.vector.tensor_tensor(vd[here, p, :, 0:P], v[here, p].rearrange("t (c n) -> t c n", c=DC),
                                            v_prev[here].rearrange("t (c n) -> t c n", c=DC),
                                            ALU.subtract).then_inc(vd_ready, 1)
                    nc.vector.tensor_tensor(rden_b[q_rows, s], rden[q_rows, s], beta[q_rows], ALU.mult).then_inc(beta_ready, 1)
                    reached(dve, beta_ready, h, p, s + 1, 2)
                    freed(dve, a_ready, h, p)
                    for b in range(2):
                        cols = slice(b * 8 * DK, (b + 1) * 8 * DK)
                        nc.vector.tensor_tensor(
                            from_memory[here, p, cols].rearrange("t (c n k) -> t c n k", c=2, k=DK),
                            psM[q_rows, b, :, 0:P].rearrange("t c (n k) -> t c n k", k=DK),
                            rden_b[q_rows, s, b * 8:b * 8 + 8].rearrange("t (c n) -> t c n", c=2).unsqueeze(3)
                            .to_broadcast([SEG, 2, HC, DK]), ALU.mult).then_inc(fm_ready, 1)
                return stage

            def mask_update(s):
                def stage(h, p):
                    reached(dve, u_psum, h, p, s + 1, 2)
                    freed(dve, m_ready, h, p, s + 1, 2, back=1)
                    nc.vector.tensor_tensor(update[:, s].rearrange("p (b c) n -> p b c n", b=2), psM,
                                            blocks[:].unsqueeze(1).unsqueeze(1).to_broadcast([P, 2, 2, CW]),
                                            ALU.mult).then_inc(masked, 1)
                return stage

            def shift(h, p):
                reached(dve, scores, h, p)
                freed(dve, total_ready, h, p)
                nc.vector.tensor_tensor(score[:, p], psS.rearrange("t (n k) -> t n k", n=H),
                                        causal[:].unsqueeze(1).to_broadcast([P, H, SEG]), ALU.add).then_inc(biased, 1)
                reached(dve, biased, h, p)
                freed(dve, shifted, h, p)
                nc.vector.tensor_reduce(top[:, p], score[:, p], AX_X, ALU.max).then_inc(top_ready, 1)
                reached(dve, top_ready, h, p)
                nc.vector.tensor_tensor(score[:, p], score[:, p], top[:, p].unsqueeze(2).to_broadcast([P, H, SEG]),
                                        ALU.subtract).then_inc(shifted, 1)

            def combine(h, p):
                reached(dve, e_ready, h, p)
                nc.vector.tensor_reduce(total[:, p], score[:, p], AX_X, ALU.add).then_inc(total_ready, 1)
                reached(dve, total_ready, h, p)
                nc.vector.reciprocal(inv[:, p], total[:, p]).then_inc(inv_ready, 1)
                reached(dve, inv_ready, h, p)
                nc.vector.tensor_tensor(inv_r[:, p], inv[:, p], rest[:], ALU.mult).then_inc(invr_ready, 1)
                reached(dve, invr_ready, h, p)
                reached(dve, pv, h, p)
                freed(dve, a_ready, h, p, back=1)
                nc.vector.tensor_tensor(heads(mixed[:]), heads(psP), inv_r[:, p].unsqueeze(2).to_broadcast([P, H, DK]),
                                        ALU.mult).then_inc(mixed_ready, 1)
                reached(dve, mixed_ready, h, p)
                reached(dve, fm_ready, h, p, 4, 4)
                freed(dve, aT_psum, h, p)
                nc.vector.tensor_tensor(a[:, p], mixed[:], from_memory[:, p], ALU.add).then_inc(a_ready, 1)

            def residual(h, p):
                reached(dve, y_psum, h, p)
                nc.vector.tensor_tensor(x[:, p, h, :], psB, x[:, p, h, :], ALU.add).then_inc(x_added, 1)

            run_stages(dve, [(3, read_memory(0)), (5, low_a), (3, mask_update(0)), (1, low_xn), (4, shift),
                             (3, read_memory(1)), (2, sigma_q), (5, residual), (0, statistics), (3, mask_update(1)),
                             (2, sigma_k), (0, normalise), (4, combine)])

        @block.scalar
        def _(act):
            flat = "p c t -> p (c t)"
            halves = "p (c s t) -> p c s t"

            def high_xn(h, p):
                reached(act, xnT_psum, h, p)
                freed(act, v_psum, h, p)
                nc.scalar.copy(xh[:, p].rearrange(flat), psT).then_inc(xh_ready, 1)

            def high_a(h, p):
                reached(act, aT_psum, h, p)
                freed(act, y_psum, h, p)
                nc.scalar.copy(ah[:, p].rearrange(flat), psT).then_inc(ah_ready, 1)

            def keep_sk(h, p):
                reached(act, skT_psum, h, p)
                freed(act, u_psum, h, p, 2, 2)
                nc.scalar.copy(sk[:, p], psT).then_inc(sk_kept, 1)

            def keep_pT(h, p):
                for g in range(4):
                    reached(act, pT_psum, h, p, g + 1, 4)
                    nc.scalar.copy(pT[:, g % 2].rearrange(flat), psS[:, g % 2 * 512:(g % 2 + 1) * 512]).then_inc(pT_ready, 1)

            def keep_q(h, p):
                reached(act, q_psum, h, p)
                freed(act, sq_ready, h, p, 2, 2, back=1)
                view = psA.rearrange(halves, c=DC, s=2)
                nc.scalar.activation(expo[:, 0], view, ACT.Exp).then_inc(q_expo, 1)
                nc.scalar.activation(relu[:, 0], view, ACT.Relu).then_inc(q_relu, 1)
                freed(act, scores, h, p)
                nc.scalar.activation(qT[:, p].rearrange(flat), psA, ACT.Copy, scale=float(DK) ** -0.5).then_inc(q_read, 1)

            def keep_k(h, p):
                reached(act, k_psum, h, p)
                freed(act, sk_ready, h, p, back=1)
                view = psB.rearrange(halves, c=DC, s=2)
                nc.scalar.activation(expo[:, 1], view, ACT.Exp).then_inc(k_expo, 1)
                nc.scalar.activation(relu[:, 1], view, ACT.Relu).then_inc(k_relu, 1)
                freed(act, scores, h, p)
                for g in range(HC):
                    r = slice(g * DK, (g + 1) * DK)
                    nc.scalar.copy(kdiag[r, p, :, :, g], psB[r].rearrange(halves, c=DC, s=2)).then_inc(k_read, 1)

            def keep_v(h, p):
                reached(act, v_psum, h, p)
                freed(act, pv, h, p)
                freed(act, vd_ready, h, p, 2, 2)
                nc.scalar.copy(v[:, p], psA).then_inc(v_ready, 1)

            def exponentials(h, p):
                reached(act, shifted, h, p)
                freed(act, pT_psum, h, p, 4, 4)
                for s in range(2):
                    nc.scalar.activation(pdiag[rows[s], p, :, rows[s]], score[rows[s], p], ACT.Exp).then_inc(probs_ready, 1)
                reached(act, probs_ready, h, p, 2, 2)
                nc.scalar.activation(score[:, p], score[:, p], ACT.Exp).then_inc(e_ready, 1)

            run_stages(act, [(3, keep_sk), (5, high_a), (2, keep_q), (1, high_xn), (2, keep_k), (4, exponentials),
                             (4, keep_pT), (2, keep_v)])

        @block.tensor
        def _(pe):
            def turn_a(h, p):
                reached(pe, a_ready, h, p)
                freed(pe, sk_kept, h, p, back=-2)
                freed(pe, al_ready, h, p, back=1)
                for c in range(DC):
                    mm = nc.tensor.transpose(psT[:, c * P:(c + 1) * P], a[:, p, c * P:(c + 1) * P], ident[:])
                mm.then_inc(aT_psum, 1)

            def turn_xn(h, p):
                reached(pe, xn_ready, h, p)
                freed(pe, al_ready, h, p, back=4)
                freed(pe, sk_kept, h, p, back=2)
                freed(pe, xl_ready, h, p, back=1)
                for c in range(DC):
                    mm = nc.tensor.transpose(psT[:, c * P:(c + 1) * P], xn[:, p, c * P:(c + 1) * P], ident[:])
                mm.then_inc(xnT_psum, 1)

            def turn_sk(h, p):
                reached(pe, sk_ready, h, p)
                freed(pe, xl_ready, h, p, back=-1)
                freed(pe, al_ready, h, p, back=3)
                freed(pe, sk_kept, h, p, back=1)
                for c in range(DC):
                    mm = nc.tensor.transpose(psT[:, c * P:(c + 1) * P], skq[:, p, c, 1:3], ident[:])
                mm.then_inc(skT_psum, 1)

            def read_memory(s):
                def stage(h, p):
                    reached(pe, sq_ready, h, p, 2, 2)
                    if s == 0:
                        freed(pe, m_ready, h, p, 2, 2)
                        freed(pe, masked, h, p, 2, 2, back=1)
                    else:
                        reached(pe, m_ready, h, p, 1, 2)
                    for c in range(DC):
                        mm = nc.tensor.matmul(psM[:, c // 2, c % 2], skq[:, p, c, 2 * s:2 * s + 2], memory[:, p, c],
                                              start=True, stop=True)
                    mm.then_inc(readout, 1)
                return stage

            def sum_update(s):
                def stage(h, p):
                    r = rows[s]
                    reached(pe, sk_kept, h, p)
                    reached(pe, vd_ready, h, p, s + 1, 2)
                    reached(pe, fm_ready, h, p, 2 * s + 2, 4)
                    for c in range(DC):
                        mm = nc.tensor.matmul(psM[:, c // 2, c % 2], sk[r, p, c * P:(c + 1) * P], vd[r, p, c],
                                              start=True, stop=True)
                    mm.then_inc(u_psum, 1)
                return stage

            def out_projection(h, p):
                reached(pe, al_ready, h, p)
                freed(pe, k_read, h, p, 4, 4, back=-3)
                passes = [(ah, wh), (al, wh), (ah, wl)]
                for n, (s, w) in enumerate(passes):
                    for c in range(DC):
                        mm = nc.tensor.matmul(psB, s[:, p, c, :], w[:, WO, c, :], start=n + c == 0,
                                              stop=n == 2 and c == DC - 1)
                mm.then_inc(y_psum, 1)

            def turned_projection(bank, weight, h, p):
                for j in range(DC):
                    for n, (w, s) in enumerate([(wh, xh), (wh, xl), (wl, xh)]):
                        for c in range(DC):
                            mm = nc.tensor.matmul(bank[:, j * P:(j + 1) * P], w[:, weight, c, j * P:(j + 1) * P],
                                                  s[:, p, c, :], start=n + c == 0, stop=n == 2 and c == DC - 1)
                return mm

            def queries(h, p):
                reached(pe, xl_ready, h, p)
                freed(pe, v_ready, h, p, back=1)
                turned_projection(psA, WQ, h, p).then_inc(q_psum, 1)

            def keys(h, p):
                freed(pe, x_added, h, p, back=4)
                freed(pe, k_read, h, p, 4, 4, back=1)
                turned_projection(psB, WK, h, p).then_inc(k_psum, 1)

            def values(h, p):
                reached(pe, q_read, h, p)
                for n, (s, w) in enumerate([(xh, wh), (xl, wh), (xh, wl)]):
                    for c in range(DC):
                        mm = nc.tensor.matmul(psA, s[:, p, c, :], w[:, WV, c, :], start=n + c == 0,
                                              stop=n == 2 and c == DC - 1)
                mm.then_inc(v_psum, 1)

            def local_scores(h, p):
                reached(pe, k_read, h, p, 4, 4)
                freed(pe, pT_ready, h, p, 4, 4, back=1)
                for s in range(2):
                    for c in range(DC):
                        mm = nc.tensor.matmul(psS[rows[s], c * HC * SEG:(c + 1) * HC * SEG], qT[:, p, c, rows[s]],
                                              kdiag[:, p, c, s], start=True, stop=True)
                mm.then_inc(scores, 1)

            def attend(h, p):
                reached(pe, probs_ready, h, p, 2, 2)
                freed(pe, mixed_ready, h, p, back=1)

                def turn(g):
                    if g >= 2:
                        reached(pe, pT_ready, h, p, g - 1, 4)
                    bank = psS[:, g % 2 * 512:(g % 2 + 1) * 512]
                    for n in range(HC):
                        mm = nc.tensor.transpose(bank[:, n * P:(n + 1) * P], pdiag[:, p, g * HC + n, :], ident[:])
                    mm.then_inc(pT_psum, 1)

                def mix(g):
                    reached(pe, pT_ready, h, p, g + 1, 4)
                    for n in range(HC):
                        c = (g * HC + n) * DK
                        mm = nc.tensor.matmul(psP[:, c:c + DK], pT[:, g % 2, n, :], v[:, p, c:c + DK], start=True, stop=True)
                    if g == 3:
                        mm.then_inc(pv, 1)

                turn(0)
                turn(1)
                for g in range(4):
                    mix(g)
                    if g < 2:
                        turn(g + 2)

            run_stages(pe, [(3, turn_sk), (3, read_memory(0)), (5, turn_a), (2, queries), (3, sum_update(0)),
                            (1, turn_xn), (2, keys), (3, read_memory(1)), (2, values), (5, out_projection),
                            (3, sum_update(1)), (4, attend), (3, local_scores)])



NEAR, FAR = range(2)


def l1_cross_attention(nc, d, x, ident, ones, minus_half, eps, consts):
    with ExitStack() as ctx:
        ph = Phase(nc, ctx, "x1")
        w0 = ph.sb("w0", [P, DC, D])
        w3 = ph.sb("w3", [P, DC, D])
        w03_in = ph.sem("w03_in")
        ctx_rows = ph.sb("ctx_rows", [K, B, D])
        gh = ph.sb("gh", [P, B, DC, K], BF16)
        gl = ph.sb("gl", [P, B, DC, K], BF16)
        crow = ph.sb("crow", [P, B, K])
        cw1 = ph.sb("cw1", [K, B, D])
        w2h = ph.sb("w2h", [P, DC, D], BF16)
        w2l = ph.sb("w2l", [P, DC, D], BF16)
        bias = ph.sb("bias", [P, D])
        ps = ph.banks()
        w_in = ph.sem("w_in")
        c_in = ph.sem("c_in")

        with ExitStack() as ctx2:
            ph2 = Phase(nc, ctx2, "x1s")
            ctxT = ph2.sb("ctxT", [P, DC, B * K])
            wsim = ph2.sb("wsim", [P, 3, DC])
            bsim = ph2.sb("bsim", [P, 1])
            w1 = ph2.sb("w1", [P, DC, D])
            w2 = ph2.sb("w2", [P, DC, D])
            w2sim = ph2.sb("w2sim", [P, DC, P])
            g = ph2.sb("g", [P, B, DC, K])
            g_ready, gh_ready, wide_ready, c_psum, cw_psum, w2h_ready = (
                ph2.sem(n) for n in "g_ready gh_ready wide_ready c_psum cw_psum w2h_ready".split())
            with nc.Block() as block:
                @block.sync
                def _(sp):
                    sp.dma_start(ctxT[:], d["ctxT"]).then_inc(c_in, 16)
                    sp.dma_start(wsim[:], d["w_sim"]).then_inc(c_in, 16)
                    sp.dma_start(bsim[:], d["b_sim"]).then_inc(c_in, 16)
                    sp.dma_start(ctx_rows[:], d["ctx_rows"]).then_inc(c_in, 16)
                    sp.dma_start(w1[:], d["w_x1_1"]).then_inc(w_in, 16)
                    sp.dma_start(w2[:], d["w_x1_2"]).then_inc(w_in, 16)
                    sp.dma_start(w0[:], d["w_x1_0"]).then_inc(w03_in, 16)
                    sp.dma_start(w3[:], d["w_x1_3"]).then_inc(w03_in, 16)
                    sp.dma_start(bias[:], d["b_x1"]).then_inc(w_in, 16)

                @block.vector
                def _(dve):
                    dve.wait_ge(c_in, 64)
                    for c in range(DC):
                        nc.vector.tensor_scalar(w2sim[:, c], ones[:], wsim[:, 1, c:c + 1], None, ALU.mult).then_inc(wide_ready, 1)
                        nc.vector.tensor_scalar(g[:, :, c], ctxT[:, c].rearrange("p (b k) -> p b k", b=B), wsim[:, 2, c:c + 1],
                                                wsim[:, 0, c:c + 1], ALU.mult, ALU.add).then_inc(g_ready, 1)
                    dve.wait_ge(gh_ready, 1)
                    nc.vector.tensor_tensor(gl[:], g[:], gh[:], ALU.subtract)
                    dve.wait_ge(c_psum, 1)
                    nc.vector.tensor_scalar(crow[:].rearrange("p b k -> p (b k)"), ps[:, 0, 0:B * K], bsim[:], None, ALU.add)
                    dve.wait_ge(w2h_ready, 1)
                    nc.vector.tensor_tensor(w2l[:], w2[:], w2h[:], ALU.subtract)

                @block.scalar
                def _(act):
                    act.wait_ge(g_ready, DC)
                    nc.scalar.copy(gh[:], g[:]).then_inc(gh_ready, 1)
                    act.wait_ge(w_in, 48)
                    nc.scalar.copy(w2h[:], w2[:]).then_inc(w2h_ready, 1)
                    for b in range(B):
                        act.wait_ge(cw_psum, b + 1)
                        nc.scalar.copy(cw1[:, b], ps[0:K, 1 + b])

                @block.tensor
                def _(pe):
                    pe.wait_ge(wide_ready, DC)
                    for c in range(DC):
                        mm = nc.tensor.matmul(ps[:, 0, 0:B * K], w2sim[:, c], ctxT[:, c], start=c == 0, stop=c == DC - 1)
                    mm.then_inc(c_psum, 1)
                    pe.wait_ge(w_in, 48)
                    for b in range(B):
                        for c in range(DC):
                            mm = nc.tensor.matmul(ps[0:K, 1 + b], ctxT[:, c, b * K:(b + 1) * K], w1[:, c],
                                                  start=c == 0, stop=c == DC - 1)
                        mm.then_inc(cw_psum, 1)

        xn = ph.sb("xn", [P, TB // 2, 2, D])
        xh = ph.sb("xh", [P, TB // 2, 2, DC, P], BF16)
        xl = ph.sb("xl", [P, TB // 2, 2, DC, P], BF16)
        wch = ph.sb("wch", [P, DC, D], BF16)
        wcl = ph.sb("wcl", [P, DC, D], BF16)
        expo = ph.sb("expo", [P, B, TB // 2, 2, K])
        ntop = ph.sb("ntop", [P, B, TB // 2, 2])
        total = ph.sb("total", [P, B, TB // 2, 2])
        inv = ph.sb("inv", [P, B, TB // 2, 2])
        flat = "p c t -> p (c t)"
        psT, psS, psP, psH, psC = ps[:, 0], ps[:, 1, 0:K], ps[0:K, 2, 0:P], ps[:, 3], ps[:, 6, 0:DC]
        psY = lambda p: ps[:, 4 + p]

        def run(near, far):
            with ExitStack() as ctx3:
                q = Phase(nc, ctx3, f"x1{near}{far}")
                names = ("stats_done mv_ready var_ready rstd_ready xc_ready xnT_psum xh_ready xl_ready sim_psum sim_ready "
                         "top_ready exp_ready inv_ready probs_ready pT_psum pT_ready xf_ready hq_psum z_ready zh_ready "
                         "zl_ready b_added y_psum x_added xn_kept").split()
                (stats_done, mv_ready, var_ready, rstd_ready, xc_ready, xnT_psum, xh_ready, xl_ready, sim_psum, sim_ready,
                 top_ready, exp_ready, inv_ready, probs_ready, pT_psum, pT_ready, xf_ready, hq_psum, z_ready, zh_ready,
                 zl_ready, b_added, y_psum, x_added, xn_kept) = (q.sem(n) for n in names)
                stats = q.sb("stats", [P, 2, 6])
                mv = q.sb("mv", [P, 2, 2])
                rs = q.sb("rs", [P, 2, 2])
                xc = q.sb("xc", [P, 2, D])
                sim = q.sb("sim", [P, 2, K])
                probs = q.sb("probs", [P, 2, K])
                pT = q.sb("pT", [K, 2, P])
                xf = q.sb("xf", [P, 2, D])
                z = q.sb("z", [P, 2, D])
                zh = q.sb("zh", [P, 2, DC, P], BF16)
                zl = q.sb("zl", [P, 2, DC, P], BF16)
                block = ctx3.enter_context(nc.Block())
                tiles = x[:].rearrange("t b (h p) n -> t b h p n", p=2)
                a, b = near, far

                def stages(eng, order):
                    behind = 3 if near is not None and far is not None else 0
                    run_stages(eng, [(lag + (behind if side == NEAR else 0), stage) for side, lag, stage in order
                                     if (near if side == NEAR else far) is not None], TB)

                def before(eng, sem, h, p, k=1, per=1, back=2):
                    freed(eng, sem, h, p, k, per, back, TB)

                @block.gpsimd
                def _(pool):
                    def layernorm_scale(h, p):
                        reached(pool, mv_ready, h, p)
                        before(pool, xc_ready, h, p)
                        nc.gpsimd.tensor_tensor(rs[:, p, 0:1], mv[:, p, 1:2], eps[:], ALU.add).then_inc(var_ready, 1)
                        reached(pool, var_ready, h, p)
                        nc.gpsimd.tensor_tensor(rs[:, p, 1:2], rs[:, p, 0:1], minus_half[:, 0:1],
                                                ALU.pow).then_inc(rstd_ready, 1)

                    def whole_xn(h, p):
                        before(pool, z_ready, h, p)
                        nc.gpsimd.tensor_tensor(xf[:, p], xh[:, h, p].rearrange(flat), xl[:, h, p].rearrange(flat),
                                                ALU.add).then_inc(xf_ready, 1)

                    def add_bias(h, p):
                        nc.gpsimd.tensor_tensor(tiles[:, b, h, p], tiles[:, b, h, p], bias[:], ALU.add).then_inc(b_added, 1)

                    stages(pool, [(NEAR, 0, layernorm_scale), (FAR, 2, whole_xn), (FAR, 2, add_bias)])

                @block.vector
                def _(dve):
                    def statistics(h, p):
                        nc.vector.bn_stats(stats[:, p, :], tiles[:, a, h, p]).then_inc(stats_done, 1)
                        reached(dve, stats_done, h, p)
                        before(dve, var_ready, h, p)
                        carry_wait(nc, dve, consts)
                        nc.vector.bn_aggr(mv[:, p, :], stats[:, p, :]).then_inc(mv_ready, 1)

                    def normalise(h, p):
                        reached(dve, rstd_ready, h, p)
                        before(dve, xnT_psum, h, p)
                        before(dve, xn_kept, h, p)
                        nc.vector.tensor_scalar(xc[:, p], tiles[:, a, h, p], mv[:, p, 0:1], rs[:, p, 1:2],
                                                ALU.subtract, ALU.mult).then_inc(xc_ready, 1)

                    def low_xn(h, p):
                        reached(dve, xh_ready, h, p)
                        if far is not None:
                            reached(dve, y_psum, h, p)
                        nc.vector.tensor_tensor(xl[:, h, p].rearrange(flat), psT, xh[:, h, p].rearrange(flat),
                                                ALU.subtract).then_inc(xl_ready, 1)

                    def tops(h, p):
                        reached(dve, sim_psum, h, p)
                        before(dve, exp_ready, h, p)
                        nc.vector.tensor_tensor(sim[:, p], psS, crow[:, a], ALU.add).then_inc(sim_ready, 1)
                        reached(dve, sim_ready, h, p)
                        nc.vector.tensor_reduce(ntop[:, a, h, p:p + 1], sim[:, p], AX_X, ALU.max,
                                                negate=True).then_inc(top_ready, 1)

                    def divide(h, p):
                        nc.vector.reciprocal(inv[:, b, h, p:p + 1], total[:, b, h, p:p + 1]).then_inc(inv_ready, 1)
                        reached(dve, inv_ready, h, p)
                        before(dve, pT_psum, h, p)
                        nc.vector.tensor_scalar(probs[:, p], expo[:, b, h, p], inv[:, b, h, p:p + 1], None,
                                                ALU.mult).then_inc(probs_ready, 1)

                    def product(h, p):
                        reached(dve, hq_psum, h, p)
                        reached(dve, xf_ready, h, p)
                        before(dve, zl_ready, h, p)
                        nc.vector.tensor_tensor(z[:, p], psH, xf[:, p], ALU.mult).then_inc(z_ready, 1)

                    def low_z(h, p):
                        reached(dve, zh_ready, h, p)
                        before(dve, y_psum, h, p)
                        nc.vector.tensor_tensor(zl[:, p].rearrange(flat), z[:, p], zh[:, p].rearrange(flat),
                                                ALU.subtract).then_inc(zl_ready, 1)

                    def residual(h, p):
                        reached(dve, y_psum, h, p)
                        reached(dve, b_added, h, p)
                        nc.vector.tensor_tensor(tiles[:, b, h, p], psY(p), tiles[:, b, h, p], ALU.add).then_inc(x_added, 1)

                    stages(dve, [(NEAR, 0, statistics), (NEAR, 1, low_xn), (FAR, 0, divide), (NEAR, 0, normalise),
                                 (FAR, 3, residual), (FAR, 2, product), (NEAR, 2, tops), (FAR, 2, low_z)])

                @block.scalar
                def _(act):
                    def high_xn(h, p):
                        reached(act, xnT_psum, h, p)
                        if far is not None:
                            reached(act, y_psum, h, p)
                        nc.scalar.copy(xh[:, h, p].rearrange(flat), psT).then_inc(xh_ready, 1)

                    def keep_xn(h, p):
                        reached(act, xc_ready, h, p)
                        nc.scalar.copy(xn[:, h, p], xc[:, p]).then_inc(xn_kept, 1)

                    def exponentials(h, p):
                        reached(act, top_ready, h, p)
                        nc.scalar.activation(expo[:, a, h, p], sim[:, p], ACT.Exp, bias=ntop[:, a, h, p:p + 1],
                                             accum_out=total[:, a, h, p:p + 1]).then_inc(exp_ready, 1)

                    def keep_pT(h, p):
                        reached(act, pT_psum, h, p)
                        before(act, y_psum, h, p)
                        nc.scalar.copy(pT[:, p], psP).then_inc(pT_ready, 1)

                    def high_z(h, p):
                        reached(act, z_ready, h, p)
                        before(act, y_psum, h, p)
                        nc.scalar.copy(zh[:, p].rearrange(flat), z[:, p]).then_inc(zh_ready, 1)

                    stages(act, [(NEAR, 1, high_xn), (NEAR, 0, keep_xn), (FAR, 1, keep_pT), (FAR, 2, high_z),
                                 (NEAR, 2, exponentials)])

                @block.tensor
                def _(pe):
                    def turn_xn(h, p):
                        reached(pe, xc_ready, h, p)
                        before(pe, xl_ready, h, p, back=1)
                        for c in range(DC):
                            mm = nc.tensor.transpose(psT[:, c * P:(c + 1) * P], xc[:, p, c * P:(c + 1) * P], ident[:])
                        mm.then_inc(xnT_psum, 1)

                    def similarity(h, p):
                        reached(pe, xl_ready, h, p)
                        before(pe, sim_ready, h, p, back=1)
                        for n, (s, w) in enumerate([(xh, gh), (xl, gh), (xh, gl)]):
                            for c in range(DC):
                                mm = nc.tensor.matmul(psS, s[:, h, p, c], w[:, a, c], start=n + c == 0,
                                                      stop=n == 2 and c == DC - 1)
                        mm.then_inc(sim_psum, 1)

                    def turn_probs(h, p):
                        reached(pe, probs_ready, h, p)
                        before(pe, pT_ready, h, p, back=1)
                        nc.tensor.transpose(psP, probs[:, p], ident[:]).then_inc(pT_psum, 1)

                    def context_means(h, p):
                        reached(pe, pT_ready, h, p)
                        before(pe, z_ready, h, p, back=1)
                        for c in range(DC):
                            mm = nc.tensor.matmul(psH[:, c * P:(c + 1) * P], ctx_rows[:, b, c * P:(c + 1) * P], pT[:, p],
                                                  start=True, stop=True)
                        mm.then_inc(hq_psum, 1)

                    def project(h, p):
                        before(pe, x_added, h, p)
                        for n, (s, w) in enumerate([(xh, wch), (xl, wch), (xh, wcl)]):
                            for c in range(DC):
                                nc.tensor.matmul(psY(p), s[:, h, p, c], w[:, c], start=n + c == 0, stop=False)
                        nc.tensor.matmul(psY(p), pT[:, p], cw1[:, b], start=False, stop=False)
                        reached(pe, zl_ready, h, p)
                        for n, (s, w) in enumerate([(zh, w2h), (zl, w2h), (zh, w2l)]):
                            for c in range(DC):
                                mm = nc.tensor.matmul(psY(p), s[:, p, c], w[:, c], start=False,
                                                      stop=n == 2 and c == DC - 1)
                        mm.then_inc(y_psum, 1)

                    stages(pe, [(NEAR, 1, turn_xn), (FAR, 3, project), (FAR, 2, context_means), (FAR, 1, turn_probs),
                                (NEAR, 2, similarity)])

        def context_mean(b):
            with ExitStack() as ctx3:
                q = Phase(nc, ctx3, f"x1hc{b}")
                col = q.sb("col", [P, 8])
                weights = q.sb("weights", [P, TB // 2, 2])
                hc = q.sb("hc", [P, DC])
                wc = q.sb("wc", [P, DC, D])
                (top_ready, tops_ready, ntop_ready, w_ready, sum_ready, inv_ready, hc_psum, hc_ready, wc_ready,
                 wch_ready) = (q.sem(n) for n in ("top_ready tops_ready ntop_ready w_ready sum_ready inv_ready hc_psum "
                                                  "hc_ready wc_ready wch_ready").split())
                with nc.Block() as block:
                    @block.gpsimd
                    def _(pool):
                        pool.wait_ge(top_ready, 1)
                        nc.gpsimd.partition_all_reduce(col[:, 1:2], col[:, 0:1], P, bass.bass_isa.ReduceOp.max).then_inc(tops_ready, 1)
                        pool.wait_ge(w_ready, 1)
                        nc.gpsimd.partition_all_reduce(col[:, 4:5], col[:, 3:4], P, bass.bass_isa.ReduceOp.add).then_inc(sum_ready, 1)

                    @block.vector
                    def _(dve):
                        nc.vector.tensor_reduce(col[:, 0:1], ntop[:, b].rearrange("t h p -> t (h p)"), AX_X, ALU.min,
                                                negate=True).then_inc(top_ready, 1)
                        dve.wait_ge(tops_ready, 1)
                        nc.vector.tensor_scalar(col[:, 2:3], col[:, 1:2], -1.0, None, ALU.mult).then_inc(ntop_ready, 1)
                        dve.wait_ge(sum_ready, 1)
                        nc.vector.reciprocal(col[:, 5:6], col[:, 4:5]).then_inc(inv_ready, 1)
                        dve.wait_ge(inv_ready, 1)
                        dve.wait_ge(hc_psum, 1)
                        nc.vector.tensor_scalar(hc[:], psC, col[:, 5:6], None, ALU.mult).then_inc(hc_ready, 1)
                        dve.wait_ge(hc_ready, 1)
                        dve.wait_ge(w03_in, 32)
                        for c in range(DC):
                            nc.vector.scalar_tensor_tensor(out=wc[:, c], in0=w3[:, c], scalar=hc[:, c:c + 1], in1=w0[:, c],
                                                           op0=ALU.mult, op1=ALU.add).then_inc(wc_ready, 1)
                        for c in range(DC):
                            dve.wait_ge(wch_ready, c + 1)
                            nc.vector.tensor_tensor(wcl[:, c], wc[:, c], wch[:, c], ALU.subtract)

                    @block.scalar
                    def _(act):
                        act.wait_ge(ntop_ready, 1)
                        nc.scalar.activation(weights[:], ntop[:, b], ACT.Exp, scale=-1.0, bias=col[:, 2:3],
                                             accum_out=col[:, 3:4]).then_inc(w_ready, 1)
                        for c in range(DC):
                            act.wait_ge(wc_ready, c + 1)
                            nc.scalar.copy(wch[:, c], wc[:, c]).then_inc(wch_ready, 1)

                    @block.tensor
                    def _(pe):
                        pe.wait_ge(w_ready, 1)
                        for c in range(DC):
                            for t in range(TB):
                                mm = nc.tensor.matmul(psC[:, c:c + 1], xn[:, t // 2, t % 2, c * P:(c + 1) * P],
                                                      weights[:, t // 2, t % 2:t % 2 + 1], start=t == 0, stop=t == TB - 1)
                        mm.then_inc(hc_psum, 1)

        run(0, None)
        context_mean(0)
        run(1, 0)
        context_mean(1)
        run(None, 1)



E = 8
UNITS = E * FC
TE = TB // E
RING = 4
LAST_AT = {1: [0], 2: [1], 3: [2, 3]}


def run_experts(eng, unit):
    def expert(e, last):
        for f in range(RING):
            unit(e, f, f)
        with eng.Fori(1, FC // RING - last) as k:
            for r in range(RING):
                unit(e, k * RING + r, r)
        for f in range(FC - RING * last, FC):
            unit(e, f, f % RING)

    expert(0, False)
    expert(1, False)
    with eng.Fori(2, E - 1) as e:
        expert(e, False)
    expert(E - 1, True)


def at_least(eng, sem, value):
    if not (isinstance(value, int) and value <= 0):
        eng.wait_ge(sem, value)


def l1_ffn(nc, d, x, out, ident, minus_half, eps, consts):
    flat = "p c t -> p (c t)"
    with ExitStack() as ctx:
        ph = Phase(nc, ctx, "f1")
        xah = ph.sb("xah", [P, DC, TB, B, P], BF16)
        xal = ph.sb("xal", [P, DC, TB, B, P], BF16)
        wnh = ph.sb("wnh", [P, 1, DC, D], BF16)
        wnl = ph.sb("wnl", [P, 1, DC, D], BF16)

        with ExitStack() as ctx2:
            q = Phase(nc, ctx2, "f1a")
            wh, wl = split_weights(nc, q, d, ["w_f1a", "w_f1n"], [DC, D])
            ln_scale = q.sb("ln_scale", [P, D])
            ln_bias = q.sb("ln_bias", [P, D])
            attn_bias = q.sb("attn_bias", [P, D])
            stats = q.sb("stats", [P, 2, 6])
            mv = q.sb("mv", [P, 2, 2])
            rs = q.sb("rs", [P, 2, 6])
            xL = q.sb("xL", [P, 2, D])
            xLb = q.sb("xLb", [P, 2, D])
            xs = q.sb("xs", [P, 2, D])
            xh = q.sb("xh", [P, 2, DC, P], BF16)
            xl = q.sb("xl", [P, 2, DC, P], BF16)
            xa = q.sb("xa", [P, 2, D])
            ps = q.banks()
            psT, psA = (lambda p: ps[:, p]), (lambda p: ps[:, 2 + p])
            psY = lambda p: ps[:, 4 + p]
            v_in = q.sem("v_in")
            names = ("stats_done mv_ready rs_own xL_ready xs_scaled xs_ready xLb_ready xT_psum xh_ready xl_ready y_psum "
                     "xa_ready aT_psum ah_ready al_ready").split()
            (stats_done, mv_ready, rs_own, xL_ready, xs_scaled, xs_ready, xLb_ready, xT_psum, xh_ready, xl_ready, y_psum,
             xa_ready, aT_psum, ah_ready, al_ready) = (q.sem(n) for n in names)
            block = ctx2.enter_context(nc.Block())

            @block.sync
            def _(sp):
                sp.dma_start(ln_scale[:], d["ln_scale"]).then_inc(v_in, 16)
                sp.dma_start(ln_bias[:], d["ln_bias"]).then_inc(v_in, 16)
                sp.dma_start(attn_bias[:], d["b_f1a"]).then_inc(v_in, 16)

            @block.gpsimd
            def _(pool):
                tt = nc.gpsimd.tensor_tensor
                nc.gpsimd.tensor_copy(wnh[:, 0], wh[:, 1])
                nc.gpsimd.tensor_copy(wnl[:, 0], wl[:, 1])
                pool.wait_ge(v_in, 48)

                def roots(h, p):
                    v = mv[:, p, 1:2]
                    r = [rs[:, p, n:n + 1] for n in range(6)]
                    reached(pool, mv_ready, h, p)
                    freed(pool, xs_scaled, h, p)
                    steps = [(r[0], v, eps[:], ALU.add), (r[1], r[0], minus_half[:, 0:1], ALU.pow), (r[2], v, r[1], ALU.mult),
                             (r[3], r[2], r[1], ALU.mult), (r[4], r[3], eps[:], ALU.add),
                             (r[5], r[4], minus_half[:, 0:1], ALU.pow)]
                    for n, (to, a, b, op) in enumerate(steps):
                        if n:
                            reached(pool, rs_own, h, p, n, 6)
                        tt(to, a, b, op).then_inc(rs_own, 1)

                def biases(h, p):
                    reached(pool, xs_scaled, h, p)
                    tt(xs[:, p], xs[:, p], ln_bias[:], ALU.add).then_inc(xs_ready, 1)
                    freed(pool, xa_ready, h, p)
                    tt(xLb[:, p], xL[:, p], attn_bias[:], ALU.add).then_inc(xLb_ready, 1)

                run_stages(pool, [(0, roots), (0, biases)])

            @block.vector
            def _(dve):
                dve.wait_ge(v_in, 48)

                def statistics(h, p):
                    nc.vector.bn_stats(stats[:, p, :], x[:, p, h, :]).then_inc(stats_done, 1)
                    reached(dve, stats_done, h, p)
                    freed(dve, rs_own, h, p, 3, 6)
                    carry_wait(nc, dve, consts)
                    nc.vector.bn_aggr(mv[:, p, :], stats[:, p, :]).then_inc(mv_ready, 1)

                def normalise(h, p):
                    reached(dve, rs_own, h, p, 2, 6)
                    freed(dve, xLb_ready, h, p)
                    nc.vector.tensor_scalar(xL[:, p, :], x[:, p, h, :], mv[:, p, 0:1], rs[:, p, 1:2],
                                            ALU.subtract, ALU.mult).then_inc(xL_ready, 1)
                    reached(dve, xL_ready, h, p)
                    reached(dve, rs_own, h, p, 6, 6)
                    freed(dve, xT_psum, h, p)
                    nc.vector.scalar_tensor_tensor(out=xs[:, p], in0=xL[:, p], scalar=rs[:, p, 5:6], in1=ln_scale[:],
                                                   op0=ALU.mult, op1=ALU.mult).then_inc(xs_scaled, 1)

                def low_x(h, p):
                    reached(dve, xh_ready, h, p)
                    freed(dve, y_psum, h, p)
                    nc.vector.tensor_tensor(xl[:, p].rearrange(flat), psT(p), xh[:, p].rearrange(flat),
                                            ALU.subtract).then_inc(xl_ready, 1)

                def add_xL(h, p):
                    reached(dve, y_psum, h, p)
                    reached(dve, xLb_ready, h, p)
                    freed(dve, aT_psum, h, p)
                    nc.vector.tensor_tensor(xa[:, p], psY(p), xLb[:, p], ALU.add).then_inc(xa_ready, 1)

                def low_a(h, p):
                    reached(dve, ah_ready, h, p)
                    nc.vector.tensor_tensor(xal[:, :, h, p], psA(p).rearrange("p (c t) -> p c t", c=DC), xah[:, :, h, p],
                                            ALU.subtract).then_inc(al_ready, 1)

                run_stages(dve, [(0, statistics), (1, low_x), (2, add_xL), (3, low_a), (0, normalise)])

            @block.scalar
            def _(act):
                def high_x(h, p):
                    reached(act, xT_psum, h, p)
                    freed(act, y_psum, h, p)
                    nc.scalar.copy(xh[:, p].rearrange(flat), psT(p)).then_inc(xh_ready, 1)

                def high_a(h, p):
                    reached(act, aT_psum, h, p)
                    nc.scalar.copy(xah[:, :, h, p], psA(p).rearrange("p (c t) -> p c t", c=DC)).then_inc(ah_ready, 1)

                run_stages(act, [(1, high_x), (3, high_a)])

            @block.tensor
            def _(pe):
                def turn(bank, tile):
                    for c in range(DC):
                        mm = nc.tensor.transpose(bank[:, c * P:(c + 1) * P], tile[:, c * P:(c + 1) * P], ident[:])
                    return mm

                def turn_x(h, p):
                    reached(pe, xs_ready, h, p)
                    freed(pe, xl_ready, h, p)
                    turn(psT(p), xs[:, p]).then_inc(xT_psum, 1)

                def turn_a(h, p):
                    reached(pe, xa_ready, h, p)
                    freed(pe, al_ready, h, p)
                    turn(psA(p), xa[:, p]).then_inc(aT_psum, 1)

                def project(h, p):
                    reached(pe, xl_ready, h, p)
                    freed(pe, xa_ready, h, p)
                    for n, (s, w) in enumerate([(xh, wh), (xl, wh), (xh, wl)]):
                        for c in range(DC):
                            mm = nc.tensor.matmul(psY(p), s[:, p, c], w[:, 0, c], start=n + c == 0,
                                                  stop=n == 2 and c == DC - 1)
                    mm.then_inc(y_psum, 1)

                run_stages(pe, [(1, turn_x), (3, turn_a), (2, project)])

        b1 = ph.sb("b1", [P, E, FC])
        b2 = ph.sb("b2", [P, E, DC])
        last_bias = ph.sb("last_bias", [P, D])
        raw = ph.sb("raw", [P, RING, 2 * D])
        wh = ph.sb("wh", [P, RING, 2, DC, P], BF16)
        wl = ph.sb("wl", [P, RING, 2, DC, P], BF16)
        hid = ph.sb("hid", [P, 2, D])
        hh = ph.sb("hh", [P, 2, D], BF16)
        hl = ph.sb("hl", [P, 2, D], BF16)
        eh = ph.sb("eh", [P, DC, D], BF16)
        el = ph.sb("el", [P, DC, D], BF16)
        last = ph.sb("last", [P, 2, D])
        ps = ph.banks()
        psU, psE, psN = (lambda u: ps[:, u % 2]), (lambda j: ps[:, 2 + j]), (lambda n: ps[:, 6 + n % 2])
        raw_in = [ph.sem(f"raw_in{r}") for r in range(RING)]
        (v_in, wh_ready, wl_ready, h_psum, gelu_done, hh_ready, hl_ready, used, eh_ready, el_ready, n_psum,
         biased, last_ready, x_added, stored) = (
            ph.sem(n) for n in ("v_in wh_ready wl_ready h_psum gelu_done hh_ready hl_ready used eh_ready el_ready "
                                "n_psum biased last_ready x_added stored").split())
        block = ctx.enter_context(nc.Block())

        def before_last(f):
            return not isinstance(f, int) or f + 2 < FC

        @block.sync
        def _(sp):
            sp.dma_start(b1[:], d["b_f1_1"]).then_inc(v_in, 16)
            sp.dma_start(b2[:], d["b_f1_2"]).then_inc(v_in, 16)
            sp.dma_start(last_bias[:], d["b_f1n"]).then_inc(v_in, 16)
            for r in range(RING):
                sp.dma_start(raw[:, r], d["w_f1"][r]).then_inc(raw_in[r], 16)
            with sp.Fori(1, UNITS // RING) as k:
                for r in range(RING):
                    sp.wait_ge(wl_ready, k * RING + (r + 1 - RING))
                    sp.dma_start(raw[:, r], d["w_f1"][k * RING + r]).then_inc(raw_in[r], 16)

            def store(e):
                for n in range(4):
                    sp.wait_ge(x_added, e * 4 + (n + 1))
                    h = e * TE + n // 2
                    sp.dma_start(out[n % 2, h], x[:, n % 2, h, :]).then_inc(stored, 16)

            with sp.Fori(0, E) as e:
                store(e)
            sp.wait_ge(stored, N_TILES * 16)

        @block.scalar
        def _(act):
            act.wait_ge(v_in, 48)

            def high_weights(g, r):
                act.wait_ge(raw_in[r], (g - r) * (16 // RING) + 16)
                at_least(act, used, g - RING + 1)
                nc.scalar.copy(wh[:, r].rearrange("p w c t -> p (w c t)"), raw[:, r]).then_inc(wh_ready, 1)

            def result(e):
                act.wait_ge(used, (e + 1) * FC)
                at_least(act, n_psum, e * 4)
                for j in range(DC):
                    nc.scalar.activation(eh[:, j], psE(j), ACT.Identity, bias=b2[:, e, j:j + 1]).then_inc(eh_ready, 1)

            def last_gelu(e, n):
                act.wait_ge(biased, e * 4 + (n + 1))
                nc.scalar.activation(last[:, n % 2], last[:, n % 2], ACT.Gelu).then_inc(last_ready, 1)

            def unit(e, f, r):
                g = e * FC + f
                final = isinstance(e, int) and e == E - 1
                if not final or before_last(f):
                    high_weights(g + 2, (r + 2) % RING)
                act.wait_ge(h_psum, g + 1)
                at_least(act, hl_ready, g - 1)
                nc.scalar.activation(hid[:, r % 2], psU(r), ACT.Gelu, bias=b1[:, e, f:f + 1] if isinstance(f, int) else
                                     b1[:, e, bass.ds(f, 1)]).then_inc(gelu_done, 1)
                act.wait_ge(gelu_done, g + 1)
                at_least(act, used, g - 1)
                nc.scalar.copy(hh[:, r % 2], hid[:, r % 2]).then_inc(hh_ready, 1)
                if isinstance(f, int) and not (isinstance(e, int) and e == 0):
                    if f == 0:
                        result(e - 1)
                    if f in LAST_AT:
                        for n in LAST_AT[f]:
                            last_gelu(e - 1, n)

            high_weights(0, 0)
            high_weights(1, 1)
            run_experts(act, unit)
            result(E - 1)
            for n in range(4):
                last_gelu(E - 1, n)

        @block.vector
        def _(dve):
            dve.wait_ge(v_in, 48)

            def low_weights(g, r):
                dve.wait_ge(wh_ready, g + 1)
                nc.vector.tensor_tensor(wl[:, r].rearrange("p w c t -> p (w c t)"), raw[:, r],
                                        wh[:, r].rearrange("p w c t -> p (w c t)"), ALU.subtract).then_inc(wl_ready, 1)

            def result(e):
                for j in range(DC):
                    dve.wait_ge(eh_ready, e * 4 + (j + 1))
                    nc.vector.scalar_tensor_tensor(out=el[:, j], in0=psE(j), scalar=b2[:, e, j:j + 1], in1=eh[:, j],
                                                   op0=ALU.add, op1=ALU.subtract).then_inc(el_ready, 1)

            def last_bias_add(e, n):
                dve.wait_ge(n_psum, e * 4 + (n + 1))
                at_least(dve, x_added, e * 4 + (n - 1))
                nc.vector.tensor_tensor(last[:, n % 2], psN(n), last_bias[:], ALU.add).then_inc(biased, 1)

            def unit(e, f, r):
                g = e * FC + f
                final = isinstance(e, int) and e == E - 1
                if not final or before_last(f):
                    low_weights(g + 2, (r + 2) % RING)
                dve.wait_ge(hh_ready, g + 1)
                nc.vector.tensor_tensor(hl[:, r % 2], hid[:, r % 2], hh[:, r % 2], ALU.subtract).then_inc(hl_ready, 1)
                if isinstance(f, int) and not (isinstance(e, int) and e == 0):
                    if f == 0:
                        result(e - 1)
                    if f in LAST_AT:
                        for n in LAST_AT[f]:
                            last_bias_add(e - 1, n)

            low_weights(0, 0)
            low_weights(1, 1)
            run_experts(dve, unit)
            result(E - 1)
            for n in range(4):
                last_bias_add(E - 1, n)

        @block.gpsimd
        def _(pool):
            def add(e):
                for n in range(4):
                    pool.wait_ge(last_ready, e * 4 + (n + 1))
                    tile = x[:, n % 2, e * TE + n // 2, :]
                    nc.gpsimd.tensor_tensor(tile, tile, last[:, n % 2], ALU.add).then_inc(x_added, 1)

            with pool.Fori(0, E) as e:
                add(e)

        @block.tensor
        def _(pe):
            def up(e, f, r):
                g = e * FC + f
                pe.wait_ge(wl_ready, g + 1)
                at_least(pe, gelu_done, g - 1)
                tokens = slice(e * TE, (e + 1) * TE) if isinstance(e, int) else bass.ds(e * TE, TE)
                for n, (w, s) in enumerate([(wh, xah), (wh, xal), (wl, xah)]):
                    for c in range(DC):
                        mm = nc.tensor.matmul(psU(r), w[:, r, 0, c], s[:, c, tokens].rearrange("p h b t -> p (h b t)"),
                                              start=n + c == 0, stop=n == 2 and c == DC - 1)
                mm.then_inc(h_psum, 1)

            def down(e, f, r):
                g = e * FC + f
                first = isinstance(f, int) and f == 0
                final = isinstance(f, int) and f == FC - 1
                pe.wait_ge(hl_ready, g + 1)
                if first:
                    at_least(pe, el_ready, e * 4)
                for j in range(DC):
                    for n, (w, s) in enumerate([(wh, hh), (wl, hh), (wh, hl)]):
                        mm = nc.tensor.matmul(psE(j), w[:, r, 1, j], s[:, r % 2], start=first and n == 0,
                                              stop=final and n == 2, skip_group_check=True)
                mm.then_inc(used, 1)

            def last_projection(e, n):
                pe.wait_ge(el_ready, e * 4 + 4)
                at_least(pe, biased, e * 4 + (n - 1))
                for m, (s, w) in enumerate([(eh, wnh), (el, wnh), (eh, wnl)]):
                    for c in range(DC):
                        mm = nc.tensor.matmul(psN(n), s[:, c, n * P:(n + 1) * P], w[:, 0, c], start=m + c == 0,
                                              stop=m == 2 and c == DC - 1)
                mm.then_inc(n_psum, 1)

            def unit(e, f, r):
                up(e, f, r)
                if isinstance(f, int) and f == 0:
                    if not (isinstance(e, int) and e == 0):
                        down(e - 1, FC - 1, RING - 1)
                else:
                    down(e, f - 1, (r - 1) % RING)
                if isinstance(f, int) and f in LAST_AT and not (isinstance(e, int) and e == 0):
                    for n in LAST_AT[f]:
                        last_projection(e - 1, n)

            run_experts(pe, unit)
            down(E - 1, FC - 1, RING - 1)
            for n in range(4):
                last_projection(E - 1, n)



def build(nc, d, out):
    with ExitStack() as ctx:
        ph = Phase(nc, ctx, "all")
        x = ph.sb("x", [P, B, TB, D])
        ident = ph.sb("ident", [P, P])
        ones = ph.sb("ones", [P, P])
        minus_half = ph.sb("minus_half", [P, 2])
        eps = ph.sb("eps", [P, 1])
        carried = ph.sb("carried", [P, 2])
        consts = (minus_half, carried)
        made = ph.sem("made")
        with nc.Block() as block:
            @block.gpsimd
            def _(pool):
                nc.gpsimd.memset(ident[:], 0.0).then_inc(made, 1)
                nc.gpsimd.memset(ones[:], 1.0).then_inc(made, 1)
                nc.gpsimd.memset(minus_half[:], -0.5).then_inc(made, 1)
                nc.gpsimd.memset(eps[:], LN_EPS).then_inc(made, 1)
                pool.wait_ge(made, 4)
                nc.gpsimd.affine_select(out=ident[:], in_=ident[:], compare_op=ALU.not_equal, fill=1.0, base=0,
                                        pattern=[[-1, P]], channel_multiplier=1).then_inc(made, 1)
                pool.wait_ge(made, 5)
        with ExitStack() as ctx2:
            ph = Phase(nc, ctx2, "l0")
            q_hat = ph.sb("q_hat", [P, B, TB, D])
            gf = ph.sb("gf", [P, B, D])
            l0_attention(nc, d, x, q_hat, gf, ident, ones, minus_half, consts)
            l0_cross_attention(nc, d, x, q_hat, gf, ident, minus_half, eps, consts)
        l0_ffn(nc, d, x, ident, ones, minus_half, eps, consts)
        l1_attention(nc, d, x, ident, minus_half, eps, consts)
        l1_cross_attention(nc, d, x, ident, ones, minus_half, eps, consts)
        l1_ffn(nc, d, x, out, ident, minus_half, eps, consts)


def layouts(i):
    import numpy as np

    def lin(w):
        return w.reshape(w.shape[0] // P, P, -1).transpose(1, 0, 2)

    def rows(v):
        return np.broadcast_to(v, (P, *v.shape))

    return {
        "x": i["x"].reshape(B, TB, P, D),
        "w_a0": np.stack([lin(i[f"L0_attn_W_{n}"].T) for n in "qkv"], 1),
        "ctxT": lin(i["ctx_1024"].reshape(B * K, D).T),
        "mask": rows(i["mask_BxS2_if1"]),
        "w_f0_1": lin(i["L0_ffn_w1"].T),
        "w_f0_2": lin(i["L0_ffn_w2"].T).reshape(P, 4, F),
        "b_f0_1": rows(i["L0_ffn_b1"]),
        "b_f0_2": rows(i["L0_ffn_b2"]),
        "w_a1q": lin(i["L1_attn_W_q"].T),
        "w_a1k": lin(i["L1_attn_W_k"].T),
        "w_a1v": lin(i["L1_attn_W_v"].T),
        "w_a1o": lin(i["L1_attn_W_o"].T),
        "beta": rows(i["L1_attn_beta_param"]),
        "ctx_rows": i["ctx_1024"].transpose(1, 0, 2),
        "w_sim": i["L1_xattn_w_sim"].reshape(3, DC, P).transpose(2, 0, 1),
        "b_sim": rows(i["L1_xattn_b_sim"]),
        "b_x1": rows(i["L1_xattn_b_qv"]),
        **{f"w_x1_{n}": lin(i["L1_xattn_W_qv"][n * D:(n + 1) * D]) for n in range(4)},
        "w_f1a": lin(i["L1_ffn_attn_w"].T),
        "w_f1n": lin(i["L1_ffn_next_w"].T),
        "b_f1a": rows(i["L1_ffn_attn_b"]),
        "b_f1n": rows(i["L1_ffn_next_b"]),
        "ln_scale": rows(i["L1_ffn_ln_scale"]),
        "ln_bias": rows(i["L1_ffn_ln_bias"]),
        "b_f1_1": i["L1_ffn_b1"].reshape(E, FC, P).transpose(2, 0, 1),
        "b_f1_2": i["L1_ffn_b2"].reshape(E, DC, P).transpose(2, 0, 1),
        "w_f1": np.concatenate([
            i["L1_ffn_w1"].reshape(E, DC, P, FC, P).transpose(0, 3, 2, 1, 4).reshape(UNITS, P, D),
            i["L1_ffn_w2"].reshape(UNITS, P, D)], 2),
        "w_x0q": lin(i["L0_xattn_Wq"]),
        "w_x0k": lin(i["L0_xattn_Wk"]),
        "w_x0v": lin(i["L0_xattn_Wv"]),
        "w_x0o": lin(i["L0_xattn_Wo"]),
    }


def kernel(**inputs):
    import numpy as _np
    import concourse.bacc as _bacc
    from concourse import mybir as _mybir
    from concourse.bass_utils import run_bass_kernel_spmd as _run

    nc = _bacc.Bacc("TRN2", target_bir_lowering=False, num_devices=1)
    arrays, d = {}, {}
    for name, a in layouts({k: _np.asarray(v) for k, v in inputs.items()}).items():
        a = _np.ascontiguousarray(a)
        arrays[f"in_{name}"] = a
        d[name] = nc.dram_tensor(f"in_{name}", a.shape, _mybir.dt.from_np(a.dtype), kind="ExternalInput").ap()
    out = nc.dram_tensor("out_0", (B, TB, P, D), F32, kind="ExternalOutput").ap()
    build(nc, d, out)
    r = _run(nc, [arrays], core_ids=[0])
    return r.results[0]["out_0"].reshape(B, S, D)
```

```python
from contextlib import ExitStack

import concourse.bass as bass
from concourse import mybir

F32 = mybir.dt.float32
BF16 = mybir.dt.bfloat16
I32 = mybir.dt.int32
ALU = mybir.AluOpType
ACT = mybir.ActivationFunctionType
AX_X = mybir.AxisListType.X

P = 128
B = 2
S = 2048
D = 512
DC = D // P
TB = S // P
N_TILES = B * TB
LN_EPS = 1e-5



def run_stages(eng, stages, n=N_TILES):
    top = max(lag for lag, _ in stages)
    head = top + 2

    def once(i):
        for lag, stage in stages:
            if 0 <= i - lag < n:
                stage((i - lag) // 2, (i - lag) % 2)

    for i in range(head):
        once(i)
    pairs = (n - head) // 2
    if pairs:
        with eng.Fori(0, pairs) as k:
            for u in (0, 1):
                for lag, stage in stages:
                    c = head + u - lag
                    stage(k + c // 2, c % 2)
    for i in range(head + 2 * pairs, n + top):
        once(i)


def reached(eng, sem, h, p, k=1, per=1):
    eng.wait_ge(sem, h * (2 * per) + (p * per + k))


def freed(eng, sem, h, p, k=1, per=1, back=2, n=N_TILES):
    if isinstance(h, int):
        t = min(2 * h + p - back, n - 1)
        if t >= 0:
            eng.wait_ge(sem, t * per + k)
        return
    eng.wait_ge(sem, h * (2 * per) + ((p - back) * per + k))


def carry_wait(nc, eng, consts):
    a, b = consts
    if eng is nc.gpsimd:
        nc.gpsimd.tensor_tensor(b[:, 0:1], a[:, 0:1], a[:, 1:2], ALU.add)
    else:
        nc.vector.tensor_copy(b[:, 1:2], a[:, 0:1])


class Phase:

    def __init__(self, nc, ctx, name):
        self.nc, self.ctx, self.name = nc, ctx, name
        self.sems = []
        ctx.callback(self.end)

    def sb(self, name, shape, dt=F32):
        return self.ctx.enter_context(self.nc.sbuf_tensor(f"{self.name}_{name}", shape, dt))

    def banks(self, n=8):
        return self.ctx.enter_context(self.nc.psum_tensor(f"{self.name}_banks", [P, n, 512], F32))

    def sem(self, name):
        self.sems.append(self.nc.alloc_semaphore(f"{self.name}_{name}"))
        return self.sems[-1]

    def end(self):
        if self.sems:
            self.nc.clear_and_free_semaphores(self.sems)
            self.nc.all_engine_barrier()



def l0_attention(nc, d, x, q_hat, gf, ident, ones, minus_half, consts):
    with ExitStack() as ctx:
        ph = Phase(nc, ctx, "a0")
        w = ph.sb("w", [P, 3, DC, D])
        xn = ph.sb("xn", [P, 2, D])
        wh = ph.sb("wh", [P, 3, DC, D], BF16)
        wl = ph.sb("wl", [P, 3, DC, D], BF16)
        xh = ph.sb("xh", [P, 2, DC, P], BF16)
        xl = ph.sb("xl", [P, 2, DC, P], BF16)
        stats = ph.sb("stats", [P, 2, 6])
        mv = ph.sb("mv", [P, 2, 2])
        var_eps = ph.sb("var_eps", [P, 2])
        rstd = ph.sb("rstd", [P, 2])
        squares = ph.sb("squares", [P, D])
        ss = ph.sb("ss", [P, 2, 2])
        ss_max = ph.sb("ss_max", [P, 2, 2])
        rnorm = ph.sb("rnorm", [P, 2, 2])
        v_sb = ph.sb("v_sb", [P, 2, D])
        kv = ph.sb("kv", [P, 2, D])
        acc = ph.sb("acc", [P, 2, D])
        ps = ph.banks()
        psT, psG = ps[:, 0], ps[:, 7]
        psQ, psK, psV = (lambda p: ps[:, 1 + p]), (lambda p: ps[:, 3 + p]), (lambda p: ps[:, 5 + p])

        x_in = [ph.sem(f"x_in{p}") for p in range(2)]
        w_in = [ph.sem(f"w_in{j}") for j in range(3)]
        wh_ready = ph.sem("wh_ready")
        wl_ready = ph.sem("wl_ready")
        acc_zero = ph.sem("acc_zero")
        stats_done = ph.sem("stats_done")
        mv_ready = ph.sem("mv_ready")
        var_ready = ph.sem("var_ready")
        ss_ready = ph.sem("ss_ready")
        rstd_ready = ph.sem("rstd_ready")
        xn_ready = ph.sem("xn_ready")
        xnT_psum = ph.sem("xnT_psum")
        xh_ready = ph.sem("xh_ready")
        xl_ready = ph.sem("xl_ready")
        proj = ph.sem("proj")
        act_qkv = ph.sem("act_qkv")
        rnorm_ready = ph.sem("rnorm_ready")
        q_kept = ph.sem("q_kept")
        kv_ready = ph.sem("kv_ready")
        kv_added = ph.sem("kv_added")
        gf_psum = ph.sem("gf_psum")
        gf_ready = ph.sem("gf_ready")
        block = ctx.enter_context(nc.Block())

        @block.sync
        def _(sp):
            def load(h, p):
                if not (isinstance(h, int) and h == 0):
                    sp.wait_ge(x_in[p], h * 16)
                sp.dma_start(x[:, p, h, :], d["x"][p, h]).then_inc(x_in[p], 16)

            run_stages(sp, [(0, load)])
            for p in range(2):
                sp.wait_ge(x_in[p], TB * 16)

        @block.gpsimd
        def _(pool):
            nc.gpsimd.memset(acc[:], 0.0).then_inc(acc_zero, 1)

            def layernorm_scale(h, p):
                reached(pool, mv_ready, h, p)
                freed(pool, rstd_ready, h, p)
                carry_wait(nc, pool, consts)
                nc.gpsimd.tensor_scalar(var_eps[:, p:p + 1], mv[:, p, 1:2], LN_EPS, None, ALU.add).then_inc(var_ready, 1)
                reached(pool, var_ready, h, p)
                nc.gpsimd.tensor_tensor(rstd[:, p:p + 1], var_eps[:, p:p + 1], minus_half[:, 0:1],
                                        ALU.pow).then_inc(rstd_ready, 1)

            def norms(h, p):
                reached(pool, act_qkv, h, p, 2, 3)
                freed(pool, rnorm_ready, h, p)
                carry_wait(nc, pool, consts)
                nc.gpsimd.tensor_scalar(ss_max[:, p, :], ss[:, p, :], 1e-24, None, ALU.max).then_inc(ss_ready, 1)
                reached(pool, ss_ready, h, p)
                freed(pool, kv_ready, h, p)
                nc.gpsimd.tensor_tensor(rnorm[:, p, :], ss_max[:, p, :], minus_half[:, 0:2],
                                        ALU.pow).then_inc(rnorm_ready, 1)

            def add_kv(h, p):
                reached(pool, kv_ready, h, p)
                freed(pool, kv_added, h, p)
                nc.gpsimd.tensor_tensor(acc[:, p, :], acc[:, p, :], kv[:, p, :], ALU.add).then_inc(kv_added, 1)

            pool.wait_ge(acc_zero, 1)
            run_stages(pool, [(0, layernorm_scale), (2, norms), (2, add_kv)])

        @block.vector
        def _(dve):
            def normalise(h, p):
                dve.wait_ge(x_in[p], h * 16 + 16)
                nc.vector.bn_stats(stats[:, p, :], x[:, p, h, :]).then_inc(stats_done, 1)
                reached(dve, stats_done, h, p)
                carry_wait(nc, dve, consts)
                nc.vector.bn_aggr(mv[:, p, :], stats[:, p, :]).then_inc(mv_ready, 1)
                reached(dve, rstd_ready, h, p)
                freed(dve, xnT_psum, h, p)
                nc.vector.tensor_scalar(xn[:, p, :], x[:, p, h, :], mv[:, p, 0:1], rstd[:, p:p + 1],
                                        ALU.subtract, ALU.mult).then_inc(xn_ready, 1)

            def products(h, p):
                reached(dve, rnorm_ready, h, p)
                nc.vector.tensor_scalar(q_hat[:, h, p, :], psQ(p), rnorm[:, p, 0:1], None,
                                        ALU.mult).then_inc(q_kept, 1)
                reached(dve, act_qkv, h, p, 3, 3)
                freed(dve, kv_added, h, p)
                nc.vector.scalar_tensor_tensor(out=kv[:, p, :], in0=psK(p), scalar=rnorm[:, p, 1:2],
                                               in1=v_sb[:, p, :], op0=ALU.mult, op1=ALU.mult).then_inc(kv_ready, 1)

            def low_x(h, p):
                reached(dve, xh_ready, h, p)
                freed(dve, proj, h, p, 3, 3)
                nc.vector.tensor_tensor(xl[:, p].rearrange("p c t -> p (c t)"), psT, xh[:, p].rearrange("p c t -> p (c t)"),
                                        ALU.subtract).then_inc(xl_ready, 1)

            def low_weights(h, p):
                if isinstance(h, int) and 2 * h + p == 0:
                    for j in range(3):
                        dve.wait_ge(wh_ready, j + 1)
                        nc.vector.tensor_tensor(wl[:, j], w[:, j], wh[:, j], ALU.subtract).then_inc(wl_ready, 1)

            run_stages(dve, [(1, low_x), (0, normalise), (0, low_weights), (2, products)])
            for p in range(2):
                dve.wait_ge(gf_psum, p + 1)
                nc.vector.tensor_scalar(gf[:, p, :], psG, 1.0 / S, None, ALU.mult).then_inc(gf_ready, 1)

        @block.scalar
        def _(act):
            for j in range(3):
                act.dma_start(w[:, j], d["w_a0"][:, j]).then_inc(w_in[j], 16)
            for j in range(3):
                act.wait_ge(w_in[j], 16)
                nc.scalar.copy(wh[:, j], w[:, j]).then_inc(wh_ready, 1)

            def high_x(h, p):
                reached(act, xnT_psum, h, p)
                freed(act, proj, h, p, 3, 3)
                nc.scalar.copy(xh[:, p].rearrange("p c t -> p (c t)"), psT).then_inc(xh_ready, 1)

            def square_sums(h, p):
                freed(act, rnorm_ready, h, p)
                freed(act, act_qkv, h, p, 2, 3, back=1)
                reached(act, proj, h, p, 1, 3)
                nc.scalar.activation(squares[:], psQ(p), ACT.Square, accum_out=ss[:, p, 0:1]).then_inc(act_qkv, 1)
                reached(act, proj, h, p, 2, 3)
                reached(act, act_qkv, h, p, 1, 3)
                nc.scalar.activation(squares[:], psK(p), ACT.Square, accum_out=ss[:, p, 1:2]).then_inc(act_qkv, 1)
                reached(act, proj, h, p, 3, 3)
                freed(act, kv_ready, h, p)
                nc.scalar.copy(v_sb[:, p, :], psV(p)).then_inc(act_qkv, 1)

            run_stages(act, [(1, high_x), (2, square_sums)])

        @block.tensor
        def _(pe):
            def transposes(h, p):
                reached(pe, xn_ready, h, p)
                freed(pe, xl_ready, h, p, back=1)
                for c in range(DC):
                    mm = nc.tensor.transpose(psT[:, c * P:(c + 1) * P], xn[:, p, c * P:(c + 1) * P], ident[:])
                mm.then_inc(xnT_psum, 1)

            def project(h, p):
                reached(pe, xl_ready, h, p)
                freed(pe, act_qkv, h, p, 3, 3)
                freed(pe, q_kept, h, p)
                freed(pe, kv_ready, h, p)
                for j, bank in enumerate((psQ(p), psK(p), psV(p))):
                    if isinstance(h, int) and 2 * h + p == 0:
                        pe.wait_ge(wl_ready, j + 1)
                    for n, (s, half) in enumerate([(xh, wh), (xl, wh), (xh, wl)]):
                        for c in range(DC):
                            mm = nc.tensor.matmul(bank, s[:, p, c, :], half[:, j, c, :], start=n + c == 0,
                                                  stop=n == 2 and c == DC - 1)
                    mm.then_inc(proj, 1)

            run_stages(pe, [(1, transposes), (2, project)])
            pe.wait_ge(kv_added, N_TILES)
            for p in range(2):
                if p:
                    pe.wait_ge(gf_ready, p)
                nc.tensor.matmul(psG, ones[:], acc[:, p, :], start=True, stop=True).then_inc(gf_psum, 1)



K = 77
H = 16
DK = D // H
HC = P // DK
NEG = -1e30


def l0_cross_attention(nc, d, x, q_hat, gf, ffn_raw, ffn_in, ident, minus_half, eps, consts):
    with ExitStack() as ctx:
        ph = Phase(nc, ctx, "x0")
        wq = ph.sb("wq", [P, DC, D])
        wo = ph.sb("wo", [P, DC, D])
        keys = ph.sb("keys", [P, B, DC, HC * K])
        values = ph.sb("values", [K, B, H, P])
        bias = ph.sb("bias", [P, 2, B, K])
        ps = ph.banks()
        ctx_in = ph.sem("ctx_in")
        w_in = ph.sem("w_in")

        with ExitStack() as ctx2:
            ph2 = Phase(nc, ctx2, "x0s")
            ctxT = ph2.sb("ctxT", [P, DC, B * K])
            wk = ph2.sb("wk", [P, DC, D])
            wv = ph2.sb("wv", [P, DC, D])
            mask = ph2.sb("mask", [P, B, K], I32)
            wv_in = ph2.sem("wv_in")
            mask_in = ph2.sem("mask_in")
            keys_zero = ph2.sem("keys_zero")
            masked_made = ph2.sem("masked_made")
            causal_made = ph2.sem("causal_made")
            k_psum = ph2.sem("k_psum")
            k_kept = ph2.sem("k_kept")
            v_psum = ph2.sem("v_psum")
            v_kept = ph2.sem("v_kept")
            with nc.Block() as block:
                @block.sync
                def _(sp):
                    sp.dma_start(ctxT[:], d["ctxT"]).then_inc(ctx_in, 16)
                    sp.dma_start(wk[:], d["w_x0k"]).then_inc(ctx_in, 16)
                    sp.dma_start(wv[:], d["w_x0v"]).then_inc(wv_in, 16)
                    sp.dma_start(mask[:], d["mask"]).then_inc(mask_in, 16)
                    sp.dma_start(wq[:], d["w_x0q"]).then_inc(w_in, 16)
                    sp.dma_start(wo[:], d["w_x0o"]).then_inc(w_in, 16)

                @block.gpsimd
                def _(pool):
                    nc.gpsimd.memset(keys[:], 0.0).then_inc(keys_zero, 1)
                    nc.gpsimd.memset(values[:], 0.0).then_inc(keys_zero, 1)
                    pool.wait_ge(masked_made, 2)
                    nc.gpsimd.affine_select(out=bias[:, 0], in_=bias[:, 0], compare_op=ALU.is_ge, fill=NEG, base=0,
                                            pattern=[[0, B], [-1, K]], channel_multiplier=1).then_inc(causal_made, 1)

                @block.tensor
                def _(pe):
                    pe.wait_ge(ctx_in, 32)
                    for j in range(DC):
                        for c in range(DC):
                            mm = nc.tensor.matmul(ps[:, j, 0:B * K], wk[:, c, j * P:(j + 1) * P], ctxT[:, c, :],
                                                  start=c == 0, stop=c == DC - 1)
                        mm.then_inc(k_psum, 1)
                    pe.wait_ge(wv_in, 16)
                    for b in range(B):
                        for c in range(DC):
                            mm = nc.tensor.matmul(ps[0:K, DC + b], ctxT[:, c, b * K:(b + 1) * K], wv[:, c, :],
                                                  start=c == 0, stop=c == DC - 1)
                        mm.then_inc(v_psum, 1)

                @block.vector
                def _(dve):
                    dve.wait_ge(mask_in, 16)
                    for n in range(2):
                        nc.vector.tensor_scalar(bias[:, n], mask[:], 0, NEG, ALU.is_equal,
                                                ALU.mult).then_inc(masked_made, 1)

                @block.scalar
                def _(act):
                    act.wait_ge(keys_zero, 2)
                    for j in range(DC):
                        act.wait_ge(k_psum, j + 1)
                        for g in range(HC):
                            r = slice(g * DK, (g + 1) * DK)
                            for b in range(B):
                                nc.scalar.activation(keys[r, b, j, g * K:(g + 1) * K], ps[r, j, b * K:(b + 1) * K],
                                                     ACT.Copy, scale=float(DK) ** -0.5).then_inc(k_kept, 1)
                    for b in range(B):
                        act.wait_ge(v_psum, b + 1)
                        for g in range(HC):
                            nc.scalar.copy(values[:, b].rearrange("k (c g) n -> k g c n", g=HC)[:, g, :, g * DK:(g + 1) * DK],
                                           ps[0:K, DC + b].rearrange("k (c g n) -> k g c n", g=HC, n=DK)[:, g]).then_inc(v_kept, 1)

        moved = ph.sb("moved", [P, 2, D])
        xn = ph.sb("xn", [P, 2, D])
        xnT = ph.sb("xnT", [P, DC, P])
        qT = ph.sb("qT", [P, 2, DC, P])
        stats = ph.sb("stats", [P, 2, 6])
        mv = ph.sb("mv", [P, 2, 2])
        var_eps = ph.sb("var_eps", [P, 2])
        rstd = ph.sb("rstd", [P, 2])
        probs = ph.sb("probs", [P, 2, H, K])
        top = ph.sb("top", [P, 2, H])
        total = ph.sb("total", [P, 2, H])
        inv = ph.sb("inv", [P, 2, H])
        pT = ph.sb("pT", [K, 2, HC, P])
        attnT = ph.sb("attnT", [P, DC, P])
        psT, psQ, psV, psY = ps[:, 0], ps[:, 1], ps[:, 6], ps[:, 7]
        psS = lambda j: ps[:, 2 + j % 2, 0:HC * K]
        psP = lambda g: ps[0:K, 4 + g % 2]

        names = ("moved_ready x_moved stats_done mv_ready var_ready rstd_ready xn_ready xnT_psum xnT_ready qT_psum "
                 "qT_ready scores biased top_ready shifted exp_ready total_ready inv_ready probs_ready pT_psum pT_ready "
                 "attnT_psum attnT_ready y_psum x_added").split()
        (moved_ready, x_moved, stats_done, mv_ready, var_ready, rstd_ready, xn_ready, xnT_psum, xnT_ready, qT_psum,
         qT_ready, scores, biased, top_ready, shifted, exp_ready, total_ready, inv_ready, probs_ready, pT_psum, pT_ready,
         attnT_psum, attnT_ready, y_psum, x_added) = (ph.sem(n) for n in names)
        block = ctx.enter_context(nc.Block())

        @block.sync
        def _(sp):
            for n in range(2):
                for q in range(4):
                    sp.wait_ge(moved_ready, (4 * n + q + 1) * (N_TILES // 8))
                    sp.dma_start(ffn_raw[:, n, q], d[f"w_f0_{n + 1}"][:, q]).then_inc(ffn_in[n], 16)

        @block.gpsimd
        def _(pool):
            def move(h, p):
                freed(pool, x_moved, h, p)
                nc.gpsimd.tensor_tensor(moved[:, p], q_hat[:, h, p, :], gf[:, p, :], ALU.mult).then_inc(moved_ready, 1)

            def layernorm_scale(h, p):
                reached(pool, mv_ready, h, p)
                freed(pool, xn_ready, h, p)
                nc.gpsimd.tensor_tensor(var_eps[:, p:p + 1], mv[:, p, 1:2], eps[:], ALU.add).then_inc(var_ready, 1)
                reached(pool, var_ready, h, p)
                nc.gpsimd.tensor_tensor(rstd[:, p:p + 1], var_eps[:, p:p + 1], minus_half[:, 0:1],
                                        ALU.pow).then_inc(rstd_ready, 1)

            run_stages(pool, [(0, move), (0, layernorm_scale)])

        @block.vector
        def _(dve):
            def statistics(h, p):
                reached(dve, moved_ready, h, p)
                nc.vector.tensor_tensor(x[:, p, h, :], x[:, p, h, :], moved[:, p], ALU.add).then_inc(x_moved, 1)
                reached(dve, x_moved, h, p)
                carry_wait(nc, dve, consts)
                nc.vector.bn_stats(stats[:, p, :], x[:, p, h, :]).then_inc(stats_done, 1)
                reached(dve, stats_done, h, p)
                freed(dve, xn_ready, h, p)
                carry_wait(nc, dve, consts)
                nc.vector.bn_aggr(mv[:, p, :], stats[:, p, :]).then_inc(mv_ready, 1)

            def normalise(h, p):
                reached(dve, rstd_ready, h, p)
                freed(dve, xnT_psum, h, p)
                nc.vector.tensor_scalar(xn[:, p, :], x[:, p, h, :], mv[:, p, 0:1], rstd[:, p:p + 1],
                                        ALU.subtract, ALU.mult).then_inc(xn_ready, 1)

            def residual(h, p):
                reached(dve, y_psum, h, p)
                nc.vector.tensor_tensor(x[:, p, h, :], psY, x[:, p, h, :], ALU.add).then_inc(x_added, 1)

            def divide(h, p):
                reached(dve, exp_ready, h, p)
                freed(dve, inv_ready, h, p)
                nc.vector.tensor_reduce(total[:, p], probs[:, p], AX_X, ALU.add).then_inc(total_ready, 1)
                reached(dve, total_ready, h, p)
                freed(dve, probs_ready, h, p)
                nc.vector.reciprocal(inv[:, p], total[:, p]).then_inc(inv_ready, 1)
                reached(dve, inv_ready, h, p)
                nc.vector.tensor_tensor(probs[:, p], probs[:, p], inv[:, p].unsqueeze(2).to_broadcast([P, H, K]),
                                        ALU.mult).then_inc(probs_ready, 1)

            def shift(h, p):
                first = 0 if isinstance(h, int) and h == 0 else 1
                freed(dve, probs_ready, h, p)
                freed(dve, pT_psum, h, p, 4, 4)
                for j in range(DC):
                    reached(dve, scores, h, p, j + 1, DC)
                    nc.vector.tensor_tensor(probs[:, p, j * HC:(j + 1) * HC], psS(j).rearrange("t (n k) -> t n k", n=HC),
                                            bias[:, first, p].unsqueeze(1).to_broadcast([P, HC, K]),
                                            ALU.add).then_inc(biased, 1)
                reached(dve, biased, h, p, DC, DC)
                freed(dve, shifted, h, p)
                nc.vector.tensor_reduce(top[:, p], probs[:, p], AX_X, ALU.max).then_inc(top_ready, 1)
                reached(dve, top_ready, h, p)
                nc.vector.tensor_tensor(probs[:, p], probs[:, p], top[:, p].unsqueeze(2).to_broadcast([P, H, K]),
                                        ALU.subtract).then_inc(shifted, 1)

            run_stages(dve, [(3, divide), (0, statistics), (2, shift), (4, residual), (0, normalise)])

        @block.scalar
        def _(act):
            flat = "p c t -> p (c t)"

            def keep_attnT(h, p):
                reached(act, attnT_psum, h, p)
                freed(act, y_psum, h, p, back=1)
                nc.scalar.copy(attnT[:].rearrange(flat), psV).then_inc(attnT_ready, 1)

            def keep_xnT(h, p):
                reached(act, xnT_psum, h, p)
                freed(act, qT_psum, h, p, back=1)
                nc.scalar.copy(xnT[:].rearrange(flat), psT).then_inc(xnT_ready, 1)

            def keep_qT(h, p):
                reached(act, qT_psum, h, p)
                freed(act, scores, h, p, DC, DC)
                nc.scalar.copy(qT[:, p].rearrange(flat), psQ).then_inc(qT_ready, 1)

            def keep_pT(chunks):
                def stage(h, p):
                    for g in chunks:
                        reached(act, pT_psum, h, p, g + 1, 4)
                        nc.scalar.copy(pT[:, g % 2].rearrange("k n t -> k (n t)"), psP(g)).then_inc(pT_ready, 1)
                return stage

            def exponentials(h, p):
                reached(act, shifted, h, p)
                flat_p = probs[:, p].rearrange("t n k -> t (n k)")
                nc.scalar.activation(flat_p, flat_p, ACT.Exp).then_inc(exp_ready, 1)

            run_stages(act, [(2, keep_qT), (3, keep_pT([0, 1])), (1, keep_xnT), (3, keep_pT([2, 3])), (3, keep_attnT),
                             (2, exponentials)])

        @block.tensor
        def _(pe):
            def turn_xn(h, p):
                reached(pe, xn_ready, h, p)
                freed(pe, xnT_ready, h, p, back=1)
                for c in range(DC):
                    mm = nc.tensor.transpose(psT[:, c * P:(c + 1) * P], xn[:, p, c * P:(c + 1) * P], ident[:])
                mm.then_inc(xnT_psum, 1)

            def out_projection(h, p):
                reached(pe, attnT_ready, h, p)
                freed(pe, x_added, h, p, back=1)
                for c in range(DC):
                    mm = nc.tensor.matmul(psY, attnT[:, c, :], wo[:, c, :], start=c == 0, stop=c == DC - 1)
                mm.then_inc(y_psum, 1)

            def queries(h, p):
                reached(pe, xnT_ready, h, p)
                freed(pe, qT_ready, h, p, back=1)
                for j in range(DC):
                    for c in range(DC):
                        mm = nc.tensor.matmul(psQ[:, j * P:(j + 1) * P], wq[:, c, j * P:(j + 1) * P], xnT[:, c, :],
                                              start=c == 0, stop=c == DC - 1)
                mm.then_inc(qT_psum, 1)

            def score(chunks):
                def stage(h, p):
                    if 0 in chunks:
                        reached(pe, qT_ready, h, p)
                    for j in chunks:
                        if j < 2:
                            freed(pe, biased, h, p, j + 3, DC, back=1)
                        else:
                            reached(pe, biased, h, p, j - 1, DC)
                        nc.tensor.matmul(psS(j), qT[:, p, j, :], keys[:, p, j, :], start=True, stop=True).then_inc(scores, 1)
                return stage

            def turn(g, h, p):
                if g < 2:
                    freed(pe, pT_ready, h, p, g + 3, 4, back=1)
                else:
                    reached(pe, pT_ready, h, p, g - 1, 4)
                for n in range(HC):
                    mm = nc.tensor.transpose(psP(g)[:, n * P:(n + 1) * P], probs[:, p, g * HC + n, :], ident[:])
                mm.then_inc(pT_psum, 1)

            def turn_first(h, p):
                reached(pe, probs_ready, h, p)
                turn(0, h, p)
                turn(1, h, p)

            def attend(h, p):
                freed(pe, attnT_ready, h, p, back=1)

                def mix(g):
                    reached(pe, pT_ready, h, p, g + 1, 4)
                    for n in range(HC):
                        mm = nc.tensor.matmul(psV[:, g * P:(g + 1) * P], values[:, p, g * HC + n], pT[:, g % 2, n, :],
                                              start=n == 0, stop=n == HC - 1)
                    if g == 3:
                        mm.then_inc(attnT_psum, 1)

                for g in range(4):
                    mix(g)
                    if g < 2:
                        turn(g + 2, h, p)

            pe.wait_ge(w_in, 32)
            run_stages(pe, [(2, queries), (4, out_projection), (3, turn_first), (2, score([0, 1])), (1, turn_xn),
                            (2, score([2, 3])), (3, attend)])



F = 4 * D
FC = F // P
ROUND = 1.5 * 2.0 ** 23


def l0_ffn(nc, d, x, store, raw, raw_in, attn_raw, attn_in, ident, ones, minus_half, eps, consts):
    with ExitStack() as ctx:
        ph = Phase(nc, ctx, "f0")
        w1 = ph.sb("w1", [P, DC, F], BF16)
        w2 = ph.sb("w2", [P, FC, D], BF16)
        b1 = ph.sb("b1", [P, F])
        b2 = ph.sb("b2", [P, D])
        w_unit = ph.sb("w_unit", [P, 2])
        identb = ph.sb("identb", [P, P], BF16)
        ps = ph.banks()
        b_in = ph.sem("b_in")

        with ExitStack() as ctx2:
            ph2 = Phase(nc, ctx2, "f0s")
            sums = ph2.sb("sums", [P, 2, 4])
            sum1 = ph2.sb("sum1", [P, 2])
            mean = ph2.sb("mean", [P, 2])
            inv = ph2.sb("inv", [P, 2])
            summed, sum_ready, sum_psum, mean_ready, inv_ready, clipped, scaled, w_ready = (
                ph2.sem(n) for n in "summed sum_ready sum_psum mean_ready inv_ready clipped scaled w_ready".split())
            with nc.Block() as block:
                @block.sync
                def _(sp):
                    sp.dma_start(b1[:], d["b_f0_1"]).then_inc(b_in, 16)
                    sp.dma_start(b2[:], d["b_f0_2"]).then_inc(b_in, 16)

                @block.vector
                def _(dve):
                    nc.vector.tensor_copy(identb[:], ident[:])
                    dve.wait_ge(raw_in[0], 64)
                    nc.vector.tensor_reduce(sums[:, 0], raw[:, 0], AX_X, ALU.add,
                                            apply_absolute_value=True).then_inc(summed, 1)
                    dve.wait_ge(summed, 5)
                    nc.vector.tensor_reduce(sum1[:], sums[:], AX_X, ALU.add).then_inc(sum_ready, 1)
                    dve.wait_ge(sum_psum, 1)
                    nc.vector.tensor_scalar(mean[:], ps[:, 0, 0:2], 1.0 / (D * F), 1e-5, ALU.mult,
                                            ALU.max).then_inc(mean_ready, 1)
                    dve.wait_ge(mean_ready, 1)
                    nc.vector.reciprocal(inv[:], mean[:]).then_inc(inv_ready, 1)
                    nc.vector.tensor_scalar(w_unit[:], mean[:], 1.0 / 127.0, None, ALU.mult)
                    dve.wait_ge(inv_ready, 1)
                    for n in range(2):
                        for q in range(4):
                            part = raw[:, n, q]
                            nc.vector.tensor_scalar(part, part, inv[:, n:n + 1], 1.0, ALU.mult, ALU.min).then_inc(clipped, 1)
                            dve.wait_ge(clipped, 4 * n + q + 1)
                            nc.vector.tensor_scalar(part, part, -1.0, ROUND, ALU.max, ALU.add).then_inc(scaled, 1)

                @block.tensor
                def _(pe):
                    pe.wait_ge(sum_ready, 1)
                    nc.tensor.matmul(ps[:, 0, 0:2], ones[:], sum1[:], start=True, stop=True).then_inc(sum_psum, 1)

                @block.scalar
                def _(act):
                    act.wait_ge(raw_in[1], 64)
                    for q in range(4):
                        nc.scalar.activation(w2[:, 4 * q:4 * q + 4].rearrange("p f n -> p (f n)"), raw[:, 1, q], ACT.Abs,
                                             accum_out=sums[:, 1, q:q + 1]).then_inc(summed, 1)
                    for n in range(2):
                        for q in range(4):
                            act.wait_ge(scaled, 4 * n + q + 1)
                            to = w1[:, q] if n == 0 else w2[:, 4 * q:4 * q + 4].rearrange("p f n -> p (f n)")
                            nc.scalar.activation(to, raw[:, n, q], ACT.Copy, bias=-ROUND).then_inc(w_ready, 1)

        xn = ph.sb("xn", [P, 2, D])
        qx = ph.sb("qx", [P, 2, D], BF16)
        qxT = ph.sb("qxT", [P, 2, DC, P], BF16)
        stats = ph.sb("stats", [P, 2, 6])
        mv = ph.sb("mv", [P, 2, 2])
        rs = ph.sb("rs", [P, 2, 6])
        ax = ph.sb("ax", [P, 2, 4])
        sx = ph.sb("sx", [P, 8])
        hid = store[:, 0:2 * F].rearrange("p (b n) -> p b n", b=2)
        squares = store[:, 2 * F:3 * F]
        qh = store[:, 3 * F:4 * F].bitcast(BF16).rearrange("p (b n) -> p b n", b=2)
        ssh = ph.sb("ssh", [P, 2])
        rh = ph.sb("rh", [P, 2, 3])
        ah = ph.sb("ah", [P, 2, 4])
        sh = ph.sb("sh", [P, 2])
        qhT = ph.sb("qhT", [P, 2, FC, P], BF16)
        inv_f = ph.sb("inv_f", [P, 1])
        psT = ps[:, 0, 0:D // 2].bitcast(BF16)
        psH = lambda n: ps[:, 1 + n]
        psU = [ps[:, 5 + n].bitcast(BF16) for n in range(2)]
        psY = ps[:, 7]

        names = ("stats_done mv_ready rs_own rx_ready xn_ready top_ready ax_own kx_ready rounded qx_ready qxT_psum "
                 "qxT_ready b2_added h_psum h_biased gelu_done square_done hsquare_own rh_ready toph_ready ah_own "
                 "kh_ready h_rounded qh_ready qhT_psum qhT_ready y_psum x_added made").split()
        (stats_done, mv_ready, rs_own, rx_ready, xn_ready, top_ready, ax_own, kx_ready, rounded, qx_ready, qxT_psum,
         qxT_ready, b2_added, h_psum, h_biased, gelu_done, square_done, hsquare_own, rh_ready, toph_ready, ah_own,
         kh_ready, h_rounded, qh_ready, qhT_psum, qhT_ready, y_psum, x_added, made) = (ph.sem(n) for n in names)
        block = ctx.enter_context(nc.Block())

        @block.sync
        def _(sp):
            for n, name in enumerate("qkvo"):
                sp.dma_start(attn_raw[:, n], d[f"w_a1{name}"]).then_inc(attn_in[n], 16)

        @block.gpsimd
        def _(pool):
            nc.gpsimd.memset(inv_f[:], 1.0 / F).then_inc(made, 1)
            pool.wait_ge(made, 1)
            pool.wait_ge(b_in, 32)
            tt = nc.gpsimd.tensor_tensor

            def x_roots(h, p):
                v = mv[:, p, 1:2]
                r = [rs[:, p, n:n + 1] for n in range(6)]
                reached(pool, mv_ready, h, p)
                freed(pool, kx_ready, h, p)
                steps = [(r[0], v, eps[:], ALU.add), (r[1], r[0], minus_half[:, 0:1], ALU.pow), (r[2], v, r[1], ALU.mult),
                         (r[3], r[2], r[1], ALU.mult), (r[4], r[3], eps[:], ALU.add),
                         (r[5], r[4], minus_half[:, 0:1], ALU.pow)]
                for n, (out, a, b, op) in enumerate(steps):
                    if n:
                        reached(pool, rs_own, h, p, n, 6)
                    tt(out, a, b, op).then_inc(rs_own, 1)

            def add_b2(h, p):
                reached(pool, xn_ready, h, p)
                tt(x[:, p, h, :], x[:, p, h, :], b2[:], ALU.add).then_inc(b2_added, 1)

            def h_root(h, p):
                reached(pool, square_done, h, p)
                freed(pool, kh_ready, h, p)
                tt(rh[:, p, 0:1], ssh[:, p:p + 1], inv_f[:], ALU.mult).then_inc(hsquare_own, 1)
                reached(pool, hsquare_own, h, p, 1, 2)
                tt(rh[:, p, 1:2], rh[:, p, 0:1], eps[:], ALU.add).then_inc(hsquare_own, 1)
                reached(pool, hsquare_own, h, p, 2, 2)
                tt(rh[:, p, 2:3], rh[:, p, 1:2], minus_half[:, 0:1], ALU.pow).then_inc(rh_ready, 1)

            def round_h(h, p):
                freed(pool, qhT_psum, h, p, 2, 2)
                reached(pool, h_rounded, h, p)
                carry_wait(nc, pool, consts)
                nc.gpsimd.tensor_scalar(qh[:, p], hid[:, p], -ROUND, 1.0, ALU.add, ALU.mult).then_inc(qh_ready, 1)

            run_stages(pool, [(3, round_h), (0, x_roots), (2, h_root), (2, add_b2)])

        @block.vector
        def _(dve):
            def statistics(h, p):
                nc.vector.bn_stats(stats[:, p, :], x[:, p, h, :]).then_inc(stats_done, 1)

            def mean_and_variance(h, p):
                reached(dve, stats_done, h, p)
                freed(dve, rs_own, h, p, 3, 6)
                carry_wait(nc, dve, consts)
                nc.vector.bn_aggr(mv[:, p, :], stats[:, p, :]).then_inc(mv_ready, 1)

            def normalise(h, p):
                reached(dve, rs_own, h, p, 2, 6)
                freed(dve, qx_ready, h, p)
                nc.vector.tensor_scalar(xn[:, p, :], x[:, p, h, :], mv[:, p, 0:1], rs[:, p, 1:2],
                                        ALU.subtract, ALU.mult).then_inc(xn_ready, 1)

            def top_x(h, p):
                reached(dve, xn_ready, h, p)
                freed(dve, ax_own, h, p, 1, 2)
                nc.vector.tensor_reduce(ax[:, p, 0:1], xn[:, p, :], AX_X, ALU.max,
                                        apply_absolute_value=True).then_inc(top_ready, 1)

            def bound_x(h, p):
                reached(dve, top_ready, h, p)
                reached(dve, rs_own, h, p, 6, 6)
                freed(dve, kx_ready, h, p)
                nc.vector.tensor_scalar(ax[:, p, 1:2], ax[:, p, 0:1], rs[:, p, 5:6], 1e-5, ALU.mult,
                                        ALU.max).then_inc(ax_own, 1)

            def quantise(h, p):
                reached(dve, ax_own, h, p, 1, 2)
                nc.vector.reciprocal(ax[:, p, 2:3], ax[:, p, 1:2]).then_inc(ax_own, 1)
                nc.vector.tensor_scalar(sx[:, p:p + 1], ax[:, p, 1:2], w_unit[:, 0:1], None, ALU.mult)
                reached(dve, ax_own, h, p, 2, 2)
                freed(dve, rounded, h, p)
                nc.vector.tensor_scalar(ax[:, p, 3:4], ax[:, p, 2:3], rs[:, p, 5:6], 127.0, ALU.mult,
                                        ALU.mult).then_inc(kx_ready, 1)
                reached(dve, kx_ready, h, p)
                nc.vector.tensor_scalar(xn[:, p], xn[:, p], ax[:, p, 3:4], ROUND, ALU.mult, ALU.add).then_inc(rounded, 1)

            def bias(h, p):
                freed(dve, qh_ready, h, p)
                for n in range(4):
                    reached(dve, h_psum, h, p, n + 1, 4)
                    cols = slice(n * D, (n + 1) * D)
                    nc.vector.scalar_tensor_tensor(out=hid[:, p, cols], in0=psH(n), scalar=sx[:, p:p + 1],
                                                   in1=b1[:, cols], op0=ALU.mult, op1=ALU.add).then_inc(h_biased, 1)

            def top_h(h, p):
                reached(dve, gelu_done, h, p)
                freed(dve, ah_own, h, p, 1, 2)
                nc.vector.tensor_reduce(ah[:, p, 0:1], hid[:, p], AX_X, ALU.max,
                                        apply_absolute_value=True).then_inc(toph_ready, 1)

            def bound_h(h, p):
                reached(dve, toph_ready, h, p)
                reached(dve, rh_ready, h, p)
                freed(dve, kh_ready, h, p)
                nc.vector.tensor_scalar(ah[:, p, 1:2], ah[:, p, 0:1], rh[:, p, 2:3], 1e-5, ALU.mult,
                                        ALU.max).then_inc(ah_own, 1)

            def inverse_h(h, p):
                reached(dve, ah_own, h, p, 1, 2)
                nc.vector.reciprocal(ah[:, p, 2:3], ah[:, p, 1:2]).then_inc(ah_own, 1)

            def scale_h(h, p):
                freed(dve, x_added, h, p)
                nc.vector.tensor_scalar(sh[:, p:p + 1], ah[:, p, 1:2], w_unit[:, 1:2], None, ALU.mult)
                reached(dve, ah_own, h, p, 2, 2)
                freed(dve, h_rounded, h, p)
                nc.vector.tensor_scalar(ah[:, p, 3:4], ah[:, p, 2:3], rh[:, p, 2:3], 127.0, ALU.mult,
                                        ALU.mult).then_inc(kh_ready, 1)

            def residual(h, p):
                reached(dve, y_psum, h, p)
                reached(dve, b2_added, h, p)
                nc.vector.scalar_tensor_tensor(out=x[:, p, h, :], in0=psY, scalar=sh[:, p:p + 1], in1=x[:, p, h, :],
                                               op0=ALU.mult, op1=ALU.add).then_inc(x_added, 1)

            run_stages(dve, [(1, normalise), (1, top_x), (3, bound_h), (3, inverse_h), (3, scale_h), (2, bias),
                             (0, statistics), (1, bound_x), (0, mean_and_variance), (1, quantise), (2, top_h),
                             (4, residual)])

        @block.scalar
        def _(act):
            def keep_qxT(h, p):
                reached(act, qxT_psum, h, p)
                freed(act, h_psum, h, p, 4, 4)
                nc.scalar.copy(qxT[:, p].rearrange("p c t -> p (c t)"), psT).then_inc(qxT_ready, 1)

            def keep_qhT(h, p):
                freed(act, y_psum, h, p)
                for n in range(2):
                    reached(act, qhT_psum, h, p, n + 1, 2)
                    nc.scalar.copy(qhT[:, p, 8 * n:8 * n + 8].rearrange("p c t -> p (c t)"), psU[n]).then_inc(qhT_ready, 1)

            def gelu(h, p):
                reached(act, h_biased, h, p, 4, 4)
                nc.scalar.activation(hid[:, p], hid[:, p], ACT.Gelu).then_inc(gelu_done, 1)

            def integers_of_x(h, p):
                reached(act, rounded, h, p)
                freed(act, qxT_psum, h, p)
                nc.scalar.activation(qx[:, p], xn[:, p], ACT.Copy, bias=-ROUND).then_inc(qx_ready, 1)

            def square(h, p):
                reached(act, gelu_done, h, p)
                freed(act, hsquare_own, h, p, 1, 2)
                nc.scalar.activation(squares, hid[:, p], ACT.Square, accum_out=ssh[:, p:p + 1]).then_inc(square_done, 1)

            def scale_h(h, p):
                reached(act, kh_ready, h, p)
                nc.scalar.activation(hid[:, p], hid[:, p], ACT.Copy, scale=ah[:, p, 3:4], bias=ROUND).then_inc(h_rounded, 1)

            run_stages(act, [(3, scale_h), (2, gelu), (1, integers_of_x), (2, square), (1, keep_qxT), (3, keep_qhT)])

        @block.tensor
        def _(pe):
            def turn_x(h, p):
                reached(pe, qx_ready, h, p)
                freed(pe, qxT_ready, h, p, back=1)
                for c in range(DC):
                    mm = nc.tensor.transpose(psT[:, c * P:(c + 1) * P], qx[:, p, c * P:(c + 1) * P], identb[:])
                mm.then_inc(qxT_psum, 1)

            def turn_h(h, p):
                reached(pe, qh_ready, h, p)
                for n in range(2):
                    freed(pe, qhT_ready, h, p, n + 1, 2, back=1)
                    for c in range(8):
                        mm = nc.tensor.transpose(psU[n][:, c * P:(c + 1) * P],
                                                 qh[:, p, (8 * n + c) * P:(8 * n + c + 1) * P], identb[:])
                    mm.then_inc(qhT_psum, 1)

            def up(h, p):
                reached(pe, qxT_ready, h, p)
                for n in range(4):
                    freed(pe, h_biased, h, p, n + 1, 4, back=1)
                    for c in range(DC):
                        mm = nc.tensor.matmul(psH(n), qxT[:, p, c, :], w1[:, c, n * D:(n + 1) * D],
                                              start=c == 0, stop=c == DC - 1)
                    mm.then_inc(h_psum, 1)

            def down(h, p):
                freed(pe, x_added, h, p, back=1)
                for c in range(FC):
                    if c % 8 == 0:
                        reached(pe, qhT_ready, h, p, c // 8 + 1, 2)
                    mm = nc.tensor.matmul(psY, qhT[:, p, c, :], w2[:, c, :], start=c == 0, stop=c == FC - 1)
                mm.then_inc(y_psum, 1)

            run_stages(pe, [(2, up), (4, down), (1, turn_x), (3, turn_h)])



SEG = 64
CW = P + HC


def split_loaded(nc, ph, raw, w_in, high, low):
    with ExitStack() as ctx2:
        ph2 = Phase(nc, ctx2, ph.name + "w")
        high_made, low_made = ph2.sem("high_made"), ph2.sem("low_made")
        with nc.Block() as block:
            @block.scalar
            def _(act):
                for n, loaded in enumerate(w_in):
                    act.wait_ge(loaded, 16)
                    nc.scalar.copy(high[:, n], raw[:, n]).then_inc(high_made, 1)

            @block.vector
            def _(dve):
                for n in range(len(w_in)):
                    dve.wait_ge(high_made, n + 1)
                    nc.vector.tensor_tensor(low[:, n], raw[:, n], high[:, n], ALU.subtract).then_inc(low_made, 1)


def l1_attention(nc, d, x, store, raw, raw_in, ident, minus_half, eps, consts):
    with ExitStack() as ctx:
        ph = Phase(nc, ctx, "a1")
        halves_of = lambda ap: ap.bitcast(BF16).rearrange("p (w c n) -> p w c n", w=4, c=DC)
        wh, wl = halves_of(store[:, 0:4096]), halves_of(store[:, 4096:8192])
        split_loaded(nc, ph, raw, raw_in, wh, wl)
        WQ, WK, WV, WO = range(4)
        beta = ph.sb("beta", [P, H])
        rest = ph.sb("rest", [P, H])
        causal = ph.sb("causal", [P, SEG])
        blocks = ph.sb("blocks", [P, CW])
        memory = ph.sb("memory", [P, B, DC, CW])
        kdiag = store[:, 8192:12288].rearrange("p (b c s g t) -> p b c s g t", b=2, c=DC, s=2, g=HC)
        vpair = store[:, 12288:14336].rearrange("p (b s j n) -> p b s j n", b=2, s=2, j=H // 2)
        vd = ph.sb("vd", [P, 2, DC, CW])
        xn = ph.sb("xn", [P, 2, D])
        xh = ph.sb("xh", [P, 2, DC, P], BF16)
        xl = ph.sb("xl", [P, 2, DC, P], BF16)
        ah = ph.sb("ah", [P, 2, DC, P], BF16)
        al = ph.sb("al", [P, 2, DC, P], BF16)
        stats = ph.sb("stats", [P, 2, 6])
        mv = ph.sb("mv", [P, 2, 2])
        rs = ph.sb("rs", [P, 2, 2])
        expo = ph.sb("expo", [P, 2, DC, 2, SEG])
        relu = ph.sb("relu", [P, 2, DC, 2, SEG])
        qT = ph.sb("qT", [P, 2, DC, P])
        skq = ph.sb("skq", [P, 2, DC, 4, SEG])
        sk = ph.sb("sk", [P, 2, D])
        v = ph.sb("v", [P, 2, D])
        den = ph.sb("den", [P, 2, H])
        rden = ph.sb("rden", [P, 2, H])
        rden_b = ph.sb("rden_b", [P, 2, H])
        v_prev = ph.sb("v_prev", [P, D])
        update = ph.sb("update", [P, 2, DC, CW])
        from_memory = ph.sb("from_memory", [P, 2, D])
        score = ph.sb("score", [P, 2, H, SEG])
        top = ph.sb("top", [P, 2, H])
        total = ph.sb("total", [P, 2, H])
        inv = ph.sb("inv", [P, 2, H])
        inv_r = ph.sb("inv_r", [P, 2, H])
        pT = ph.sb("pT", [P, 2, 4, P])
        mixed = ph.sb("mixed", [P, D])
        a = ph.sb("a", [P, 2, D])
        ps = ph.banks()
        psT, psA, psB, psP = ps[:, 0], ps[:, 1], ps[:, 2], ps[:, 5]
        psS = ps[:, 3:5].rearrange("p b n -> p (b n)")
        psM = ps[:, 6:8, 0:2 * CW].rearrange("p b (c n) -> p b c n", c=2)

        made, beta_in, causal_made = ph.sem("made"), ph.sem("beta_in"), ph.sem("causal_made")
        with nc.Block() as block:
            @block.sync
            def _(sp):
                sp.dma_start(beta[:], d["beta"]).then_inc(beta_in, 16)

            @block.scalar
            def _(act):
                act.wait_ge(beta_in, 16)
                nc.scalar.activation(beta[:], beta[:], ACT.Sigmoid).then_inc(beta_in, 1)
                act.wait_ge(beta_in, 17)
                nc.scalar.activation(rest[:], beta[:], ACT.Copy, scale=-1.0, bias=1.0)

            @block.vector
            def _(dve):
                nc.vector.memset(memory[:], 0.0)
                nc.vector.memset(blocks[:], 0.0).then_inc(made, 1)
                dve.wait_ge(made, 1)
                for g in range(HC):
                    nc.vector.memset(blocks[g * DK:(g + 1) * DK, g * DK:(g + 1) * DK], 1.0)
                    nc.vector.memset(blocks[g * DK:(g + 1) * DK, P + g:P + g + 1], 1.0)
                nc.vector.memset(store[:, 8192:12288], 0.0)
                nc.vector.memset(vd[:], 1.0)

            @block.gpsimd
            def _(pool):
                nc.gpsimd.memset(store[:, 12288:14336], 0.0).then_inc(causal_made, 1)
                nc.gpsimd.memset(causal[:], 0.0).then_inc(causal_made, 1)
                for s in range(2):
                    pool.wait_ge(causal_made, 2 + s)
                    half = causal[s * SEG:(s + 1) * SEG]
                    nc.gpsimd.affine_select(out=half, in_=half, compare_op=ALU.is_ge, fill=NEG, base=0,
                                            pattern=[[-1, SEG]], channel_multiplier=1).then_inc(causal_made, 1)

        names = ("stats_done mv_ready var_ready rstd_ready xn_ready xnT_psum xh_ready xl_ready q_psum q_expo q_relu "
                 "q_read k_psum k_expo k_relu k_read v_psum v_ready sq_ready sk_ready skT_psum sk_kept readout "
                 "den_ready rden_ready beta_ready vprev_ready vd_ready fm_ready u_psum masked m_ready scores biased "
                 "top_ready shifted e_ready pair_ready total_ready inv_ready invr_ready pT_psum pT_ready pv mixed_ready "
                 "a_ready aT_psum ah_ready al_ready y_psum x_added").split()
        (stats_done, mv_ready, var_ready, rstd_ready, xn_ready, xnT_psum, xh_ready, xl_ready, q_psum, q_expo, q_relu,
         q_read, k_psum, k_expo, k_relu, k_read, v_psum, v_ready, sq_ready, sk_ready, skT_psum, sk_kept, readout,
         den_ready, rden_ready, beta_ready, vprev_ready, vd_ready, fm_ready, u_psum, masked, m_ready, scores, biased,
         top_ready, shifted, e_ready, pair_ready, total_ready, inv_ready, invr_ready, pT_psum, pT_ready, pv, mixed_ready,
         a_ready, aT_psum, ah_ready, al_ready, y_psum, x_added) = (ph.sem(n) for n in names)
        block = ctx.enter_context(nc.Block())
        rows = [slice(0, SEG), slice(SEG, P)]

        def heads(ap):
            return ap.rearrange("t (n k) -> t n k", k=DK)

        @block.gpsimd
        def _(pool):
            def layernorm_scale(h, p):
                reached(pool, mv_ready, h, p)
                freed(pool, xn_ready, h, p)
                nc.gpsimd.tensor_tensor(rs[:, p, 0:1], mv[:, p, 1:2], eps[:], ALU.add).then_inc(var_ready, 1)
                reached(pool, var_ready, h, p)
                nc.gpsimd.tensor_tensor(rs[:, p, 1:2], rs[:, p, 0:1], minus_half[:, 0:1], ALU.pow).then_inc(rstd_ready, 1)

            def remember(s):
                def stage(h, p):
                    reached(pool, masked, h, p, s + 1, 2)
                    nc.gpsimd.tensor_tensor(memory[:, p], memory[:, p], update[:, s], ALU.add).then_inc(m_ready, 1)
                return stage

            run_stages(pool, [(3, remember(0)), (0, layernorm_scale), (3, remember(1))])

        @block.vector
        def _(dve):
            def statistics(h, p):
                nc.vector.bn_stats(stats[:, p, :], x[:, p, h, :]).then_inc(stats_done, 1)
                reached(dve, stats_done, h, p)
                freed(dve, var_ready, h, p)
                carry_wait(nc, dve, consts)
                nc.vector.bn_aggr(mv[:, p, :], stats[:, p, :]).then_inc(mv_ready, 1)

            def normalise(h, p):
                reached(dve, rstd_ready, h, p)
                freed(dve, xnT_psum, h, p)
                nc.vector.tensor_scalar(xn[:, p, :], x[:, p, h, :], mv[:, p, 0:1], rs[:, p, 1:2],
                                        ALU.subtract, ALU.mult).then_inc(xn_ready, 1)

            def low_xn(h, p):
                reached(dve, xh_ready, h, p)
                freed(dve, v_psum, h, p)
                flat = "p c t -> p (c t)"
                nc.vector.tensor_tensor(xl[:, p].rearrange(flat), psT, xh[:, p].rearrange(flat),
                                        ALU.subtract).then_inc(xl_ready, 1)

            def low_a(h, p):
                reached(dve, ah_ready, h, p)
                freed(dve, y_psum, h, p)
                flat = "p c t -> p (c t)"
                nc.vector.tensor_tensor(al[:, p].rearrange(flat), psT, ah[:, p].rearrange(flat),
                                        ALU.subtract).then_inc(al_ready, 1)

            def sigma_q(h, p):
                reached(dve, q_relu, h, p)
                freed(dve, readout, h, p, 2, 2)
                for s in range(2):
                    nc.vector.scalar_tensor_tensor(out=skq[:, p, :, 3 * s], in0=expo[:, 0, :, s], scalar=1.0,
                                                   in1=relu[:, 0, :, s], op0=ALU.min, op1=ALU.add).then_inc(sq_ready, 1)

            def sigma_k(h, p):
                reached(dve, k_relu, h, p)
                freed(dve, skT_psum, h, p)
                nc.vector.scalar_tensor_tensor(out=skq[:, p, :, 1:3], in0=expo[:, 1], scalar=1.0, in1=relu[:, 1],
                                               op0=ALU.min, op1=ALU.add).then_inc(sk_ready, 1)

            def read_memory(s):
                def stage(h, p):
                    here, k_rows, q_rows = rows[s], rows[1 - s], rows[s]
                    reached(dve, readout, h, p, s + 1, 2)
                    flat_den = den[:, s].rearrange("p (b c n) -> p b c n", b=2, c=2)
                    nc.vector.tensor_scalar(flat_den, psM[:, :, :, P:CW], 1e-6, None, ALU.add).then_inc(den_ready, 1)
                    reached(dve, den_ready, h, p, s + 1, 2)
                    nc.vector.reciprocal(rden[:, s], den[:, s]).then_inc(rden_ready, 1)
                    reached(dve, rden_ready, h, p, s + 1, 2)
                    for b in range(2):
                        cols = slice(b * 8 * DK, (b + 1) * 8 * DK)
                        nc.vector.tensor_tensor(
                            v_prev[here, cols].rearrange("t (c n k) -> t c n k", c=2, k=DK),
                            psM[k_rows, b, :, 0:P].rearrange("t c (n k) -> t c n k", k=DK),
                            rden[k_rows, s, b * 8:b * 8 + 8].rearrange("t (c n) -> t c n", c=2).unsqueeze(3)
                            .to_broadcast([SEG, 2, HC, DK]), ALU.mult).then_inc(vprev_ready, 1)
                    reached(dve, vprev_ready, h, p, 2 * s + 2, 4)
                    reached(dve, v_ready, h, p)
                    nc.vector.tensor_tensor(vd[here, p, :, 0:P], v[here, p].rearrange("t (c n) -> t c n", c=DC),
                                            v_prev[here].rearrange("t (c n) -> t c n", c=DC),
                                            ALU.subtract).then_inc(vd_ready, 1)
                    nc.vector.tensor_tensor(rden_b[q_rows, s], rden[q_rows, s], beta[q_rows], ALU.mult).then_inc(beta_ready, 1)
                    reached(dve, beta_ready, h, p, s + 1, 2)
                    freed(dve, a_ready, h, p)
                    for b in range(2):
                        cols = slice(b * 8 * DK, (b + 1) * 8 * DK)
                        nc.vector.tensor_tensor(
                            from_memory[here, p, cols].rearrange("t (c n k) -> t c n k", c=2, k=DK),
                            psM[q_rows, b, :, 0:P].rearrange("t c (n k) -> t c n k", k=DK),
                            rden_b[q_rows, s, b * 8:b * 8 + 8].rearrange("t (c n) -> t c n", c=2).unsqueeze(3)
                            .to_broadcast([SEG, 2, HC, DK]), ALU.mult).then_inc(fm_ready, 1)
                return stage

            def mask_update(s):
                def stage(h, p):
                    reached(dve, u_psum, h, p, s + 1, 2)
                    freed(dve, m_ready, h, p, s + 1, 2, back=1)
                    nc.vector.tensor_tensor(update[:, s].rearrange("p (b c) n -> p b c n", b=2), psM,
                                            blocks[:].unsqueeze(1).unsqueeze(1).to_broadcast([P, 2, 2, CW]),
                                            ALU.mult).then_inc(masked, 1)
                return stage

            def shift(h, p):
                reached(dve, scores, h, p)
                freed(dve, total_ready, h, p)
                freed(dve, pT_psum, h, p, 2, 2)
                nc.vector.tensor_tensor(score[:, p], psS.rearrange("t (n k) -> t n k", n=H),
                                        causal[:].unsqueeze(1).to_broadcast([P, H, SEG]), ALU.add).then_inc(biased, 1)
                reached(dve, biased, h, p)
                freed(dve, shifted, h, p)
                nc.vector.tensor_reduce(top[:, p], score[:, p], AX_X, ALU.max).then_inc(top_ready, 1)
                reached(dve, top_ready, h, p)
                nc.vector.tensor_tensor(score[:, p], score[:, p], top[:, p].unsqueeze(2).to_broadcast([P, H, SEG]),
                                        ALU.subtract).then_inc(shifted, 1)

            def combine(h, p):
                reached(dve, e_ready, h, p)
                nc.vector.tensor_reduce(total[:, p], score[:, p], AX_X, ALU.add).then_inc(total_ready, 1)
                reached(dve, total_ready, h, p)
                nc.vector.reciprocal(inv[:, p], total[:, p]).then_inc(inv_ready, 1)
                reached(dve, inv_ready, h, p)
                nc.vector.tensor_tensor(inv_r[:, p], inv[:, p], rest[:], ALU.mult).then_inc(invr_ready, 1)
                reached(dve, invr_ready, h, p)
                reached(dve, pv, h, p)
                freed(dve, a_ready, h, p, back=1)
                nc.vector.tensor_tensor(heads(mixed[:]), heads(psP), inv_r[:, p].unsqueeze(2).to_broadcast([P, H, DK]),
                                        ALU.mult).then_inc(mixed_ready, 1)
                reached(dve, mixed_ready, h, p)
                reached(dve, fm_ready, h, p, 4, 4)
                freed(dve, aT_psum, h, p)
                nc.vector.tensor_tensor(a[:, p], mixed[:], from_memory[:, p], ALU.add).then_inc(a_ready, 1)

            def residual(h, p):
                reached(dve, y_psum, h, p)
                nc.vector.tensor_tensor(x[:, p, h, :], psB, x[:, p, h, :], ALU.add).then_inc(x_added, 1)

            run_stages(dve, [(3, read_memory(0)), (5, low_a), (3, mask_update(0)), (1, low_xn), (4, shift),
                             (3, read_memory(1)), (2, sigma_q), (5, residual), (0, statistics), (3, mask_update(1)),
                             (2, sigma_k), (0, normalise), (4, combine)])

        @block.scalar
        def _(act):
            flat = "p c t -> p (c t)"
            halves = "p (c s t) -> p c s t"

            def high_xn(h, p):
                reached(act, xnT_psum, h, p)
                freed(act, v_psum, h, p)
                nc.scalar.copy(xh[:, p].rearrange(flat), psT).then_inc(xh_ready, 1)

            def high_a(h, p):
                reached(act, aT_psum, h, p)
                freed(act, y_psum, h, p)
                nc.scalar.copy(ah[:, p].rearrange(flat), psT).then_inc(ah_ready, 1)

            def keep_sk(h, p):
                reached(act, skT_psum, h, p)
                freed(act, u_psum, h, p, 2, 2)
                nc.scalar.copy(sk[:, p], psT).then_inc(sk_kept, 1)

            def keep_pT(h, p):
                for g in range(2):
                    reached(act, pT_psum, h, p, g + 1, 2)
                    nc.scalar.copy(pT[:, g].rearrange(flat), psS[:, g * 512:(g + 1) * 512]).then_inc(pT_ready, 1)

            def keep_q(h, p):
                reached(act, q_psum, h, p)
                freed(act, sq_ready, h, p, 2, 2, back=1)
                view = psA.rearrange(halves, c=DC, s=2)
                nc.scalar.activation(expo[:, 0], view, ACT.Exp).then_inc(q_expo, 1)
                nc.scalar.activation(relu[:, 0], view, ACT.Relu).then_inc(q_relu, 1)
                freed(act, scores, h, p)
                nc.scalar.activation(qT[:, p].rearrange(flat), psA, ACT.Copy, scale=float(DK) ** -0.5).then_inc(q_read, 1)

            def keep_k(h, p):
                reached(act, k_psum, h, p)
                freed(act, sk_ready, h, p, back=1)
                view = psB.rearrange(halves, c=DC, s=2)
                nc.scalar.activation(expo[:, 1], view, ACT.Exp).then_inc(k_expo, 1)
                nc.scalar.activation(relu[:, 1], view, ACT.Relu).then_inc(k_relu, 1)
                freed(act, scores, h, p)
                for g in range(HC):
                    r = slice(g * DK, (g + 1) * DK)
                    nc.scalar.copy(kdiag[r, p, :, :, g], psB[r].rearrange(halves, c=DC, s=2)).then_inc(k_read, 1)

            def keep_v(h, p):
                reached(act, v_psum, h, p)
                freed(act, pv, h, p)
                freed(act, vd_ready, h, p, 2, 2)
                for s in range(2):
                    for n in range(2):
                        nc.scalar.copy(vpair[n * SEG:(n + 1) * SEG, p, s, :, n * DK:(n + 1) * DK],
                                       psA[rows[s]].rearrange("t (j n k) -> t n j k", n=2, k=DK)[:, n]).then_inc(pair_ready, 1)
                nc.scalar.copy(v[:, p], psA).then_inc(v_ready, 1)

            def exponentials(h, p):
                reached(act, shifted, h, p)
                nc.scalar.activation(score[:, p], score[:, p], ACT.Exp).then_inc(e_ready, 1)

            run_stages(act, [(3, keep_sk), (5, high_a), (2, keep_q), (1, high_xn), (2, keep_k), (4, exponentials),
                             (4, keep_pT), (2, keep_v)])

        @block.tensor
        def _(pe):
            def turn_a(h, p):
                reached(pe, a_ready, h, p)
                freed(pe, sk_kept, h, p, back=-2)
                freed(pe, al_ready, h, p, back=1)
                for c in range(DC):
                    mm = nc.tensor.transpose(psT[:, c * P:(c + 1) * P], a[:, p, c * P:(c + 1) * P], ident[:])
                mm.then_inc(aT_psum, 1)

            def turn_xn(h, p):
                reached(pe, xn_ready, h, p)
                freed(pe, al_ready, h, p, back=4)
                freed(pe, sk_kept, h, p, back=2)
                freed(pe, xl_ready, h, p, back=1)
                for c in range(DC):
                    mm = nc.tensor.transpose(psT[:, c * P:(c + 1) * P], xn[:, p, c * P:(c + 1) * P], ident[:])
                mm.then_inc(xnT_psum, 1)

            def turn_sk(h, p):
                reached(pe, sk_ready, h, p)
                freed(pe, xl_ready, h, p, back=-1)
                freed(pe, al_ready, h, p, back=3)
                freed(pe, sk_kept, h, p, back=1)
                for c in range(DC):
                    mm = nc.tensor.transpose(psT[:, c * P:(c + 1) * P], skq[:, p, c, 1:3], ident[:])
                mm.then_inc(skT_psum, 1)

            def read_memory(s):
                def stage(h, p):
                    reached(pe, sq_ready, h, p, 2, 2)
                    if s == 0:
                        freed(pe, m_ready, h, p, 2, 2)
                        freed(pe, masked, h, p, 2, 2, back=1)
                    else:
                        reached(pe, m_ready, h, p, 1, 2)
                    for c in range(DC):
                        mm = nc.tensor.matmul(psM[:, c // 2, c % 2], skq[:, p, c, 2 * s:2 * s + 2], memory[:, p, c],
                                              start=True, stop=True)
                    mm.then_inc(readout, 1)
                return stage

            def sum_update(s):
                def stage(h, p):
                    r = rows[s]
                    reached(pe, sk_kept, h, p)
                    reached(pe, vd_ready, h, p, s + 1, 2)
                    reached(pe, fm_ready, h, p, 2 * s + 2, 4)
                    for c in range(DC):
                        mm = nc.tensor.matmul(psM[:, c // 2, c % 2], sk[r, p, c * P:(c + 1) * P], vd[r, p, c],
                                              start=True, stop=True)
                    mm.then_inc(u_psum, 1)
                return stage

            def out_projection(h, p):
                reached(pe, al_ready, h, p)
                freed(pe, k_read, h, p, 4, 4, back=-3)
                passes = [(ah, wh), (al, wh), (ah, wl)]
                for n, (s, w) in enumerate(passes):
                    for c in range(DC):
                        mm = nc.tensor.matmul(psB, s[:, p, c, :], w[:, WO, c, :], start=n + c == 0,
                                              stop=n == 2 and c == DC - 1)
                mm.then_inc(y_psum, 1)

            def turned_projection(bank, weight, h, p):
                for j in range(DC):
                    for n, (w, s) in enumerate([(wh, xh), (wh, xl), (wl, xh)]):
                        for c in range(DC):
                            mm = nc.tensor.matmul(bank[:, j * P:(j + 1) * P], w[:, weight, c, j * P:(j + 1) * P],
                                                  s[:, p, c, :], start=n + c == 0, stop=n == 2 and c == DC - 1)
                return mm

            def queries(h, p):
                reached(pe, xl_ready, h, p)
                freed(pe, v_ready, h, p, back=1)
                turned_projection(psA, WQ, h, p).then_inc(q_psum, 1)

            def keys(h, p):
                freed(pe, x_added, h, p, back=4)
                freed(pe, k_read, h, p, 4, 4, back=1)
                turned_projection(psB, WK, h, p).then_inc(k_psum, 1)

            def values(h, p):
                reached(pe, q_read, h, p)
                for n, (s, w) in enumerate([(xh, wh), (xl, wh), (xh, wl)]):
                    for c in range(DC):
                        mm = nc.tensor.matmul(psA, s[:, p, c, :], w[:, WV, c, :], start=n + c == 0,
                                              stop=n == 2 and c == DC - 1)
                mm.then_inc(v_psum, 1)

            def local_scores(h, p):
                reached(pe, k_read, h, p, 4, 4)
                freed(pe, pT_ready, h, p, 2, 2, back=1)
                for s in range(2):
                    for c in range(DC):
                        mm = nc.tensor.matmul(psS[rows[s], c * HC * SEG:(c + 1) * HC * SEG], qT[:, p, c, rows[s]],
                                              kdiag[:, p, c, s], start=True, stop=True)
                mm.then_inc(scores, 1)

            def turn_probs(h, p):
                reached(pe, e_ready, h, p)
                pairs = score[:, p].rearrange("t (j n) k -> t j (n k)", n=2)
                for g in range(2):
                    for n in range(4):
                        mm = nc.tensor.transpose(psS[:, (4 * g + n) * P:(4 * g + n + 1) * P], pairs[:, 4 * g + n], ident[:])
                    mm.then_inc(pT_psum, 1)

            def attend(h, p):
                reached(pe, pair_ready, h, p, 4, 4)
                freed(pe, mixed_ready, h, p, back=1)
                for g in range(2):
                    reached(pe, pT_ready, h, p, g + 1, 2)
                    for j in range(4 * g, 4 * g + 4):
                        for s in range(2):
                            mm = nc.tensor.matmul(psP[rows[s], j * 2 * DK:(j + 1) * 2 * DK], pT[:, g, j % 4, rows[s]],
                                                  vpair[:, p, s, j], start=True, stop=True)
                mm.then_inc(pv, 1)

            run_stages(pe, [(3, turn_sk), (3, read_memory(0)), (5, turn_a), (2, queries), (3, sum_update(0)),
                            (1, turn_xn), (2, keys), (3, read_memory(1)), (2, values), (5, out_projection),
                            (4, turn_probs), (3, sum_update(1)), (4, attend), (3, local_scores)])



NEAR, FAR = range(2)


def l1_cross_attention(nc, d, x, raw, raw_in, ident, ones, minus_half, eps, consts):
    with ExitStack() as ctx:
        ph = Phase(nc, ctx, "x1")
        w0, w3 = raw[:, 0], raw[:, 1]
        w03_in = ph.sem("w03_in")
        ctx_rows = ph.sb("ctx_rows", [K, B, D])
        gh = ph.sb("gh", [P, B, DC, K], BF16)
        gl = ph.sb("gl", [P, B, DC, K], BF16)
        crow = ph.sb("crow", [P, B, K])
        cw1 = ph.sb("cw1", [K, B, D])
        w2h = ph.sb("w2h", [P, DC, D], BF16)
        w2l = ph.sb("w2l", [P, DC, D], BF16)
        bias = ph.sb("bias", [P, D])
        ps = ph.banks()
        w_in = ph.sem("w_in")
        c_in = ph.sem("c_in")

        xn = ph.sb("xn", [P, TB // 2, 2, D])
        xh = ph.sb("xh", [P, TB // 2, 2, DC, P], BF16)
        xl = ph.sb("xl", [P, TB // 2, 2, DC, P], BF16)
        wch = ph.sb("wch", [P, DC, D], BF16)
        wcl = ph.sb("wcl", [P, DC, D], BF16)
        expo = ph.sb("expo", [P, B, TB // 2, 2, K])
        ntop = ph.sb("ntop", [P, B, TB // 2, 2])
        total = ph.sb("total", [P, B, TB // 2, 2])
        inv = ph.sb("inv", [P, B, TB // 2, 2])
        raws = ExitStack()
        raw_ph = Phase(nc, raws, "x1raw")
        w1 = raw_ph.sb("w1", [P, DC, D])
        w2 = raw_ph.sb("w2", [P, DC, D])
        ctxT = raw_ph.sb("ctxT", [P, DC, B * K])
        with ExitStack() as ctx2:
            ph2 = Phase(nc, ctx2, "x1s")
            wsim = ph2.sb("wsim", [P, 3, DC])
            bsim = ph2.sb("bsim", [P, 1])
            w2sim = ph2.sb("w2sim", [P, DC, P])
            g = ph2.sb("g", [P, B, DC, K])
            g_ready, gh_ready, wide_ready, c_psum = (ph2.sem(n) for n in "g_ready gh_ready wide_ready c_psum".split())
            with nc.Block() as block:
                @block.sync
                def _(sp):
                    sp.dma_start(ctxT[:], d["ctxT"]).then_inc(c_in, 16)
                    sp.dma_start(wsim[:], d["w_sim"]).then_inc(c_in, 16)
                    sp.dma_start(bsim[:], d["b_sim"]).then_inc(c_in, 16)
                    sp.dma_start(w1[:], d["w_x1_1"]).then_inc(w_in, 16)
                    sp.dma_start(w2[:], d["w_x1_2"]).then_inc(w_in, 16)
                    sp.dma_start(w0, d["w_x1_0"]).then_inc(w03_in, 16)
                    sp.dma_start(w3, d["w_x1_3"]).then_inc(w03_in, 16)
                    sp.dma_start(ctx_rows[:], d["ctx_rows"]).then_inc(w_in, 16)
                    sp.dma_start(bias[:], d["b_x1"]).then_inc(w_in, 16)

                @block.vector
                def _(dve):
                    dve.wait_ge(c_in, 48)
                    for c in range(DC):
                        nc.vector.tensor_scalar(w2sim[:, c], ones[:], wsim[:, 1, c:c + 1], None, ALU.mult).then_inc(wide_ready, 1)
                        nc.vector.tensor_scalar(g[:, :, c], ctxT[:, c].rearrange("p (b k) -> p b k", b=B), wsim[:, 2, c:c + 1],
                                                wsim[:, 0, c:c + 1], ALU.mult, ALU.add).then_inc(g_ready, 1)
                    dve.wait_ge(gh_ready, 1)
                    nc.vector.tensor_tensor(gl[:], g[:], gh[:], ALU.subtract)
                    dve.wait_ge(c_psum, 1)
                    nc.vector.tensor_scalar(crow[:].rearrange("p b k -> p (b k)"), ps[:, 0, 0:B * K], bsim[:], None, ALU.add)

                @block.scalar
                def _(act):
                    act.wait_ge(g_ready, DC)
                    nc.scalar.copy(gh[:], g[:]).then_inc(gh_ready, 1)

                @block.tensor
                def _(pe):
                    pe.wait_ge(wide_ready, DC)
                    for c in range(DC):
                        mm = nc.tensor.matmul(ps[:, 0, 0:B * K], w2sim[:, c], ctxT[:, c], start=c == 0, stop=c == DC - 1)
                    mm.then_inc(c_psum, 1)

        flat = "p c t -> p (c t)"
        psT, psS, psP, psH, psC = ps[:, 0], ps[:, 1, 0:K], ps[0:K, 2, 0:P], ps[:, 3], ps[:, 6, 0:DC]
        psD = ps[:, 7, 0:DC]
        psY = lambda p: ps[:, 4 + p]

        def run(near, far):
            with ExitStack() as ctx3:
                q = Phase(nc, ctx3, f"x1{near}{far}")
                names = ("stats_done mv_ready var_ready rstd_ready xc_ready xnT_psum xh_ready xl_ready sim_psum sim_ready "
                         "top_ready exp_ready inv_ready probs_ready pT_psum pT_ready xf_ready hq_psum z_ready zh_ready "
                         "zl_ready b_added y_psum x_added xn_kept").split()
                (stats_done, mv_ready, var_ready, rstd_ready, xc_ready, xnT_psum, xh_ready, xl_ready, sim_psum, sim_ready,
                 top_ready, exp_ready, inv_ready, probs_ready, pT_psum, pT_ready, xf_ready, hq_psum, z_ready, zh_ready,
                 zl_ready, b_added, y_psum, x_added, xn_kept) = (q.sem(n) for n in names)
                if near is not None:
                    stats = q.sb("stats", [P, 2, 6])
                    mv = q.sb("mv", [P, 2, 2])
                    rs = q.sb("rs", [P, 2, 2])
                    xc = q.sb("xc", [P, 2, D])
                    sim = q.sb("sim", [P, 2, K])
                if far is not None:
                    probs = q.sb("probs", [P, 2, K])
                    pT = q.sb("pT", [K, 2, P])
                    xf = q.sb("xf", [P, 2, D])
                    z = q.sb("z", [P, 2, D])
                    zh = q.sb("zh", [P, 2, DC, P], BF16)
                    zl = q.sb("zl", [P, 2, DC, P], BF16)
                block = ctx3.enter_context(nc.Block())
                tiles = x[:].rearrange("t b (h p) n -> t b h p n", p=2)
                a, b = near, far

                def stages(eng, order):
                    behind = 3 if near is not None and far is not None else 0
                    run_stages(eng, [(lag + (behind if side == NEAR else 0), stage) for side, lag, stage in order
                                     if (near if side == NEAR else far) is not None], TB)

                def before(eng, sem, h, p, k=1, per=1, back=2):
                    freed(eng, sem, h, p, k, per, back, TB)

                if near is None:
                    @block.sync
                    def _(sp):
                        for n, name in enumerate(("w_f1a", "w_f1n")):
                            sp.dma_start(raw[:, n], d[name]).then_inc(raw_in[n], 16)

                @block.gpsimd
                def _(pool):
                    def layernorm_scale(h, p):
                        reached(pool, mv_ready, h, p)
                        before(pool, xc_ready, h, p)
                        nc.gpsimd.tensor_tensor(rs[:, p, 0:1], mv[:, p, 1:2], eps[:], ALU.add).then_inc(var_ready, 1)
                        reached(pool, var_ready, h, p)
                        nc.gpsimd.tensor_tensor(rs[:, p, 1:2], rs[:, p, 0:1], minus_half[:, 0:1],
                                                ALU.pow).then_inc(rstd_ready, 1)

                    def whole_xn(h, p):
                        before(pool, z_ready, h, p)
                        nc.gpsimd.tensor_tensor(xf[:, p], xh[:, h, p].rearrange(flat), xl[:, h, p].rearrange(flat),
                                                ALU.add).then_inc(xf_ready, 1)

                    def add_bias(h, p):
                        nc.gpsimd.tensor_tensor(tiles[:, b, h, p], tiles[:, b, h, p], bias[:], ALU.add).then_inc(b_added, 1)

                    stages(pool, [(NEAR, 0, layernorm_scale), (FAR, 2, whole_xn), (FAR, 2, add_bias)])

                @block.vector
                def _(dve):
                    def statistics(h, p):
                        nc.vector.bn_stats(stats[:, p, :], tiles[:, a, h, p]).then_inc(stats_done, 1)
                        reached(dve, stats_done, h, p)
                        before(dve, var_ready, h, p)
                        carry_wait(nc, dve, consts)
                        nc.vector.bn_aggr(mv[:, p, :], stats[:, p, :]).then_inc(mv_ready, 1)

                    def normalise(h, p):
                        reached(dve, rstd_ready, h, p)
                        before(dve, xnT_psum, h, p)
                        before(dve, xn_kept, h, p)
                        nc.vector.tensor_scalar(xc[:, p], tiles[:, a, h, p], mv[:, p, 0:1], rs[:, p, 1:2],
                                                ALU.subtract, ALU.mult).then_inc(xc_ready, 1)

                    def low_xn(h, p):
                        reached(dve, xh_ready, h, p)
                        if far is not None:
                            reached(dve, y_psum, h, p)
                        nc.vector.tensor_tensor(xl[:, h, p].rearrange(flat), psT, xh[:, h, p].rearrange(flat),
                                                ALU.subtract).then_inc(xl_ready, 1)

                    def tops(h, p):
                        reached(dve, sim_psum, h, p)
                        before(dve, exp_ready, h, p)
                        nc.vector.tensor_tensor(sim[:, p], psS, crow[:, a], ALU.add).then_inc(sim_ready, 1)
                        reached(dve, sim_ready, h, p)
                        nc.vector.tensor_reduce(ntop[:, a, h, p:p + 1], sim[:, p], AX_X, ALU.max,
                                                negate=True).then_inc(top_ready, 1)

                    def divide(h, p):
                        nc.vector.reciprocal(inv[:, b, h, p:p + 1], total[:, b, h, p:p + 1]).then_inc(inv_ready, 1)
                        reached(dve, inv_ready, h, p)
                        before(dve, pT_psum, h, p)
                        nc.vector.tensor_scalar(probs[:, p], expo[:, b, h, p], inv[:, b, h, p:p + 1], None,
                                                ALU.mult).then_inc(probs_ready, 1)

                    def product(h, p):
                        reached(dve, hq_psum, h, p)
                        reached(dve, xf_ready, h, p)
                        before(dve, zl_ready, h, p)
                        nc.vector.tensor_tensor(z[:, p], psH, xf[:, p], ALU.mult).then_inc(z_ready, 1)

                    def low_z(h, p):
                        reached(dve, zh_ready, h, p)
                        before(dve, y_psum, h, p)
                        nc.vector.tensor_tensor(zl[:, p].rearrange(flat), z[:, p], zh[:, p].rearrange(flat),
                                                ALU.subtract).then_inc(zl_ready, 1)

                    def residual(h, p):
                        reached(dve, y_psum, h, p)
                        reached(dve, b_added, h, p)
                        nc.vector.tensor_tensor(tiles[:, b, h, p], psY(p), tiles[:, b, h, p], ALU.add).then_inc(x_added, 1)

                    stages(dve, [(NEAR, 0, statistics), (NEAR, 1, low_xn), (FAR, 0, divide), (NEAR, 0, normalise),
                                 (FAR, 3, residual), (FAR, 2, product), (NEAR, 2, tops), (FAR, 2, low_z)])

                @block.scalar
                def _(act):
                    def high_xn(h, p):
                        reached(act, xnT_psum, h, p)
                        if far is not None:
                            reached(act, y_psum, h, p)
                        nc.scalar.copy(xh[:, h, p].rearrange(flat), psT).then_inc(xh_ready, 1)

                    def keep_xn(h, p):
                        reached(act, xc_ready, h, p)
                        nc.scalar.copy(xn[:, h, p], xc[:, p]).then_inc(xn_kept, 1)

                    def exponentials(h, p):
                        reached(act, top_ready, h, p)
                        nc.scalar.activation(expo[:, a, h, p], sim[:, p], ACT.Exp, bias=ntop[:, a, h, p:p + 1],
                                             accum_out=total[:, a, h, p:p + 1]).then_inc(exp_ready, 1)

                    def keep_pT(h, p):
                        reached(act, pT_psum, h, p)
                        before(act, y_psum, h, p)
                        nc.scalar.copy(pT[:, p], psP).then_inc(pT_ready, 1)

                    def high_z(h, p):
                        reached(act, z_ready, h, p)
                        before(act, y_psum, h, p)
                        nc.scalar.copy(zh[:, p].rearrange(flat), z[:, p]).then_inc(zh_ready, 1)

                    stages(act, [(NEAR, 1, high_xn), (NEAR, 0, keep_xn), (FAR, 1, keep_pT), (FAR, 2, high_z),
                                 (NEAR, 2, exponentials)])

                @block.tensor
                def _(pe):
                    def turn_xn(h, p):
                        reached(pe, xc_ready, h, p)
                        before(pe, xl_ready, h, p, back=1)
                        for c in range(DC):
                            mm = nc.tensor.transpose(psT[:, c * P:(c + 1) * P], xc[:, p, c * P:(c + 1) * P], ident[:])
                        mm.then_inc(xnT_psum, 1)

                    def similarity(h, p):
                        reached(pe, xl_ready, h, p)
                        before(pe, sim_ready, h, p, back=1)
                        for n, (s, w) in enumerate([(xh, gh), (xl, gh), (xh, gl)]):
                            for c in range(DC):
                                mm = nc.tensor.matmul(psS, s[:, h, p, c], w[:, a, c], start=n + c == 0,
                                                      stop=n == 2 and c == DC - 1)
                        mm.then_inc(sim_psum, 1)

                    def turn_probs(h, p):
                        reached(pe, probs_ready, h, p)
                        before(pe, pT_ready, h, p, back=1)
                        nc.tensor.transpose(psP, probs[:, p], ident[:]).then_inc(pT_psum, 1)

                    def context_means(h, p):
                        reached(pe, pT_ready, h, p)
                        before(pe, z_ready, h, p, back=1)
                        for c in range(DC):
                            mm = nc.tensor.matmul(psH[:, c * P:(c + 1) * P], ctx_rows[:, b, c * P:(c + 1) * P], pT[:, p],
                                                  start=True, stop=True)
                        mm.then_inc(hq_psum, 1)

                    def project(h, p):
                        before(pe, x_added, h, p)
                        for n, (s, w) in enumerate([(xh, wch), (xl, wch), (xh, wcl)]):
                            for c in range(DC):
                                nc.tensor.matmul(psY(p), s[:, h, p, c], w[:, c], start=n + c == 0, stop=False)
                        nc.tensor.matmul(psY(p), pT[:, p], cw1[:, b], start=False, stop=False)
                        reached(pe, zl_ready, h, p)
                        for n, (s, w) in enumerate([(zh, w2h), (zl, w2h), (zh, w2l)]):
                            for c in range(DC):
                                mm = nc.tensor.matmul(psY(p), s[:, p, c], w[:, c], start=False,
                                                      stop=n == 2 and c == DC - 1)
                        mm.then_inc(y_psum, 1)

                    stages(pe, [(NEAR, 1, turn_xn), (FAR, 3, project), (FAR, 2, context_means), (FAR, 1, turn_probs),
                                (NEAR, 2, similarity)])

        def context_mean(b):
            with ExitStack() as ctx3:
                q = Phase(nc, ctx3, f"x1hc{b}")
                col = q.sb("col", [P, 8])
                weights = q.sb("weights", [P, TB // 2, 2])
                hc = q.sb("hc", [P, DC])
                hc_half = q.sb("hc_half", [P, DC])
                wc = q.sb("wc", [P, 2, D])
                (top_ready, tops_ready, ntop_ready, w_ready, sum_ready, inv_ready, hc_psum, hc_ready, wc_ready,
                 wch_ready, wcl_ready, cw_psum, w2h_ready, acc_ready) = (
                    q.sem(n) for n in ("top_ready tops_ready ntop_ready w_ready sum_ready inv_ready hc_psum hc_ready "
                                       "wc_ready wch_ready wcl_ready cw_psum w2h_ready acc_ready").split())
                with nc.Block() as block:
                    @block.gpsimd
                    def _(pool):
                        pool.wait_ge(top_ready, 1)
                        nc.gpsimd.partition_all_reduce(col[:, 1:2], col[:, 0:1], P, bass.bass_isa.ReduceOp.max).then_inc(tops_ready, 1)
                        pool.wait_ge(w_ready, 1)
                        nc.gpsimd.partition_all_reduce(col[:, 4:5], col[:, 3:4], P, bass.bass_isa.ReduceOp.add).then_inc(sum_ready, 1)

                    @block.vector
                    def _(dve):
                        nc.vector.tensor_reduce(col[:, 0:1], ntop[:, b].rearrange("t h p -> t (h p)"), AX_X, ALU.min,
                                                negate=True).then_inc(top_ready, 1)
                        dve.wait_ge(tops_ready, 1)
                        nc.vector.tensor_scalar(col[:, 2:3], col[:, 1:2], -1.0, None, ALU.mult).then_inc(ntop_ready, 1)
                        acc = wc[:, 0]
                        dve.wait_ge(w_ready, 1)
                        for t in range(TB // 2):
                            weight = weights[:, t // 2, t % 2:t % 2 + 1]
                            if t == 0:
                                nc.vector.tensor_scalar(acc, xn[:, 0, 0], weight, None, ALU.mult).then_inc(acc_ready, 1)
                            else:
                                dve.wait_ge(acc_ready, t)
                                nc.vector.scalar_tensor_tensor(out=acc, in0=xn[:, t // 2, t % 2], scalar=weight, in1=acc,
                                                               op0=ALU.mult, op1=ALU.add).then_inc(acc_ready, 1)
                        if b == 0:
                            dve.wait_ge(w2h_ready, 1)
                            nc.vector.tensor_tensor(w2l[:], w2[:], w2h[:], ALU.subtract)
                        dve.wait_ge(sum_ready, 1)
                        nc.vector.reciprocal(col[:, 5:6], col[:, 4:5]).then_inc(inv_ready, 1)
                        dve.wait_ge(inv_ready, 1)
                        dve.wait_ge(hc_psum, 1)
                        nc.vector.tensor_scalar(hc_half[:], psC, col[:, 5:6], None, ALU.mult).then_inc(hc_ready, 1)
                        dve.wait_ge(hc_ready, 1)
                        nc.vector.scalar_tensor_tensor(out=hc[:], in0=psD, scalar=col[:, 5:6], in1=hc_half[:],
                                                       op0=ALU.mult, op1=ALU.add).then_inc(hc_ready, 1)
                        dve.wait_ge(hc_ready, 2)
                        dve.wait_ge(w03_in, 32)
                        def low(c):
                            dve.wait_ge(wch_ready, c + 1)
                            nc.vector.tensor_tensor(wcl[:, c], wc[:, c % 2], wch[:, c], ALU.subtract).then_inc(wcl_ready, 1)

                        for c in range(DC):
                            if c >= 2:
                                dve.wait_ge(wcl_ready, c - 1)
                            nc.vector.scalar_tensor_tensor(out=wc[:, c % 2], in0=w3[:, c], scalar=hc[:, c:c + 1], in1=w0[:, c],
                                                           op0=ALU.mult, op1=ALU.add).then_inc(wc_ready, 1)
                            if c >= 1:
                                low(c - 1)
                        low(DC - 1)

                    @block.scalar
                    def _(act):
                        act.wait_ge(ntop_ready, 1)
                        nc.scalar.activation(weights[:], ntop[:, b], ACT.Exp, scale=-1.0, bias=col[:, 2:3],
                                             accum_out=col[:, 3:4]).then_inc(w_ready, 1)
                        if b == 0:
                            act.wait_ge(w_in, 64)
                            nc.scalar.copy(w2h[:], w2[:]).then_inc(w2h_ready, 1)
                        for c in range(DC):
                            act.wait_ge(wc_ready, c + 1)
                            nc.scalar.copy(wch[:, c], wc[:, c % 2]).then_inc(wch_ready, 1)
                        if b == 0:
                            for other in range(B):
                                act.wait_ge(cw_psum, other + 1)
                                nc.scalar.copy(cw1[:, other], ps[0:K, 1 + other])

                    @block.tensor
                    def _(pe):
                        pe.wait_ge(w_ready, 1)
                        for c in range(DC):
                            for t in range(TB // 2, TB):
                                nc.tensor.matmul(psC[:, c:c + 1], xn[:, t // 2, t % 2, c * P:(c + 1) * P],
                                                 weights[:, t // 2, t % 2:t % 2 + 1], start=t == TB // 2, stop=t == TB - 1)
                        pe.wait_ge(acc_ready, TB // 2)
                        for c in range(DC):
                            mm = nc.tensor.matmul(psD[:, c:c + 1], wc[:, 0, c * P:(c + 1) * P], ones[:, 0:1],
                                                  start=True, stop=True)
                        mm.then_inc(hc_psum, 1)
                        if b == 0:
                            pe.wait_ge(w_in, 64)
                            for other in range(B):
                                for c in range(DC):
                                    mm = nc.tensor.matmul(ps[0:K, 1 + other], ctxT[:, c, other * K:(other + 1) * K],
                                                          w1[:, c], start=c == 0, stop=c == DC - 1)
                                mm.then_inc(cw_psum, 1)

        with raws:
            run(0, None)
            context_mean(0)
        run(1, 0)
        context_mean(1)
        run(None, 1)



E = 8
UNITS = E * FC
TE = TB // E
RING = 4
LAST_AT = {1: [0], 2: [1], 3: [2, 3]}


def run_experts(eng, unit):
    def expert(e, last):
        for f in range(RING):
            unit(e, f, f)
        with eng.Fori(1, FC // RING - last) as k:
            for r in range(RING):
                unit(e, k * RING + r, r)
        for f in range(FC - RING * last, FC):
            unit(e, f, f % RING)

    expert(0, False)
    expert(1, False)
    with eng.Fori(2, E - 1) as e:
        expert(e, False)
    expert(E - 1, True)


def at_least(eng, sem, value):
    if not (isinstance(value, int) and value <= 0):
        eng.wait_ge(sem, value)


def l1_ffn(nc, d, x, out, proj_raw, proj_in, ident, minus_half, eps, consts):
    flat = "p c t -> p (c t)"
    with ExitStack() as ctx:
        ph = Phase(nc, ctx, "f1")
        xah = ph.sb("xah", [P, DC, TB, B, P], BF16)
        xal = ph.sb("xal", [P, DC, TB, B, P], BF16)
        proj_h = ph.sb("proj_h", [P, 2, DC, D], BF16)
        proj_l = ph.sb("proj_l", [P, 2, DC, D], BF16)
        INNER, LAST = range(2)
        b1 = ph.sb("b1", [P, E, FC])
        b2 = ph.sb("b2", [P, E, DC])
        last_bias = ph.sb("last_bias", [P, D])
        raw = proj_raw[:].rearrange("p w c n -> p (w c n)").rearrange("p (r n) -> p r n", r=RING)
        raw_in = [ph.sem(f"raw_in{r}") for r in range(RING)]
        v_in = ph.sem("v_in")
        split_loaded(nc, ph, proj_raw, proj_in, proj_h, proj_l)

        with ExitStack() as ctx2:
            q = Phase(nc, ctx2, "f1a")
            ln_scale = q.sb("ln_scale", [P, D])
            ln_bias = q.sb("ln_bias", [P, D])
            attn_bias = q.sb("attn_bias", [1, D])
            bias_h = q.sb("bias_h", [1, D], BF16)
            bias_l = q.sb("bias_l", [1, D], BF16)
            ones_row = q.sb("ones_row", [1, P], BF16)
            stats = q.sb("stats", [P, 2, 6])
            mv = q.sb("mv", [P, 2, 2])
            rs = q.sb("rs", [P, 2, 6])
            xL = q.sb("xL", [P, 2, D])
            xL_copy = q.sb("xL_copy", [P, 2, D])
            xs = q.sb("xs", [P, 2, D])
            xh = q.sb("xh", [P, 2, DC, P], BF16)
            xl = q.sb("xl", [P, 2, DC, P], BF16)
            xa = q.sb("xa", [P, 2, D])
            ps = q.banks()
            psT, psA = (lambda p: ps[:, p]), (lambda p: ps[:, 2 + p])
            psY = lambda p: ps[:, 4 + p]
            q_in = q.sem("q_in")
            names = ("stats_done mv_ready rs_own xL_ready xs_scaled xs_ready xL_kept xT_psum xh_ready xl_ready y_psum "
                     "bias_made xa_ready aT_psum ah_ready al_ready").split()
            (stats_done, mv_ready, rs_own, xL_ready, xs_scaled, xs_ready, xL_kept, xT_psum, xh_ready, xl_ready, y_psum,
             bias_made, xa_ready, aT_psum, ah_ready, al_ready) = (q.sem(n) for n in names)
            block = ctx2.enter_context(nc.Block())

            @block.sync
            def _(sp):
                sp.dma_start(ln_scale[:], d["ln_scale"]).then_inc(q_in, 16)
                sp.dma_start(ln_bias[:], d["ln_bias"]).then_inc(q_in, 16)
                sp.dma_start(attn_bias[:], d["b_f1a"][0:1]).then_inc(q_in, 16)
                sp.dma_start(b1[:], d["b_f1_1"]).then_inc(v_in, 16)
                sp.dma_start(b2[:], d["b_f1_2"]).then_inc(v_in, 16)
                sp.dma_start(last_bias[:], d["b_f1n"]).then_inc(v_in, 16)
                for r in range(RING):
                    sp.dma_start(raw[:, r], d["w_f1"][r]).then_inc(raw_in[r], 16)

            @block.gpsimd
            def _(pool):
                tt = nc.gpsimd.tensor_tensor
                pool.wait_ge(q_in, 48)

                def roots(h, p):
                    v = mv[:, p, 1:2]
                    r = [rs[:, p, n:n + 1] for n in range(6)]
                    reached(pool, mv_ready, h, p)
                    freed(pool, xs_scaled, h, p)
                    steps = [(r[0], v, eps[:], ALU.add), (r[1], r[0], minus_half[:, 0:1], ALU.pow), (r[2], v, r[1], ALU.mult),
                             (r[3], r[2], r[1], ALU.mult), (r[4], r[3], eps[:], ALU.add),
                             (r[5], r[4], minus_half[:, 0:1], ALU.pow)]
                    for n, (to, a, b, op) in enumerate(steps):
                        if n:
                            reached(pool, rs_own, h, p, n, 6)
                        tt(to, a, b, op).then_inc(rs_own, 1)

                def bias_of_norm(h, p):
                    reached(pool, xs_scaled, h, p)
                    tt(xs[:, p], xs[:, p], ln_bias[:], ALU.add).then_inc(xs_ready, 1)

                run_stages(pool, [(1, roots), (2, bias_of_norm)])

            @block.vector
            def _(dve):
                nc.vector.memset(ones_row[:], 1.0).then_inc(bias_made, 1)
                dve.wait_ge(q_in, 48)
                nc.vector.tensor_copy(bias_h[:], attn_bias[:]).then_inc(bias_made, 1)
                dve.wait_ge(bias_made, 2)
                nc.vector.tensor_tensor(bias_l[:], attn_bias[:], bias_h[:], ALU.subtract).then_inc(bias_made, 1)

                def statistics(h, p):
                    nc.vector.bn_stats(stats[:, p, :], x[:, p, h, :]).then_inc(stats_done, 1)
                    reached(dve, stats_done, h, p)
                    freed(dve, rs_own, h, p, 3, 6)
                    freed(dve, xL_ready, h, p)
                    carry_wait(nc, dve, consts)
                    nc.vector.bn_aggr(mv[:, p, :], stats[:, p, :]).then_inc(mv_ready, 1)

                def normalise(h, p):
                    reached(dve, mv_ready, h, p)
                    reached(dve, rs_own, h, p, 2, 6)
                    freed(dve, xL_kept, h, p)
                    nc.vector.tensor_scalar(xL[:, p, :], x[:, p, h, :], mv[:, p, 0:1], rs[:, p, 1:2],
                                            ALU.subtract, ALU.mult).then_inc(xL_ready, 1)
                    reached(dve, xL_ready, h, p)
                    reached(dve, rs_own, h, p, 6, 6)
                    freed(dve, xT_psum, h, p)
                    nc.vector.scalar_tensor_tensor(out=xs[:, p], in0=xL[:, p], scalar=rs[:, p, 5:6], in1=ln_scale[:],
                                                   op0=ALU.mult, op1=ALU.mult).then_inc(xs_scaled, 1)

                def low_x(h, p):
                    reached(dve, xh_ready, h, p)
                    freed(dve, y_psum, h, p)
                    nc.vector.tensor_tensor(xl[:, p].rearrange(flat), psT(p), xh[:, p].rearrange(flat),
                                            ALU.subtract).then_inc(xl_ready, 1)

                def add_xL(h, p):
                    reached(dve, y_psum, h, p)
                    reached(dve, xL_kept, h, p)
                    freed(dve, aT_psum, h, p)
                    nc.vector.tensor_tensor(xa[:, p], psY(p), xL_copy[:, p], ALU.add).then_inc(xa_ready, 1)

                def low_a(h, p):
                    reached(dve, ah_ready, h, p)
                    nc.vector.tensor_tensor(xal[:, :, h, p], psA(p).rearrange("p (c t) -> p c t", c=DC), xah[:, :, h, p],
                                            ALU.subtract).then_inc(al_ready, 1)

                run_stages(dve, [(2, normalise), (0, statistics), (6, low_a), (3, low_x), (4, add_xL)])

            @block.scalar
            def _(act):
                def high_x(h, p):
                    reached(act, xT_psum, h, p)
                    freed(act, y_psum, h, p)
                    nc.scalar.copy(xh[:, p].rearrange(flat), psT(p)).then_inc(xh_ready, 1)

                def keep_xL(h, p):
                    reached(act, xL_ready, h, p)
                    freed(act, xa_ready, h, p)
                    nc.scalar.copy(xL_copy[:, p], xL[:, p]).then_inc(xL_kept, 1)

                def high_a(h, p):
                    reached(act, aT_psum, h, p)
                    nc.scalar.copy(xah[:, :, h, p], psA(p).rearrange("p (c t) -> p c t", c=DC)).then_inc(ah_ready, 1)

                run_stages(act, [(3, high_x), (2, keep_xL), (5, high_a)])

            @block.tensor
            def _(pe):
                def turn(bank, tile):
                    for c in range(DC):
                        mm = nc.tensor.transpose(bank[:, c * P:(c + 1) * P], tile[:, c * P:(c + 1) * P], ident[:])
                    return mm

                def turn_x(h, p):
                    reached(pe, xs_ready, h, p)
                    freed(pe, xl_ready, h, p)
                    turn(psT(p), xs[:, p]).then_inc(xT_psum, 1)

                def turn_a(h, p):
                    reached(pe, xa_ready, h, p)
                    freed(pe, al_ready, h, p)
                    turn(psA(p), xa[:, p]).then_inc(aT_psum, 1)

                def project(h, p):
                    reached(pe, xl_ready, h, p)
                    freed(pe, xa_ready, h, p)
                    for n, half in enumerate((bias_h, bias_l)):
                        nc.tensor.matmul(psY(p), ones_row[:], half[:], start=n == 0, stop=False)
                    for n, (s, w) in enumerate([(xh, proj_h), (xl, proj_h), (xh, proj_l)]):
                        for c in range(DC):
                            mm = nc.tensor.matmul(psY(p), s[:, p, c], w[:, INNER, c], start=False,
                                                  stop=n == 2 and c == DC - 1)
                    mm.then_inc(y_psum, 1)

                pe.wait_ge(bias_made, 3)
                run_stages(pe, [(3, turn_x), (4, project), (5, turn_a)])

        wh = ph.sb("wh", [P, RING, 2, DC, P], BF16)
        wl = ph.sb("wl", [P, RING, 2, DC, P], BF16)
        hid = ph.sb("hid", [P, 2, D])
        hh = ph.sb("hh", [P, 2, D], BF16)
        hl = ph.sb("hl", [P, 2, D], BF16)
        eh = ph.sb("eh", [P, DC, D], BF16)
        el = ph.sb("el", [P, DC, D], BF16)
        last = ph.sb("last", [P, 2, D])
        ps = ph.banks()
        psU, psE, psN = (lambda u: ps[:, u % 2]), (lambda j: ps[:, 2 + j]), (lambda n: ps[:, 6 + n % 2])
        (wh_ready, wl_ready, h_psum, gelu_done, hh_ready, hl_ready, used, eh_ready, el_ready, n_psum,
         biased, last_ready, x_added, stored) = (
            ph.sem(n) for n in ("wh_ready wl_ready h_psum gelu_done hh_ready hl_ready used eh_ready el_ready "
                                "n_psum biased last_ready x_added stored").split())
        block = ctx.enter_context(nc.Block())

        def before_last(f):
            return not isinstance(f, int) or f + 2 < FC

        @block.sync
        def _(sp):
            with sp.Fori(1, UNITS // RING) as k:
                for r in range(RING):
                    sp.wait_ge(wl_ready, k * RING + (r + 1 - RING))
                    sp.dma_start(raw[:, r], d["w_f1"][k * RING + r]).then_inc(raw_in[r], 16)

            def store(e):
                for n in range(4):
                    sp.wait_ge(x_added, e * 4 + (n + 1))
                    h = e * TE + n // 2
                    sp.dma_start(out[n % 2, h], x[:, n % 2, h, :]).then_inc(stored, 16)

            with sp.Fori(0, E) as e:
                store(e)
            sp.wait_ge(stored, N_TILES * 16)

        @block.scalar
        def _(act):
            act.wait_ge(v_in, 48)

            def high_weights(g, r):
                act.wait_ge(raw_in[r], (g - r) * (16 // RING) + 16)
                at_least(act, used, g - RING + 1)
                nc.scalar.copy(wh[:, r].rearrange("p w c t -> p (w c t)"), raw[:, r]).then_inc(wh_ready, 1)

            def result(e):
                act.wait_ge(used, (e + 1) * FC)
                at_least(act, n_psum, e * 4)
                for j in range(DC):
                    nc.scalar.activation(eh[:, j], psE(j), ACT.Identity, bias=b2[:, e, j:j + 1]).then_inc(eh_ready, 1)

            def last_gelu(e, n):
                act.wait_ge(biased, e * 4 + (n + 1))
                nc.scalar.activation(last[:, n % 2], last[:, n % 2], ACT.Gelu).then_inc(last_ready, 1)

            def unit(e, f, r):
                g = e * FC + f
                final = isinstance(e, int) and e == E - 1
                if not final or before_last(f):
                    high_weights(g + 2, (r + 2) % RING)
                act.wait_ge(h_psum, g + 1)
                at_least(act, hl_ready, g - 1)
                nc.scalar.activation(hid[:, r % 2], psU(r), ACT.Gelu, bias=b1[:, e, f:f + 1] if isinstance(f, int) else
                                     b1[:, e, bass.ds(f, 1)]).then_inc(gelu_done, 1)
                act.wait_ge(gelu_done, g + 1)
                at_least(act, used, g - 1)
                nc.scalar.copy(hh[:, r % 2], hid[:, r % 2]).then_inc(hh_ready, 1)
                if isinstance(f, int) and not (isinstance(e, int) and e == 0):
                    if f == 0:
                        result(e - 1)
                    if f in LAST_AT:
                        for n in LAST_AT[f]:
                            last_gelu(e - 1, n)

            high_weights(0, 0)
            high_weights(1, 1)
            run_experts(act, unit)
            result(E - 1)
            for n in range(4):
                last_gelu(E - 1, n)

        @block.vector
        def _(dve):
            dve.wait_ge(v_in, 48)

            def low_weights(g, r):
                dve.wait_ge(wh_ready, g + 1)
                nc.vector.tensor_tensor(wl[:, r].rearrange("p w c t -> p (w c t)"), raw[:, r],
                                        wh[:, r].rearrange("p w c t -> p (w c t)"), ALU.subtract).then_inc(wl_ready, 1)

            def result(e):
                for j in range(DC):
                    dve.wait_ge(eh_ready, e * 4 + (j + 1))
                    nc.vector.scalar_tensor_tensor(out=el[:, j], in0=psE(j), scalar=b2[:, e, j:j + 1], in1=eh[:, j],
                                                   op0=ALU.add, op1=ALU.subtract).then_inc(el_ready, 1)

            def last_bias_add(e, n):
                dve.wait_ge(n_psum, e * 4 + (n + 1))
                at_least(dve, x_added, e * 4 + (n - 1))
                nc.vector.tensor_tensor(last[:, n % 2], psN(n), last_bias[:], ALU.add).then_inc(biased, 1)

            def unit(e, f, r):
                g = e * FC + f
                final = isinstance(e, int) and e == E - 1
                if not final or before_last(f):
                    low_weights(g + 2, (r + 2) % RING)
                dve.wait_ge(hh_ready, g + 1)
                nc.vector.tensor_tensor(hl[:, r % 2], hid[:, r % 2], hh[:, r % 2], ALU.subtract).then_inc(hl_ready, 1)
                if isinstance(f, int) and not (isinstance(e, int) and e == 0):
                    if f == 0:
                        result(e - 1)
                    if f in LAST_AT:
                        for n in LAST_AT[f]:
                            last_bias_add(e - 1, n)

            low_weights(0, 0)
            low_weights(1, 1)
            run_experts(dve, unit)
            result(E - 1)
            for n in range(4):
                last_bias_add(E - 1, n)

        @block.gpsimd
        def _(pool):
            def add(e):
                for n in range(4):
                    pool.wait_ge(last_ready, e * 4 + (n + 1))
                    tile = x[:, n % 2, e * TE + n // 2, :]
                    nc.gpsimd.tensor_tensor(tile, tile, last[:, n % 2], ALU.add).then_inc(x_added, 1)

            with pool.Fori(0, E) as e:
                add(e)

        @block.tensor
        def _(pe):
            def up(e, f, r):
                g = e * FC + f
                pe.wait_ge(wl_ready, g + 1)
                at_least(pe, gelu_done, g - 1)
                tokens = slice(e * TE, (e + 1) * TE) if isinstance(e, int) else bass.ds(e * TE, TE)
                for n, (w, s) in enumerate([(wh, xah), (wh, xal), (wl, xah)]):
                    for c in range(DC):
                        mm = nc.tensor.matmul(psU(r), w[:, r, 0, c], s[:, c, tokens].rearrange("p h b t -> p (h b t)"),
                                              start=n + c == 0, stop=n == 2 and c == DC - 1)
                mm.then_inc(h_psum, 1)

            def down(e, f, r):
                g = e * FC + f
                first = isinstance(f, int) and f == 0
                final = isinstance(f, int) and f == FC - 1
                pe.wait_ge(hl_ready, g + 1)
                if first:
                    at_least(pe, el_ready, e * 4)
                for j in range(DC):
                    for n, (w, s) in enumerate([(wh, hh), (wl, hh), (wh, hl)]):
                        mm = nc.tensor.matmul(psE(j), w[:, r, 1, j], s[:, r % 2], start=first and n == 0,
                                              stop=final and n == 2, skip_group_check=True)
                mm.then_inc(used, 1)

            def last_projection(e, n):
                pe.wait_ge(el_ready, e * 4 + 4)
                at_least(pe, biased, e * 4 + (n - 1))
                for m, (s, w) in enumerate([(eh, proj_h), (el, proj_h), (eh, proj_l)]):
                    for c in range(DC):
                        mm = nc.tensor.matmul(psN(n), s[:, c, n * P:(n + 1) * P], w[:, LAST, c], start=m + c == 0,
                                              stop=m == 2 and c == DC - 1)
                mm.then_inc(n_psum, 1)

            def unit(e, f, r):
                up(e, f, r)
                if isinstance(f, int) and f == 0:
                    if not (isinstance(e, int) and e == 0):
                        down(e - 1, FC - 1, RING - 1)
                else:
                    down(e, f - 1, (r - 1) % RING)
                if isinstance(f, int) and f in LAST_AT and not (isinstance(e, int) and e == 0):
                    for n in LAST_AT[f]:
                        last_projection(e - 1, n)

            run_experts(pe, unit)
            down(E - 1, FC - 1, RING - 1)
            for n in range(4):
                last_projection(E - 1, n)



def build(nc, d, out):
    with ExitStack() as ctx:
        ph = Phase(nc, ctx, "all")
        x = ph.sb("x", [P, B, TB, D])
        ident = ph.sb("ident", [P, P])
        ones = ph.sb("ones", [P, P])
        minus_half = ph.sb("minus_half", [P, 2])
        eps = ph.sb("eps", [P, 1])
        carried = ph.sb("carried", [P, 2])
        consts = (minus_half, carried)
        made = ph.sem("made")
        with nc.Block() as block:
            @block.gpsimd
            def _(pool):
                nc.gpsimd.memset(ident[:], 0.0).then_inc(made, 1)
                nc.gpsimd.memset(ones[:], 1.0).then_inc(made, 1)
                nc.gpsimd.memset(minus_half[:], -0.5).then_inc(made, 1)
                nc.gpsimd.memset(eps[:], LN_EPS).then_inc(made, 1)
                pool.wait_ge(made, 4)
                nc.gpsimd.affine_select(out=ident[:], in_=ident[:], compare_op=ALU.not_equal, fill=1.0, base=0,
                                        pattern=[[-1, P]], channel_multiplier=1).then_inc(made, 1)
                pool.wait_ge(made, 5)
        with ExitStack() as ctx2:
            ph = Phase(nc, ctx2, "store")
            store = ph.sb("store", [P, TB * B * D])
            q_hat = store[:].rearrange("p (t b n) -> p t b n", t=TB, b=B)
            ffn_raw = store[:].rearrange("p (w q n) -> p w q n", w=2, q=4)
            attn_raw = store[:, 8192:16384].rearrange("p (w c n) -> p w c n", w=4, c=DC)
            ffn_in = [ph.sem(f"ffn_in{n}") for n in range(2)]
            attn_in = [ph.sem(f"attn_in{n}") for n in range(4)]
            with ExitStack() as ctx3:
                gf = Phase(nc, ctx3, "l0").sb("gf", [P, B, D])
                l0_attention(nc, d, x, q_hat, gf, ident, ones, minus_half, consts)
                l0_cross_attention(nc, d, x, q_hat, gf, ffn_raw, ffn_in, ident, minus_half, eps, consts)
            l0_ffn(nc, d, x, store, ffn_raw, ffn_in, attn_raw, attn_in, ident, ones, minus_half, eps, consts)
            l1_attention(nc, d, x, store, attn_raw, attn_in, ident, minus_half, eps, consts)
        ph = Phase(nc, ctx, "l1")
        proj_raw = ph.sb("proj_raw", [P, 2, DC, D])
        proj_in = [ph.sem(f"proj_in{n}") for n in range(2)]
        l1_cross_attention(nc, d, x, proj_raw, proj_in, ident, ones, minus_half, eps, consts)
        l1_ffn(nc, d, x, out, proj_raw, proj_in, ident, minus_half, eps, consts)


def layouts(i):
    import numpy as np

    def lin(w):
        return w.reshape(w.shape[0] // P, P, -1).transpose(1, 0, 2)

    def rows(v):
        return np.broadcast_to(v, (P, *v.shape))

    return {
        "x": i["x"].reshape(B, TB, P, D),
        "w_a0": np.stack([lin(i[f"L0_attn_W_{n}"].T) for n in "qkv"], 1),
        "ctxT": lin(i["ctx_1024"].reshape(B * K, D).T),
        "mask": rows(i["mask_BxS2_if1"]),
        "w_f0_1": lin(i["L0_ffn_w1"].T),
        "w_f0_2": lin(i["L0_ffn_w2"].T).reshape(P, 4, F),
        "b_f0_1": rows(i["L0_ffn_b1"]),
        "b_f0_2": rows(i["L0_ffn_b2"]),
        "w_a1q": lin(i["L1_attn_W_q"].T),
        "w_a1k": lin(i["L1_attn_W_k"].T),
        "w_a1v": lin(i["L1_attn_W_v"].T),
        "w_a1o": lin(i["L1_attn_W_o"].T),
        "beta": rows(i["L1_attn_beta_param"]),
        "ctx_rows": i["ctx_1024"].transpose(1, 0, 2),
        "w_sim": i["L1_xattn_w_sim"].reshape(3, DC, P).transpose(2, 0, 1),
        "b_sim": rows(i["L1_xattn_b_sim"]),
        "b_x1": rows(i["L1_xattn_b_qv"]),
        **{f"w_x1_{n}": lin(i["L1_xattn_W_qv"][n * D:(n + 1) * D]) for n in range(4)},
        "w_f1a": lin(i["L1_ffn_attn_w"].T),
        "w_f1n": lin(i["L1_ffn_next_w"].T),
        "b_f1a": rows(i["L1_ffn_attn_b"]),
        "b_f1n": rows(i["L1_ffn_next_b"]),
        "ln_scale": rows(i["L1_ffn_ln_scale"]),
        "ln_bias": rows(i["L1_ffn_ln_bias"]),
        "b_f1_1": i["L1_ffn_b1"].reshape(E, FC, P).transpose(2, 0, 1),
        "b_f1_2": i["L1_ffn_b2"].reshape(E, DC, P).transpose(2, 0, 1),
        "w_f1": np.concatenate([
            i["L1_ffn_w1"].reshape(E, DC, P, FC, P).transpose(0, 3, 2, 1, 4).reshape(UNITS, P, D),
            i["L1_ffn_w2"].reshape(UNITS, P, D)], 2),
        "w_x0q": lin(i["L0_xattn_Wq"]),
        "w_x0k": lin(i["L0_xattn_Wk"]),
        "w_x0v": lin(i["L0_xattn_Wv"]),
        "w_x0o": lin(i["L0_xattn_Wo"]),
    }


def kernel(**inputs):
    import numpy as _np
    import concourse.bacc as _bacc
    from concourse import mybir as _mybir
    from concourse.bass_utils import run_bass_kernel_spmd as _run

    nc = _bacc.Bacc("TRN2", target_bir_lowering=False, num_devices=1)
    arrays, d = {}, {}
    for name, a in layouts({k: _np.asarray(v) for k, v in inputs.items()}).items():
        a = _np.ascontiguousarray(a)
        arrays[f"in_{name}"] = a
        d[name] = nc.dram_tensor(f"in_{name}", a.shape, _mybir.dt.from_np(a.dtype), kind="ExternalInput").ap()
    out = nc.dram_tensor("out_0", (B, TB, P, D), F32, kind="ExternalOutput").ap()
    build(nc, d, out)
    r = _run(nc, [arrays], core_ids=[0])
    return r.results[0]["out_0"].reshape(B, S, D)
```
